# Optimizing a Trainium2 kernel written in Bass

```python
import numpy as np
import jax
import jax.numpy as jnp

def _softmax(x, axis=-1):
    return jax.nn.softmax(x, axis=axis)

def _gelu(x):
    return jax.nn.gelu(x, approximate=True)

def _silu(x):
    return jax.nn.silu(x)

def _sigmoid(x):
    return jax.nn.sigmoid(x)

def _layernorm(x, axis=-1, eps=1e-05):
    m = jnp.mean(x, axis=axis, keepdims=True)
    v = jnp.var(x, axis=axis, keepdims=True)
    return (x - m) / jnp.sqrt(v + eps)

def _scatter_add(tgt, idx, src, axis=0):
    return tgt.at[idx].add(src)

def _segment_sum(src, seg, n):
    return jax.ops.segment_sum(src, seg, n)
kernel_name = 'mk_decoder_postln_d2_seqx_r8_f65e7d'

def setup_inputs(seed: int=0):
    np.random.seed(seed)
    _w = jnp.asarray

    def _rec_inputs():
        import jax
        import jax.numpy as jnp
        _rk = jax.random.key(seed)
        x = 7.22e-05 + 1 * jax.random.normal(jax.random.fold_in(_rk, 1), (16, 128, 256), jnp.float32)
        _lenS = 128 - jax.random.randint(jax.random.fold_in(_rk, 7), (16,), 0, max(1, 128 // 4) + 1, jnp.int32)
        _lenS2 = 128 - jax.random.randint(jax.random.fold_in(_rk, 8), (16,), 0, max(1, 128 // 4) + 1, jnp.int32)
        _ctx_1024P = jax.random.normal(jax.random.fold_in(_rk, 11), (16, 16, 128), jnp.float32)
        _ctx_1024c = jax.random.dirichlet(jax.random.fold_in(_rk, 511), 0.3 * jnp.ones((16,), jnp.float32), (16, 128))
        _ctx_1024t = jnp.einsum('bsk,bkd->bsd', _ctx_1024c, _ctx_1024P)
        _ctx_1024t = _ctx_1024t * jax.lax.rsqrt(jnp.mean(jnp.square(_ctx_1024t)) + 1e-12) * 0.953939
        ctx_1024 = -1.39393e-06 + 0.999914 * (_ctx_1024t + 0.3 * jax.random.normal(jax.random.fold_in(_rk, 611), (16, 128, 128), jnp.float32))
        fside_BxSx2_0 = jax.random.uniform(jax.random.fold_in(_rk, 12), (16, 128, 2), jnp.float32, 0.0, 0.999707)
        return (x, ctx_1024, fside_BxSx2_0)
    x, ctx_1024, fside_BxSx2_0 = _rec_inputs()

    def _L0_attn_setup():
        import jax, jax.numpy as jnp
        import numpy as np
        N_HEADS = 16
        key = jax.random.key(seed)
        ks = jax.random.split(key, 9)
        B, S, D = (2, 256, 256)
        s = 0.02
        return {'X': jax.random.normal(ks[0], (B, S, D), jnp.float32), 'Wq': jax.random.normal(ks[1], (D, D), jnp.float32) * s, 'bq': jax.random.normal(ks[2], (D,), jnp.float32) * s, 'Wk': jax.random.normal(ks[3], (D, D), jnp.float32) * s, 'bk': jax.random.normal(ks[4], (D,), jnp.float32) * s, 'Wv': jax.random.normal(ks[5], (D, D), jnp.float32) * s, 'bv': jax.random.normal(ks[6], (D,), jnp.float32) * s, 'Wo': jax.random.normal(ks[7], (D, D), jnp.float32) * s, 'bo': jax.random.normal(ks[8], (D,), jnp.float32) * s}
    _L0_attn_all = _L0_attn_setup()
    _L0_attn_in = {k: v for k, v in _L0_attn_all.items() if k in ('Wq', 'bq', 'Wk', 'bk', 'Wv', 'bv', 'Wo', 'bo')}
    del _L0_attn_all

    def _L0_xattn_setup():
        import jax, jax.numpy as jnp
        import numpy as np
        DIM = 256
        CTX_DIM = 128
        N_HEADS = 32
        HEAD_DIM = DIM // N_HEADS
        POS_DIM = 2
        B, N, CTXN = (2, 256, 256)
        ROPE_BASE = 10000.0

        def apply_axial_rope(x, pos):
            b, n, h, d = x.shape
            p = pos.shape[-1]
            dpa = d // p
            half = dpa // 2
            freqs = ROPE_BASE ** (-jnp.arange(half, dtype=x.dtype) / half)
            ang = pos[..., :, None] * freqs
            cos = jnp.cos(ang)[:, :, None, :, :]
            sin = jnp.sin(ang)[:, :, None, :, :]
            xr = x.reshape(b, n, h, p, half, 2)
            x1, x2 = (xr[..., 0], xr[..., 1])
            out = jnp.stack([x1 * cos - x2 * sin, x1 * sin + x2 * cos], axis=-1)
            return out.reshape(b, n, h, d)
        key = jax.random.key(seed)
        ks = jax.random.split(key, 8)
        x = jax.random.normal(ks[0], (B, N, DIM), jnp.float32)
        ctx = jax.random.normal(ks[1], (B, CTXN, CTX_DIM), jnp.float32)
        pos_map = jax.random.uniform(ks[2], (B, N, POS_DIM), jnp.float32)
        ctx_pos_map = jax.random.uniform(ks[3], (B, CTXN, POS_DIM), jnp.float32)
        Wq = jax.random.normal(ks[4], (DIM, DIM), jnp.float32) / np.sqrt(DIM)
        Wkv = jax.random.normal(ks[5], (CTX_DIM, 2 * DIM), jnp.float32) / np.sqrt(CTX_DIM)
        Wout = jax.random.normal(ks[6], (DIM, DIM), jnp.float32) / np.sqrt(DIM)
        bout = jnp.zeros((DIM,), jnp.float32)
        return {'x': x, 'ctx': ctx, 'pos_map': pos_map, 'ctx_pos_map': ctx_pos_map, 'Wq': Wq, 'Wkv': Wkv, 'Wout': Wout, 'bout': bout}
    _L0_xattn_all = _L0_xattn_setup()
    _L0_xattn_in = {k: v for k, v in _L0_xattn_all.items() if k in ('Wq', 'Wkv', 'Wout', 'bout')}
    del _L0_xattn_all

    def _L0_ffn_setup():
        import jax, jax.numpy as jnp
        import numpy as np
        E, R, K = (8, 8, 2)
        D, F = (256, 1024)
        B, S = (2, 256)
        SCALING = 16.0 / 8.0

        def act(x):
            return jax.nn.gelu(x, approximate=True)
        key = jax.random.key(seed)
        ks = jax.random.split(key, 12)
        return {'hidden_states': jax.random.normal(ks[0], (B, S, D), jnp.float32), 'W_r': jax.random.normal(ks[1], (E, D), jnp.float32) * 0.02, 'b_r': jnp.zeros((E,), jnp.float32), 'W1': jax.random.normal(ks[2], (F, D), jnp.float32) * 0.02, 'b1': jnp.zeros((F,), jnp.float32), 'W2': jax.random.normal(ks[3], (D, F), jnp.float32) * 0.02, 'b2': jnp.zeros((D,), jnp.float32), 'A1': jax.random.normal(ks[4], (E, R, D), jnp.float32) * 0.02, 'B1': jax.random.normal(ks[5], (F, R) * 1 + ()).reshape(1, F, R).repeat(1, 0) * 0.0 + jax.random.normal(ks[5], (E, F, R), jnp.float32) * 0.02, 'A2': jax.random.normal(ks[6], (E, R, F), jnp.float32) * 0.02, 'B2': jax.random.normal(ks[7], (E, D, R), jnp.float32) * 0.02}
    _L0_ffn_all = _L0_ffn_setup()
    _L0_ffn_in = {k: v for k, v in _L0_ffn_all.items() if k in ('W_r', 'b_r', 'W1', 'b1', 'W2', 'b2', 'A1', 'B1', 'A2', 'B2')}
    del _L0_ffn_all

    def _L1_attn_setup():
        import jax, jax.numpy as jnp
        import numpy as np
        import math
        B, S, DIM = (2, 256, 256)
        H, NOPE, ROPE, VDIM = (16, 128, 64, 128)
        Q_RANK, KV_RANK = (128, 64)
        EPS = 1e-06
        ROPE_THETA = 10000.0

        def _rmsnorm(x, w, eps=EPS):
            return x * jax.lax.rsqrt(jnp.mean(x * x, axis=-1, keepdims=True) + eps) * w

        def _rope_cos_sin(seq_len, head_dim, dtype=jnp.float32):
            inv_freq = 1.0 / ROPE_THETA ** (jnp.arange(0, head_dim, 2, dtype=jnp.float32) / head_dim)
            t = jnp.arange(seq_len, dtype=jnp.float32)
            freqs = jnp.outer(t, inv_freq)
            return (jnp.cos(freqs).astype(dtype), jnp.sin(freqs).astype(dtype))

        def _apply_rope(x, cos, sin):
            x1, x2 = (x[..., 0::2], x[..., 1::2])
            c = cos[None, :, None, :]
            s = sin[None, :, None, :]
            o1 = x1 * c - x2 * s
            o2 = x1 * s + x2 * c
            return jnp.stack([o1, o2], axis=-1).reshape(x.shape)
        key = jax.random.key(seed)
        ks = jax.random.split(key, 9)
        s = 0.02
        return {'x': jax.random.normal(ks[0], (B, S, DIM), jnp.float32), 'wq_down': jax.random.normal(ks[1], (Q_RANK, DIM), jnp.float32) * s, 'q_norm_w': jnp.ones((Q_RANK,), jnp.float32), 'wq_up': jax.random.normal(ks[2], (H * NOPE, Q_RANK), jnp.float32) * s, 'wq_rope': jax.random.normal(ks[3], (H * ROPE, Q_RANK), jnp.float32) * s, 'wkv_down': jax.random.normal(ks[4], (KV_RANK, DIM), jnp.float32) * s, 'kv_norm_w': jnp.ones((KV_RANK,), jnp.float32), 'wkv_up': jax.random.normal(ks[5], (H * (NOPE + VDIM), KV_RANK), jnp.float32) * s, 'wk_rope': jax.random.normal(ks[6], (ROPE, DIM), jnp.float32) * s, 'wo': jax.random.normal(ks[7], (DIM, H * VDIM), jnp.float32) * s}
    _L1_attn_all = _L1_attn_setup()
    _L1_attn_in = {k: v for k, v in _L1_attn_all.items() if k in ('wq_down', 'q_norm_w', 'wq_up', 'wq_rope', 'wkv_down', 'kv_norm_w', 'wkv_up', 'wk_rope', 'wo')}
    del _L1_attn_all

    def _L1_xattn_setup():
        import jax, jax.numpy as jnp
        import numpy as np
        DIM = 256
        CTX_DIM = 128
        N_HEADS = 32
        HEAD_DIM = DIM // N_HEADS
        POS_DIM = 2
        B, N, CTXN = (2, 256, 256)
        ROPE_BASE = 10000.0

        def apply_axial_rope(x, pos):
            b, n, h, d = x.shape
            p = pos.shape[-1]
            dpa = d // p
            half = dpa // 2
            freqs = ROPE_BASE ** (-jnp.arange(half, dtype=x.dtype) / half)
            ang = pos[..., :, None] * freqs
            cos = jnp.cos(ang)[:, :, None, :, :]
            sin = jnp.sin(ang)[:, :, None, :, :]
            xr = x.reshape(b, n, h, p, half, 2)
            x1, x2 = (xr[..., 0], xr[..., 1])
            out = jnp.stack([x1 * cos - x2 * sin, x1 * sin + x2 * cos], axis=-1)
            return out.reshape(b, n, h, d)
        key = jax.random.key(seed)
        ks = jax.random.split(key, 8)
        x = jax.random.normal(ks[0], (B, N, DIM), jnp.float32)
        ctx = jax.random.normal(ks[1], (B, CTXN, CTX_DIM), jnp.float32)
        pos_map = jax.random.uniform(ks[2], (B, N, POS_DIM), jnp.float32)
        ctx_pos_map = jax.random.uniform(ks[3], (B, CTXN, POS_DIM), jnp.float32)
        Wq = jax.random.normal(ks[4], (DIM, DIM), jnp.float32) / np.sqrt(DIM)
        Wkv = jax.random.normal(ks[5], (CTX_DIM, 2 * DIM), jnp.float32) / np.sqrt(CTX_DIM)
        Wout = jax.random.normal(ks[6], (DIM, DIM), jnp.float32) / np.sqrt(DIM)
        bout = jnp.zeros((DIM,), jnp.float32)
        return {'x': x, 'ctx': ctx, 'pos_map': pos_map, 'ctx_pos_map': ctx_pos_map, 'Wq': Wq, 'Wkv': Wkv, 'Wout': Wout, 'bout': bout}
    _L1_xattn_all = _L1_xattn_setup()
    _L1_xattn_in = {k: v for k, v in _L1_xattn_all.items() if k in ('Wq', 'Wkv', 'Wout', 'bout')}
    del _L1_xattn_all

    def _L1_ffn_setup():
        import jax, jax.numpy as jnp
        import numpy as np
        D_MODEL = 256
        HIDDEN = 4 * D_MODEL
        B, S = (2, 512)

        def bit_linear(x, w, b):
            gamma_x = jnp.clip(jnp.max(jnp.abs(x), axis=-1, keepdims=True), 1e-05, None)
            scale_x = 127.0 / gamma_x
            x_dq = jnp.clip(jnp.round(x * scale_x), -128.0, 127.0) / scale_x
            x_ste = x + jax.lax.stop_gradient(x_dq - x)
            gamma_w = jnp.clip(jnp.mean(jnp.abs(w)), 1e-05, None)
            w_dq = jnp.clip(jnp.round(w / gamma_w), -1.0, 1.0) * gamma_w
            w_ste = w + jax.lax.stop_gradient(w_dq - w)
            return jnp.einsum('bsd,hd->bsh', x_ste, w_ste) + b
        key = jax.random.key(seed)
        ks = jax.random.split(key, 7)
        std = 0.02
        return {'x': jax.random.normal(ks[0], (B, S, D_MODEL), dtype=jnp.float32), 'gate_w': jax.random.normal(ks[1], (HIDDEN, D_MODEL), dtype=jnp.float32) * std, 'gate_b': jnp.zeros((HIDDEN,), dtype=jnp.float32), 'val_w': jax.random.normal(ks[2], (HIDDEN, D_MODEL), dtype=jnp.float32) * std, 'val_b': jnp.zeros((HIDDEN,), dtype=jnp.float32), 'out_w': jax.random.normal(ks[3], (D_MODEL, HIDDEN), dtype=jnp.float32) * std, 'out_b': jnp.zeros((D_MODEL,), dtype=jnp.float32)}
    _L1_ffn_all = _L1_ffn_setup()
    _L1_ffn_in = {k: v for k, v in _L1_ffn_all.items() if k in ('gate_w', 'gate_b', 'val_w', 'val_b', 'out_w', 'out_b')}
    del _L1_ffn_all
    return {'x': x, 'ctx_1024': ctx_1024, 'fside_BxSx2_0': fside_BxSx2_0, 'L0_attn_Wq': _L0_attn_in['Wq'], 'L0_attn_bq': _L0_attn_in['bq'], 'L0_attn_Wk': _L0_attn_in['Wk'], 'L0_attn_bk': _L0_attn_in['bk'], 'L0_attn_Wv': _L0_attn_in['Wv'], 'L0_attn_bv': _L0_attn_in['bv'], 'L0_attn_Wo': _L0_attn_in['Wo'], 'L0_attn_bo': _L0_attn_in['bo'], 'L0_xattn_Wq': _L0_xattn_in['Wq'], 'L0_xattn_Wkv': _L0_xattn_in['Wkv'], 'L0_xattn_Wout': _L0_xattn_in['Wout'], 'L0_xattn_bout': _L0_xattn_in['bout'], 'L0_ffn_W_r': _L0_ffn_in['W_r'], 'L0_ffn_b_r': _L0_ffn_in['b_r'], 'L0_ffn_W1': _L0_ffn_in['W1'], 'L0_ffn_b1': _L0_ffn_in['b1'], 'L0_ffn_W2': _L0_ffn_in['W2'], 'L0_ffn_b2': _L0_ffn_in['b2'], 'L0_ffn_A1': _L0_ffn_in['A1'], 'L0_ffn_B1': _L0_ffn_in['B1'], 'L0_ffn_A2': _L0_ffn_in['A2'], 'L0_ffn_B2': _L0_ffn_in['B2'], 'L1_attn_wq_down': _L1_attn_in['wq_down'], 'L1_attn_q_norm_w': _L1_attn_in['q_norm_w'], 'L1_attn_wq_up': _L1_attn_in['wq_up'], 'L1_attn_wq_rope': _L1_attn_in['wq_rope'], 'L1_attn_wkv_down': _L1_attn_in['wkv_down'], 'L1_attn_kv_norm_w': _L1_attn_in['kv_norm_w'], 'L1_attn_wkv_up': _L1_attn_in['wkv_up'], 'L1_attn_wk_rope': _L1_attn_in['wk_rope'], 'L1_attn_wo': _L1_attn_in['wo'], 'L1_xattn_Wq': _L1_xattn_in['Wq'], 'L1_xattn_Wkv': _L1_xattn_in['Wkv'], 'L1_xattn_Wout': _L1_xattn_in['Wout'], 'L1_xattn_bout': _L1_xattn_in['bout'], 'L1_ffn_gate_w': _L1_ffn_in['gate_w'], 'L1_ffn_gate_b': _L1_ffn_in['gate_b'], 'L1_ffn_val_w': _L1_ffn_in['val_w'], 'L1_ffn_val_b': _L1_ffn_in['val_b'], 'L1_ffn_out_w': _L1_ffn_in['out_w'], 'L1_ffn_out_b': _L1_ffn_in['out_b']}

def reference(x, ctx_1024, fside_BxSx2_0, L0_attn_Wq, L0_attn_bq, L0_attn_Wk, L0_attn_bk, L0_attn_Wv, L0_attn_bv, L0_attn_Wo, L0_attn_bo, L0_xattn_Wq, L0_xattn_Wkv, L0_xattn_Wout, L0_xattn_bout, L0_ffn_W_r, L0_ffn_b_r, L0_ffn_W1, L0_ffn_b1, L0_ffn_W2, L0_ffn_b2, L0_ffn_A1, L0_ffn_B1, L0_ffn_A2, L0_ffn_B2, L1_attn_wq_down, L1_attn_q_norm_w, L1_attn_wq_up, L1_attn_wq_rope, L1_attn_wkv_down, L1_attn_kv_norm_w, L1_attn_wkv_up, L1_attn_wk_rope, L1_attn_wo, L1_xattn_Wq, L1_xattn_Wkv, L1_xattn_Wout, L1_xattn_bout, L1_ffn_gate_w, L1_ffn_gate_b, L1_ffn_val_w, L1_ffn_val_b, L1_ffn_out_w, L1_ffn_out_b):
    import jax
    import jax.numpy as jnp

    def _L0_attn_ref(X, Wq, bq, Wk, bk, Wv, bv, Wo, bo):
        import jax, jax.numpy as jnp
        import numpy as np
        N_HEADS = 16
        B, S, D = X.shape
        H = N_HEADS
        d_head = D // H
        scale = jnp.asarray(1.0 / np.sqrt(np.sqrt(d_head)), X.dtype)
        Q = (X @ Wq.T + bq).reshape(B, S, H, d_head) * scale
        K = (X @ Wk.T + bk).reshape(B, S, H, d_head) * scale
        V = (X @ Wv.T + bv).reshape(B, S, H, d_head)
        scores = jnp.einsum('bqhd,bkhd->bhqk', Q, K)
        causal = jnp.tril(jnp.ones((S, S), bool))
        scores = jnp.where(causal[None, None], scores, -jnp.inf)
        attn = jax.nn.softmax(scores.astype(jnp.float32), axis=-1).astype(X.dtype)
        out = jnp.einsum('bhqk,bkhd->bqhd', attn, V).reshape(B, S, D)
        return out @ Wo.T + bo

    def _L0_xattn_ref(x, ctx, pos_map, ctx_pos_map, Wq, Wkv, Wout, bout):
        import jax, jax.numpy as jnp
        import numpy as np
        DIM = 256
        CTX_DIM = 128
        N_HEADS = 32
        HEAD_DIM = DIM // N_HEADS
        POS_DIM = 2
        B, N, CTXN = (2, 256, 256)
        ROPE_BASE = 10000.0

        def apply_axial_rope(x, pos):
            b, n, h, d = x.shape
            p = pos.shape[-1]
            dpa = d // p
            half = dpa // 2
            freqs = ROPE_BASE ** (-jnp.arange(half, dtype=x.dtype) / half)
            ang = pos[..., :, None] * freqs
            cos = jnp.cos(ang)[:, :, None, :, :]
            sin = jnp.sin(ang)[:, :, None, :, :]
            xr = x.reshape(b, n, h, p, half, 2)
            x1, x2 = (xr[..., 0], xr[..., 1])
            out = jnp.stack([x1 * cos - x2 * sin, x1 * sin + x2 * cos], axis=-1)
            return out.reshape(b, n, h, d)
        b, n, _ = x.shape
        ctx_n = ctx.shape[1]
        q = (x @ Wq).reshape(b, n, N_HEADS, HEAD_DIM)
        k, v = jnp.split(ctx @ Wkv, 2, axis=-1)
        k = k.reshape(b, ctx_n, N_HEADS, HEAD_DIM)
        v = v.reshape(b, ctx_n, N_HEADS, HEAD_DIM)
        q = apply_axial_rope(q, pos_map)
        k = apply_axial_rope(k, ctx_pos_map)
        scale = 1.0 / np.sqrt(HEAD_DIM).astype(np.float32)
        logits = jnp.einsum('bqhd,bkhd->bhqk', q, k) * scale
        w = jax.nn.softmax(logits, axis=-1)
        attn = jnp.einsum('bhqk,bkhd->bqhd', w, v)
        attn = attn.reshape(b, n, N_HEADS * HEAD_DIM)
        return attn @ Wout + bout

    def _L0_ffn_ref(hidden_states, W_r, b_r, W1, b1, W2, b2, A1, B1, A2, B2):
        import jax, jax.numpy as jnp
        import numpy as np
        E, R, K = (8, 8, 2)
        D, F = (256, 1024)
        B, S = (2, 256)
        SCALING = 16.0 / 8.0

        def act(x):
            return jax.nn.gelu(x, approximate=True)
        b, s, d = hidden_states.shape
        N = b * s
        x = hidden_states.reshape(N, d)
        probs = jax.nn.softmax(x @ W_r.T + b_r, axis=-1)
        w_topk, idx_topk = jax.lax.top_k(probs, K)
        base1 = x @ W1.T + b1
        u1 = jnp.einsum('nd,erd->ner', x, A1)
        B1_rf = B1.transpose(0, 2, 1).reshape(E * R, F)
        B2_rf = B2.transpose(0, 2, 1).reshape(E * R, d)
        res = jnp.zeros((N, d), hidden_states.dtype)
        for k in range(K):
            oh = jax.nn.one_hot(idx_topk[:, k], E, dtype=x.dtype)
            z1 = (u1 * oh[:, :, None]).reshape(N, E * R)
            h = act(base1 + z1 @ B1_rf * SCALING)
            u2 = jnp.einsum('nf,erf->ner', h, A2)
            z2 = (u2 * oh[:, :, None]).reshape(N, E * R)
            y = h @ W2.T + b2 + z2 @ B2_rf * SCALING
            res = res + w_topk[:, k:k + 1] * y
        return res.reshape(b, s, d)

    def _L1_attn_ref(x, wq_down, q_norm_w, wq_up, wq_rope, wkv_down, kv_norm_w, wkv_up, wk_rope, wo):
        import jax, jax.numpy as jnp
        import numpy as np
        import math
        B, S, DIM = (2, 256, 256)
        H, NOPE, ROPE, VDIM = (16, 128, 64, 128)
        Q_RANK, KV_RANK = (128, 64)
        EPS = 1e-06
        ROPE_THETA = 10000.0

        def _rmsnorm(x, w, eps=EPS):
            return x * jax.lax.rsqrt(jnp.mean(x * x, axis=-1, keepdims=True) + eps) * w

        def _rope_cos_sin(seq_len, head_dim, dtype=jnp.float32):
            inv_freq = 1.0 / ROPE_THETA ** (jnp.arange(0, head_dim, 2, dtype=jnp.float32) / head_dim)
            t = jnp.arange(seq_len, dtype=jnp.float32)
            freqs = jnp.outer(t, inv_freq)
            return (jnp.cos(freqs).astype(dtype), jnp.sin(freqs).astype(dtype))

        def _apply_rope(x, cos, sin):
            x1, x2 = (x[..., 0::2], x[..., 1::2])
            c = cos[None, :, None, :]
            s = sin[None, :, None, :]
            o1 = x1 * c - x2 * s
            o2 = x1 * s + x2 * c
            return jnp.stack([o1, o2], axis=-1).reshape(x.shape)
        bs, seq_len, _ = x.shape
        q_c = _rmsnorm(x @ wq_down.T, q_norm_w)
        q_nope = (q_c @ wq_up.T).reshape(bs, seq_len, H, NOPE)
        q_pe = (q_c @ wq_rope.T).reshape(bs, seq_len, H, ROPE)
        kv_c = _rmsnorm(x @ wkv_down.T, kv_norm_w)
        kv_up = (x_kv := (kv_c @ wkv_up.T)).reshape(bs, seq_len, H, NOPE + VDIM)
        k_nope, v = (kv_up[..., :NOPE], kv_up[..., NOPE:])
        k_rope_shared = (x @ wk_rope.T).reshape(bs, seq_len, 1, ROPE)
        cos, sin = _rope_cos_sin(seq_len, ROPE, x.dtype)
        q_pe = _apply_rope(q_pe, cos, sin)
        k_rope_shared = _apply_rope(k_rope_shared, cos, sin)
        k_rope = jnp.broadcast_to(k_rope_shared, (bs, seq_len, H, ROPE))
        q = jnp.concatenate([q_nope, q_pe], axis=-1)
        k = jnp.concatenate([k_nope, k_rope], axis=-1)
        scale = 1.0 / math.sqrt(NOPE + ROPE)
        scores = jnp.einsum('bqhd,bkhd->bhqk', q, k) * scale
        causal = jnp.tril(jnp.ones((seq_len, seq_len), bool))
        scores = jnp.where(causal[None, None], scores, -jnp.inf)
        probs = jax.nn.softmax(scores.astype(jnp.float32), axis=-1).astype(q.dtype)
        out = jnp.einsum('bhqk,bkhv->bqhv', probs, v).reshape(bs, seq_len, H * VDIM)
        return out @ wo.T

    def _L1_xattn_ref(x, ctx, pos_map, ctx_pos_map, Wq, Wkv, Wout, bout):
        import jax, jax.numpy as jnp
        import numpy as np
        DIM = 256
        CTX_DIM = 128
        N_HEADS = 32
        HEAD_DIM = DIM // N_HEADS
        POS_DIM = 2
        B, N, CTXN = (2, 256, 256)
        ROPE_BASE = 10000.0

        def apply_axial_rope(x, pos):
            b, n, h, d = x.shape
            p = pos.shape[-1]
            dpa = d // p
            half = dpa // 2
            freqs = ROPE_BASE ** (-jnp.arange(half, dtype=x.dtype) / half)
            ang = pos[..., :, None] * freqs
            cos = jnp.cos(ang)[:, :, None, :, :]
            sin = jnp.sin(ang)[:, :, None, :, :]
            xr = x.reshape(b, n, h, p, half, 2)
            x1, x2 = (xr[..., 0], xr[..., 1])
            out = jnp.stack([x1 * cos - x2 * sin, x1 * sin + x2 * cos], axis=-1)
            return out.reshape(b, n, h, d)
        b, n, _ = x.shape
        ctx_n = ctx.shape[1]
        q = (x @ Wq).reshape(b, n, N_HEADS, HEAD_DIM)
        k, v = jnp.split(ctx @ Wkv, 2, axis=-1)
        k = k.reshape(b, ctx_n, N_HEADS, HEAD_DIM)
        v = v.reshape(b, ctx_n, N_HEADS, HEAD_DIM)
        q = apply_axial_rope(q, pos_map)
        k = apply_axial_rope(k, ctx_pos_map)
        scale = 1.0 / np.sqrt(HEAD_DIM).astype(np.float32)
        logits = jnp.einsum('bqhd,bkhd->bhqk', q, k) * scale
        w = jax.nn.softmax(logits, axis=-1)
        attn = jnp.einsum('bhqk,bkhd->bqhd', w, v)
        attn = attn.reshape(b, n, N_HEADS * HEAD_DIM)
        return attn @ Wout + bout

    def _L1_ffn_ref(x, gate_w, gate_b, val_w, val_b, out_w, out_b):
        import jax, jax.numpy as jnp
        import numpy as np
        D_MODEL = 256
        HIDDEN = 4 * D_MODEL
        B, S = (2, 512)

        def bit_linear(x, w, b):
            gamma_x = jnp.clip(jnp.max(jnp.abs(x), axis=-1, keepdims=True), 1e-05, None)
            scale_x = 127.0 / gamma_x
            x_dq = jnp.clip(jnp.round(x * scale_x), -128.0, 127.0) / scale_x
            x_ste = x + jax.lax.stop_gradient(x_dq - x)
            gamma_w = jnp.clip(jnp.mean(jnp.abs(w)), 1e-05, None)
            w_dq = jnp.clip(jnp.round(w / gamma_w), -1.0, 1.0) * gamma_w
            w_ste = w + jax.lax.stop_gradient(w_dq - w)
            return jnp.einsum('bsd,hd->bsh', x_ste, w_ste) + b
        gate = jax.nn.silu(bit_linear(x, gate_w, gate_b))
        val = bit_linear(x, val_w, val_b)
        return bit_linear(gate * val, out_w, out_b)
    x = _layernorm(x + _L0_attn_ref(x, L0_attn_Wq, L0_attn_bq, L0_attn_Wk, L0_attn_bk, L0_attn_Wv, L0_attn_bv, L0_attn_Wo, L0_attn_bo), axis=-1)
    x = _layernorm(x + _L0_xattn_ref(x, ctx_1024, fside_BxSx2_0, fside_BxSx2_0, L0_xattn_Wq, L0_xattn_Wkv, L0_xattn_Wout, L0_xattn_bout), axis=-1)
    x = _layernorm(x + _L0_ffn_ref(x, L0_ffn_W_r, L0_ffn_b_r, L0_ffn_W1, L0_ffn_b1, L0_ffn_W2, L0_ffn_b2, L0_ffn_A1, L0_ffn_B1, L0_ffn_A2, L0_ffn_B2), axis=-1)
    x = _layernorm(x + _L1_attn_ref(x, L1_attn_wq_down, L1_attn_q_norm_w, L1_attn_wq_up, L1_attn_wq_rope, L1_attn_wkv_down, L1_attn_kv_norm_w, L1_attn_wkv_up, L1_attn_wk_rope, L1_attn_wo), axis=-1)
    x = _layernorm(x + _L1_xattn_ref(x, ctx_1024, fside_BxSx2_0, fside_BxSx2_0, L1_xattn_Wq, L1_xattn_Wkv, L1_xattn_Wout, L1_xattn_bout), axis=-1)
    x = _layernorm(x + _L1_ffn_ref(x, L1_ffn_gate_w, L1_ffn_gate_b, L1_ffn_val_w, L1_ffn_val_b, L1_ffn_out_w, L1_ffn_out_b), axis=-1)
    return x

_drawn_inputs = setup_inputs


def setup_inputs(seed=0):
    import zlib

    import numpy as np

    out = dict(_drawn_inputs(seed))
    spreads = {'L0_xattn_bout': (0.0, 0.1),
     'L0_ffn_b_r': (0.0, 0.8),
     'L0_ffn_b1': (0.0, 0.8),
     'L0_ffn_b2': (0.0, 0.301),
     'L1_attn_q_norm_w': (1.0, 0.6),
     'L1_attn_kv_norm_w': (1.0, 0.6),
     'L1_xattn_bout': (0.0, 0.1),
     'L1_ffn_gate_b': (0.0, 0.8),
     'L1_ffn_val_b': (0.0, 0.8),
     'L1_ffn_out_b': (0.0, 0.1)}
    factors = {'L0_attn_Wq': 8.0,
     'L0_attn_bq': 8.0,
     'L0_attn_Wk': 8.0,
     'L0_attn_bk': 8.0,
     'L0_attn_Wv': 3.763,
     'L0_attn_bv': 8.0,
     'L0_attn_Wo': 3.626,
     'L0_attn_bo': 4.158,
     'L0_ffn_W_r': 8.0,
     'L0_ffn_A1': 8.0,
     'L0_ffn_B1': 8.0,
     'L0_ffn_A2': 8.0,
     'L0_ffn_B2': 8.0,
     'L1_attn_wq_down': 8.0,
     'L1_attn_wq_up': 8.0,
     'L1_attn_wq_rope': 8.0,
     'L1_attn_wk_rope': 8.0,
     'L1_ffn_gate_w': 5.085,
     'L1_ffn_val_w': 5.114,
     'L1_ffn_out_w': 4.574}
    for name, (base, spread) in spreads.items():
        noise = np.random.default_rng([zlib.crc32(name.encode()), seed]).standard_normal(out[name].shape)
        drawn = base * np.exp(spread * noise) if base else spread * noise
        out[name] = jnp.asarray(drawn.astype(out[name].dtype))
    for name, factor in factors.items():
        out[name] = (out[name] * factor).astype(out[name].dtype)
    return out
```

```python
from contextlib import ExitStack

import numpy as np

import concourse.bass as bass
from concourse import mybir

F32 = mybir.dt.float32
BF16 = mybir.dt.bfloat16
ALU = mybir.AluOpType
ACT = mybir.ActivationFunctionType
AX_X = mybir.AxisListType.X

NB = 16
T = 128
D = 256
DC = D // 128
CTX = 128
F = 1024
FC = F // 128
E = 8
R = 8
ER = E * R
LA = 96
HG = 4
GW = HG * T
PVW = 96
OVW = 32
SELF_H, SELF_D = 16, 16
CROSS_H, CROSS_D = 32, 8
LAT_H, KVR = 16, 64
QR = 128
NOPE = 128
VD = 128
LN_EPS = 1e-5
RMS_EPS = 1e-6
ROUND = 1.5 * 2.0 ** 23


class Seq:

    def __init__(self, pair, b):
        self.pair, self.b = pair, b
        self.n = pair * 2 + b

    def plus(self, k):
        return Seq(self.pair + (self.b + k) // 2, (self.b + k) % 2)

    def there(self):
        return not isinstance(self.n, int) or self.n >= 0


class Phase:

    def __init__(self, kind, index, totals, heads=0, dv=0, scale=1.0, causal=False):
        self.kind, self.index, self.heads, self.dv = kind, index, heads, dv
        self.scale, self.causal = scale, causal
        self.groups = heads // HG
        self.layer = index // 3
        self.base, self.per, self.totals = {}, {}, totals

    def signals(self, **per_sequence):
        for name, per in per_sequence.items():
            self.per[name] = per
            self.base[name] = self.totals.get(name, 0)
            self.totals[name] = self.base[name] + NB * per

    def at(self, name, s, k=None):
        per = self.per[name]
        k = per if k is None else k + 1
        return s.pair * (2 * per) + (self.base[name] + per * s.b + k)

    def dma(self, name, s):
        return s.pair * 16 + (self.base[name] // 2 * 16 + 16)


def walk_attention(eng, ph, steps):
    G = ph.groups
    between = {
        "self": {(0, 0): ["qkT+1"], (0, 1): ["oT0-1"], (1, 0): ["y-1"], (1, 1): ["v+1"], (2, 1): ["xT+2"],
                 (3, 0): ["qk+2"]},
        "cross": {(0, 0): ["xT+1"], (0, 2): ["oT0-1"], (1, 1): ["y-1"], (1, 2): ["qk+1"], (3, 2): ["qkT+1"],
                  (4, 2): ["v+1"]},
        "latent": {(0, 0): ["Q0+1", "oT0-1"], (0, 2): ["K0+1", "oT1-1"], (1, 0): ["Q1+1"], (1, 1): ["y-1"],
                   (1, 2): ["K1+1", "xT+2"], (2, 0): ["Q2+1"], (2, 1): ["down+2"], (2, 2): ["norm+2", "K2+1"],
                   (3, 0): ["Q3+1"], (3, 2): ["K3+1", "cT+2", "vl+2"]},
    }[ph.kind]

    def extra(s, place, back, ahead):
        for what in between.get(place, []):
            name, shift = what[:-2], int(what[-2:])
            if shift < 0 and not back or shift > ahead:
                continue
            if name[-1].isdigit():
                steps[name[:-1]](s.plus(shift), int(name[-1]))
            else:
                steps[name](s.plus(shift))

    def body(s, back=True, ahead=2):
        for g in range(G):
            steps["PT"](s, g)
            if ph.kind != "latent" and (g or back):
                steps["PO"](s if g else s.plus(-1), (g - 1) % G)
            extra(s, (g, 0), back, ahead)
            if g + 2 < G:
                steps["S"](s, g + 2)
            elif ahead:
                steps["S"](s.plus(1), g + 2 - G)
            extra(s, (g, 1), back, ahead)
            steps["PV"](s, g)
            extra(s, (g, 2), back, ahead)

    first = Seq(0, 0)
    steps["begin"]()
    second = first.plus(1)
    if ph.kind == "latent":
        for name in ("xT", "down", "norm", "cT", "vl"):
            steps[name](first)
        steps["Q"](first, 0)
        steps["xT"](second)
        steps["K"](first, 0)
        steps["Q"](first, 1)
        steps["down"](second)
        steps["S"](first, 0)
        steps["K"](first, 1)
        steps["norm"](second)
        steps["S"](first, 1)
        steps["Q"](first, 2)
        steps["cT"](second)
        steps["vl"](second)
        steps["K"](first, 2)
        steps["Q"](first, 3)
        steps["K"](first, 3)
    else:
        for name in ("xT", "qk", "qkT", "v"):
            steps[name](first)
        steps["S"](first, 0)
        steps["S"](first, 1)
        if ph.kind == "self":
            steps["xT"](second)
            steps["qk"](second)
    body(first, back=False)
    body(first.plus(1))
    with eng.Fori(1, NB // 2 - 1) as pair:
        body(Seq(pair, 0))
        body(Seq(pair, 1))
    body(first.plus(NB - 2), ahead=1)
    body(first.plus(NB - 1), ahead=0)
    if ph.kind != "latent":
        steps["PO"](first.plus(NB - 1), G - 1)
    for r in range(ph.per["oT_ps"]):
        steps["oT"](first.plus(NB - 1), r)
    steps["y"](first.plus(NB - 1))


def walk_ffn(eng, ph, steps, before, order, after):
    def body(s):
        for name, shift in order:
            t = s.plus(shift)
            if isinstance(t.n, int) and not 0 <= t.n < NB:
                continue
            steps[name](t)

    steps["begin"]()
    for n in range(-after, 2):
        body(Seq(0, 0).plus(n))
    with eng.Fori(1, NB // 2 - 1) as pair:
        body(Seq(pair, 0))
        body(Seq(pair, 1))
    for n in range(NB - 2, NB - before):
        body(Seq(0, 0).plus(n))


LORA_ORDER = [("H", 0), ("xT", 1), ("H1", 0), ("z2T", -1), ("ru", 1), ("D", 0), ("D1", 0), ("y", -1),
              ("Y", 0), ("zT", 1), ("Y1", 0)]
BIT_ORDER = [("y", -1), ("GV", 1), ("quant", 2), ("hT", 0), ("xqT", 2), ("act", 1)]


def walk(eng, ph, steps):
    if ph.kind == "lora":
        walk_ffn(eng, ph, steps, -1, LORA_ORDER, 1)
    elif ph.kind == "bit":
        walk_ffn(eng, ph, steps, -1, BIT_ORDER, 2)
    else:
        walk_attention(eng, ph, steps)


def bc(ap, axis, n):
    a = ap.unsqueeze(axis)
    shape = list(a.shape)
    shape[axis] = n
    return a.to_broadcast(shape)


def build_decoder(nc, ins, out, sublayers=6):
    totals = {}
    phases = [
        Phase("self", 0, totals, SELF_H, SELF_D, 1.0 / np.sqrt(SELF_D), True),
        Phase("cross", 1, totals, CROSS_H, CROSS_D, 1.0 / np.sqrt(CROSS_D)),
        Phase("lora", 2, totals),
        Phase("latent", 3, totals, LAT_H, KVR, 1.0 / np.sqrt(NOPE + KVR), True),
        Phase("cross", 4, totals, CROSS_H, CROSS_D, 1.0 / np.sqrt(CROSS_D)),
        Phase("bit", 5, totals),
    ][:sublayers]
    for ph in phases:
        G = ph.groups
        ph.signals(x_loaded=1, x_stored=1, xb_ready=1, y_ps=1, z_ready=1, stats=2, rstd=3, xn_ready=1)
        if ph.kind in ("self", "cross", "latent"):
            ph.signals(xT_ps=1, xT_sb=1, s_ps=G, row_max=G, s_sub=G, p_exp=G, pT_ps=2 * G, pT_sb=2 * G, pv_ps=G,
                       rec=G, o_norm=G, oT_ps=ph.heads * ph.dv // 512 or 1,
                       oT_sb=ph.heads * ph.dv // 512 or 1)
        if ph.kind in ("self", "cross"):
            ph.signals(v_ps=1, v_sb=1, ov_sb=G, po_ps=G, qk_ps=1, qk_sb=1, qkT_ps=1, qkT_sb=1, k_diag=G)
        if ph.kind == "cross":
            ph.signals(ctx_loaded=1, qk_read=3)
        if ph.kind == "latent":
            ph.signals(down_ps=1, sumsq=2, rms=3, c_read=5, c_sb=2, cT_ps=1, cT_sb=2, q_ps=G,
                       q_abs=G, q_read=3 * G, q_sb=G, qT_ps=G, qT_sb=G)
        if ph.kind == "lora":
            ph.signals(xT_ps=1, xT_sb=1, ru_ps=1, route=19, r_exp=1, zT_ps=1, zT_sb=1, h_ps=2, h0=2, d_ps=2,
                       h1=2, yk_ps=2, mix=5, z2T_ps=1, z2T_sb=1)
        if ph.kind == "bit":
            ph.signals(quant=8, xqT_ps=1, xqT_sb=1, gv_ps=4, gpre=2, silu=2, val=2, h_ready=1, hquant=5,
                       h_round=1, hq_ready=1, hT_ps=1, hT_sb=1)

    with ExitStack() as ctx:
        def sb(name, shape, dt=F32):
            return ctx.enter_context(nc.sbuf_tensor(name, shape, dt))

        bank = [ctx.enter_context(nc.psum_tensor(f"bank{i}", [128, 512], F32)) for i in range(8)]
        s_bank, pT_bank, pv_bank = bank[0:2], bank[2:4], bank[4:6]
        front, back = bank[6], bank[7]

        ident = sb("ident", [128, 128])
        identb = sb("identb", [128, 128], BF16)
        causal = sb("causal", [128, HG, T], BF16)
        self_mask = sb("self_mask", [128, 8])
        cross_mask = sb("cross_mask", [128, 16])
        lat_cos = sb("lat_cos", [T, 2 * 32])
        lat_sin = sb("lat_sin", [T, 2 * 32])
        minus_half = sb("minus_half", [128, 2])
        ln_eps = sb("ln_eps", [128, 1])
        rms_eps = sb("rms_eps", [128, 2])
        inv_rank = sb("inv_rank", [128, 2])
        round_bias = sb("round_bias", [128, 1])

        x_all = sb("x_all", [T, NB, D])
        xs = sb("xs", [T, 2, D])
        xb = sb("xb", [T, 2, D])
        xT = sb("xT", [128, 2, DC, T])
        z = sb("z", [T, 2, D])
        stat6 = sb("stat6", [T, 2, 6])
        mv = sb("mv", [T, 2, 2])
        rs = sb("rs", [T, 2, 2])
        zc = sb("zc", [T, 2, D])
        xn = sb("xn", [T, 2, D])
        spare = sb("spare", [T, 1])

        ctxT = sb("ctxT", [CTX, 2, T])
        qk = sb("qk", [T, 2, 4, 128])
        rot_a = sb("rot_a", [T, 2, 4, 128])
        rot_b = sb("rot_b", [T, 2, 4, 128])
        qkT = sb("qkT", [128, 2, 4, T])
        kdiag = sb("kdiag", [128, 2, CROSS_H, T])
        row_max = sb("row_max", [T, 2, HG])
        shifted = sb("shifted", [T, 2, HG, T])
        probs = sb("probs", [T, 2, HG, T])
        probsT = sb("probsT", [T, 2, HG, T])
        rec = sb("rec", [T, 2, HG])
        o_sb = sb("o_sb", [T, 2, LAT_H * KVR])
        oT = sb("oT", [128, 2, 8, T])
        v_self = sb("v_self", [T, 2, SELF_H * (SELF_D + 1) + OVW])
        v_cross = sb("v_cross", [T, 2, CROSS_H * (CROSS_D + 1) + OVW])
        ov_sb = sb("ov_sb", [128, 2, T])
        v_lat = sb("v_lat", [T, 2, PVW])
        cos_x = sb("cos_x", [T, NB, 4])
        sin_x = sb("sin_x", [T, NB, 2, 4])
        ang = sb("ang", [T, 2, NB, 4])
        turns = sb("turns", [T, 2, NB, 4])

        ssq = sb("ssq", [T, 2, 2])
        rms = sb("rms", [T, 2, 2])
        junk = sb("junk", [T, QR])
        c_sb = sb("c_sb", [T, 2, 256])
        kr_a = sb("kr_a", [T, 2, 64])
        kr_b = sb("kr_b", [T, 2, 64])
        qcT = sb("qcT", [QR, 2, T])
        kT = sb("kT", [128, 2, T])
        q_sb = rot_a
        pe_a = rot_b[:, :, 0:2, :].rearrange("p b c (a d) -> p b (c a) d", a=2)
        pe_b = rot_b[:, :, 2:4, :].rearrange("p b c (a d) -> p b (c a) d", a=2)

        logit = sb("logit", [T, 2, E])
        r1 = sb("r1", [T, 2, 8])
        expd = sb("expd", [T, 2, E])
        prob = sb("prob", [T, 2, E])
        key = sb("key", [T, 2, 2, E])
        prob2 = sb("prob2", [T, 2, E])
        onehot = sb("onehot", [T, 2, 2, E])
        weighted = sb("weighted", [T, 2, 2, E])
        descend = sb("descend", [T, E])
        zcat = sb("zcat", [T, 2, 2, LA])
        ztmp = sb("ztmp", [T, 2, ER])
        zT = sb("zT", [LA, 2, 2, T])
        z2cat = sb("z2cat", [T, 2, LA])
        z2T = sb("z2T", [LA, 2, T])
        u2 = sb("u2", [T, 2, 2, ER])
        part = shifted[:].rearrange("p b (k c) t -> p b k (c t)", k=2)

        q1 = sb("q1", [T, 2, 8])
        q2 = sb("q2", [T, 2, 8])
        xq_f = sb("xq_f", [T, 2, D])
        xq = sb("xq", [T, 2, D], BF16)
        xqT = sb("xqT", [128, 2, DC, T], BF16)
        hq = o_sb[:, 0, :].bitcast(BF16).rearrange("p (b f) -> p b f", b=2)
        hqT = oT[:, 0, :, :].rearrange("p c t -> p (c t)").bitcast(BF16).rearrange(
            "p (b c t) -> p b c t", b=2, c=FC)
        w_stat = sb("w_stat", [128, 3])
        ones = sb("ones", [128, 128])
        gamma = sb("gamma", [128, 4, 3])

        w = {}
        for name, shape, dt in WEIGHT_TILES:
            if name not in BIT_SHARED:
                w[name] = sb("w_" + name, shape, dt)
        w_cat = sb("w_cat", [QR, LAT_H, 128])
        w_vo = sb("w_vo", [128, LAT_H // 2, D])
        w["bit_gate"] = w["lora_w1"][:].rearrange("p c f -> p (c f)")
        w["bit_val"] = w["lora_w2"][:].rearrange("p c f -> p (c f)")[:, 0:DC * F]
        w["bit_out"] = w_cat[:].rearrange("p h c -> p (h c)")
        w["bit_bg"] = w_vo[:, 0:4, :].rearrange("p h c -> p (h c)")
        w["bit_bv"] = w_vo[:, 4:8, :].rearrange("p h c -> p (h c)")
        w_bit = [t[:].rearrange("p b c t -> p (b c t)").bitcast(BF16) for t in (shifted, probs, probsT)]

        kd = [kdiag[:, b].rearrange("p h t -> p (h t)") for b in range(2)]
        qT = [kd[b][:, 0:LAT_H * T].rearrange("p (h t) -> p h t", h=LAT_H) for b in range(2)]
        h_act = [kd[b][:, 0:2 * F].rearrange("p (k f t) -> p k f t", k=2, f=FC) for b in range(2)]
        g_pre = [kd[b][:, 0:F] for b in range(2)]
        g_act = [kd[b][:, F:2 * F] for b in range(2)]
        val = [kd[b][:, 2 * F:3 * F] for b in range(2)]
        hid = [kd[b][:, 3 * F:4 * F] for b in range(2)]
        lat_q_raw = o_sb[:].rearrange("p b c -> p (b c)").rearrange("p (h r) -> p h r", h=LAT_H)
        lat_kv_raw = kd[0][:, 2048:4096].rearrange("p (h e c) -> p h e c", h=LAT_H, e=2)
        lat_o_raw = [kd[1][:, 2048:4096].rearrange("p (h o) -> p h o", h=LAT_H // 2),
                     oT[:].rearrange("p b c t -> p (b c t)").rearrange("p (h o) -> p h o", h=LAT_H // 2)]

        sem = {}
        for name in list(totals):
            if name not in ("x_loaded", "x_stored", "ctx_loaded"):
                sem[name] = ctx.enter_context(nc.semaphore(name))
        x_loaded = [ctx.enter_context(nc.semaphore(f"x_loaded{b}")) for b in range(2)]
        x_stored = [ctx.enter_context(nc.semaphore(f"x_stored{b}")) for b in range(2)]
        ctx_loaded = [ctx.enter_context(nc.semaphore(f"ctx_loaded{b}")) for b in range(2)]
        consts_in = ctx.enter_context(nc.semaphore("consts_in"))
        weights_in = [ctx.enter_context(nc.semaphore(f"weights_in{i}")) for i in range(6)]
        raw_in = ctx.enter_context(nc.semaphore("raw_in"))
        filled = ctx.enter_context(nc.semaphore("filled"))
        tables = ctx.enter_context(nc.semaphore("tables"))
        angles = ctx.enter_context(nc.semaphore("angles"))
        table_sin = ctx.enter_context(nc.semaphore("table_sin"))
        prep_ps = ctx.enter_context(nc.semaphore("prep_ps"))
        prep_sb = ctx.enter_context(nc.semaphore("prep_sb"))
        wsum = ctx.enter_context(nc.semaphore("wsum"))
        wsum_ps = ctx.enter_context(nc.semaphore("wsum_ps"))

        weight_dmas = [[n for n, i in WEIGHT_PHASE if i == p] for p in range(6)]
        N_CONST = len(CONSTS)
        FILLS = 13
        last = phases[-1]

        def all_done(eng, ph):
            if ph.index:
                eng.wait_ge(sem["xn_ready"], ph.base["xn_ready"])

        block = ctx.enter_context(nc.Block())

        @block.sync
        def _(sp):
            const_tiles = {"ident": ident, "identb": identb, "causal": causal, "self_mask": self_mask,
                           "cross_mask": cross_mask, "lat_cos": lat_cos, "lat_sin": lat_sin,
                           "descend": descend}

            def load_weights(p):
                for name in weight_dmas[p]:
                    sp.dma_start(w[name][:], ins[name]).then_inc(weights_in[p], 16)

            for name in CONSTS:
                tile = ang[:, 0, :, 0:2] if name == "pos" else const_tiles[name][:]
                sp.dma_start(tile, ins[name]).then_inc(consts_in, 16)
            for ph in phases:
                def load(s, ph=ph):
                    old, q = (s.plus(-2), ph) if s.plus(-2).there() else (Seq(NB // 2 - 1, s.b), phases[ph.index - 1])
                    if ph.index or s.plus(-2).there():
                        sp.wait_ge(sem["xb_ready"], q.at("xb_ready", old))
                        if q.kind == "bit":
                            sp.wait_ge(sem["quant"], q.at("quant", old))
                        else:
                            sp.wait_ge(sem["xT_ps"], q.at("xT_ps", old))
                    if ph.index and not s.plus(-2).there():
                        sp.wait_ge(x_stored[s.b], q.dma("x_stored", s))
                    src = ins["x"][:, s.n, :] if ph.index == 0 else x_all[:, s.n, :]
                    sp.dma_start(xs[:, s.b, :], src).then_inc(x_loaded[s.b], 16)
                    if ph.kind == "cross":
                        if s.plus(-2).there():
                            sp.wait_ge(sem["qk_ps"], ph.at("qk_ps", s.plus(-2)))
                            sp.wait_ge(sem["v_ps"], ph.at("v_ps", s.plus(-2)))
                        sp.dma_start(ctxT[:, s.b, :], ins["ctxT"][:, s.n, :]).then_inc(ctx_loaded[s.b], 16)

                def store(s, ph=ph):
                    sp.wait_ge(sem["xn_ready"], ph.at("xn_ready", s))
                    dst = out[:, s.n, :] if ph is last else x_all[:, s.n, :]
                    sp.dma_start(dst, xn[:, s.b, :]).then_inc(x_stored[s.b], 16)

                first = Seq(0, 0)
                if ph.index == 0:
                    load(first)
                    load(first.plus(1))
                if ph.index:
                    load(first)
                    load(first.plus(1))
                    last_stores()
                    for b in range(2):
                        sp.wait_ge(x_stored[b], ph.index * (NB // 2) * 16)
                if ph.index == 0:
                    for p in range(min(5, len(phases))):
                        load_weights(p)
                if ph.index == 4 and len(phases) > 5:
                    load_weights(5)
                if ph.index == 2 and len(phases) > 3:
                    sp.dma_start(lat_q_raw, ins["lat_q"]).then_inc(raw_in, 16)
                    sp.dma_start(lat_kv_raw, ins["lat_kv"]).then_inc(raw_in, 16)
                    for i in range(2):
                        sp.dma_start(lat_o_raw[i], ins["lat_o"][:, 8 * i:8 * i + 8, :]).then_inc(raw_in, 16)
                    sp.dma_start(w_cat[:, :, 64:128], ins["lat_rope"]).then_inc(raw_in, 16)
                load(first.plus(2))
                for n in range(2):
                    load(first.plus(n + 3))
                    store(first.plus(n))
                with sp.Fori(1, NB // 2 - 2) as pair:
                    for b in range(2):
                        load(Seq(pair, b).plus(3))
                        store(Seq(pair, b))
                load(first.plus(NB - 1))
                for n in range(NB - 4, NB - 2):
                    store(first.plus(n))

                def last_stores(store=store):
                    for n in range(NB - 2, NB):
                        store(Seq(0, 0).plus(n))

            last_stores()
            for b in range(2):
                sp.wait_ge(x_stored[b], len(phases) * (NB // 2) * 16)

        @block.tensor
        def _(pe):
            pe.wait_ge(consts_in, 16 * N_CONST)
            for ph in phases:
                def begin(ph=ph):
                    all_done(pe, ph)
                    pe.wait_ge(weights_in[ph.index], 16 * len(weight_dmas[ph.index]))
                    pe.wait_ge(filled, FILLS)
                    if ph.kind == "latent":
                        pe.wait_ge(raw_in, 80)
                        for h in range(LAT_H):
                            mm = pe.matmul(bank[h // 8][:, (h % 8) * 64:(h % 8) * 64 + 64],
                                           lat_q_raw[:, h, :], lat_kv_raw[:, h, 0, :], start=True, stop=True)
                            if h % 8 == 7:
                                mm.then_inc(prep_ps, 1)
                        for h in range(LAT_H):
                            p0 = 64 * (h % 2)
                            mm = pe.matmul(bank[2 + h // 4][p0:p0 + 64, (h // 2 % 2) * D:(h // 2 % 2) * D + D],
                                           lat_kv_raw[:, h, 1, :], lat_o_raw[h // 8][:, h % 8, :], start=True, stop=True)
                            if h % 4 == 3:
                                mm.then_inc(prep_ps, 1)
                        pe.wait_ge(prep_sb, 6)
                    if ph.kind == "bit":
                        pe.wait_ge(wsum, 1)
                        pe.matmul(bank[0][:, 0:3], ones[:, :], w_stat[:, :], start=True,
                                  stop=True).then_inc(wsum_ps, 1)
                        pe.wait_ge(wsum, WSUM_STEPS)

                def xT_step(s, ph=ph):
                    pe.wait_ge(x_loaded[s.b], ph.dma("x_loaded", s))
                    if s.plus(-1).there():
                        if ph.kind in ("self", "cross"):
                            pe.wait_ge(sem["v_sb"], ph.at("v_sb", s.plus(-1)))
                        elif ph.kind == "lora":
                            pe.wait_ge(sem["zT_sb"], ph.at("zT_sb", s.plus(-1)))
                        elif s.plus(-3).there():
                            pe.wait_ge(sem["z_ready"], ph.at("z_ready", s.plus(-3)))
                        else:
                            pe.wait_ge(sem["cT_sb"], ph.at("cT_sb", s.plus(-1)))
                    place = back if ph.kind == "latent" else front
                    for c in range(DC):
                        mm = pe.transpose(place[:, c * T:(c + 1) * T], xs[:, s.b, c * 128:(c + 1) * 128], ident[:, :])
                    mm.then_inc(sem["xT_ps"], 1)

                def v_step(s, ph=ph):
                    pe.wait_ge(sem["qkT_sb"], ph.at("qkT_sb", s))
                    if ph.kind == "self":
                        for c in range(DC):
                            mm = pe.matmul(front[:, 0:D], xT[:, s.b, c, :], w["self_qkv"][:, c, 2 * D:3 * D],
                                           start=(c == 0), stop=(c == DC - 1))
                    else:
                        mm = pe.matmul(front[:, 0:D], ctxT[:, s.b, :], w[f"cross{ph.layer}_kv"][:, D:2 * D],
                                       start=True, stop=True)
                    mm.then_inc(sem["v_ps"], 1)

                def qk_step(s, ph=ph):
                    pe.wait_ge(sem["xT_sb"], ph.at("xT_sb", s))
                    if ph.kind == "self":
                        for c in range(DC):
                            mm = pe.matmul(front[:, :], xT[:, s.b, c, :], w["self_qkv"][:, c, 0:2 * D],
                                           start=(c == 0), stop=(c == DC - 1))
                    else:
                        pe.wait_ge(ctx_loaded[s.b], ph.dma("ctx_loaded", s))
                        for c in range(DC):
                            pe.matmul(front[:, 0:D], xT[:, s.b, c, :], w[f"cross{ph.layer}_q"][:, c, :],
                                      start=(c == 0), stop=(c == DC - 1))
                        mm = pe.matmul(front[:, D:2 * D], ctxT[:, s.b, :], w[f"cross{ph.layer}_kv"][:, 0:D],
                                       start=True, stop=True)
                    mm.then_inc(sem["qk_ps"], 1)

                def qkT_step(s, ph=ph):
                    pe.wait_ge(sem["qk_sb"], ph.at("qk_sb", s))
                    for c in range(4):
                        mm = pe.transpose(front[:, c * T:(c + 1) * T], qk[:, s.b, c, :], ident[:, :])
                    mm.then_inc(sem["qkT_ps"], 1)

                def down(s, ph=ph):
                    pe.wait_ge(sem["xT_sb"], ph.at("xT_sb", s))
                    for c in range(DC):
                        mm = pe.matmul(back[:, 0:256], xT[:, s.b, c, :], w["lat_down"][:, c, :],
                                       start=(c == 0), stop=(c == DC - 1))
                    mm.then_inc(sem["down_ps"], 1)

                def cT(s, ph=ph):
                    pe.wait_ge(sem["c_sb"], ph.at("c_sb", s, 0))
                    pe.wait_ge(sem["c_read"], ph.at("c_read", s))
                    for c in range(2):
                        mm = pe.transpose(back[:, c * T:(c + 1) * T], c_sb[:, s.b, c * 128:(c + 1) * 128], ident[:, :])
                    mm.then_inc(sem["cT_ps"], 1)

                def Q(s, g, ph=ph):
                    if g == 0:
                        pe.wait_ge(sem["cT_sb"], ph.at("cT_sb", s))
                        if s.plus(-1).there():
                            pe.wait_ge(sem["qT_sb"], ph.at("qT_sb", s.plus(-1)))
                    else:
                        pe.wait_ge(sem["qT_sb"], ph.at("qT_sb", s, g - 1))
                    pe.matmul(front[:, :], qcT[:, s.b, :],
                              w_cat[:, HG * g:HG * (g + 1), :].rearrange("p h c -> p (h c)"),
                              start=True, stop=True).then_inc(sem["q_ps"], 1)

                def K(s, g, ph=ph):
                    pe.wait_ge(sem["q_sb"], ph.at("q_sb", s, g))
                    pe.wait_ge(sem["q_abs"], ph.at("q_abs", s, g))
                    for j in range(HG):
                        mm = pe.transpose(front[:, j * T:(j + 1) * T], q_sb[:, g % 2, j, :], ident[:, :])
                    mm.then_inc(sem["qT_ps"], 1)

                def S(s, g, ph=ph):
                    if s.plus(-1).there() or g >= 2:
                        pe.wait_ge(sem["s_sub"], ph.at("s_sub", s, g - 2))
                    if ph.kind == "latent":
                        pe.wait_ge(sem["qT_sb"], ph.at("qT_sb", s, g))
                    else:
                        pe.wait_ge(sem["qkT_sb"], ph.at("qkT_sb", s))
                        pe.wait_ge(sem["k_diag"], ph.at("k_diag", s, g))
                    sbank = s_bank[g % 2]
                    if ph.causal:
                        pe.matmul(sbank[:, :], identb[:, :], causal[:, :, :].rearrange("p h t -> p (h t)"),
                                  start=True, stop=False)
                    if ph.kind == "latent":
                        for j in range(HG):
                            mm = pe.matmul(sbank[:, j * T:(j + 1) * T], qT[s.b][:, HG * g + j, :], kT[:, s.b, :],
                                           start=False, stop=(j == HG - 1))
                    else:
                        chunk = g // (ph.groups // 2)
                        mm = pe.matmul(sbank[:, :], qkT[:, s.b, chunk, :],
                                       kdiag[:, s.b, HG * g:HG * (g + 1), :].rearrange("p h t -> p (h t)"),
                                       start=not ph.causal, stop=True)
                    mm.then_inc(sem["s_ps"], 1)

                def PT(s, g, ph=ph):
                    pe.wait_ge(sem["p_exp"], ph.at("p_exp", s, g))
                    for j in range(HG):
                        if j % 2 == 0 and (s.plus(-1).there() or g):
                            pe.wait_ge(sem["pT_sb"], ph.at("pT_sb", s, 2 * g - 2 + j // 2))
                        mm = pe.transpose(pT_bank[j // 2][:, j % 2 * T:(j % 2 + 1) * T], probs[:, g % 2, j, :],
                                          ident[:, :])
                        if j % 2:
                            mm.then_inc(sem["pT_ps"], 1)

                def PV(s, g, ph=ph):
                    if g == 0:
                        name = "c_sb" if ph.kind == "latent" else "v_sb"
                        pe.wait_ge(sem[name], ph.at(name, s))
                    if s.plus(-1).there() or g >= 2:
                        pe.wait_ge(sem["o_norm"], ph.at("o_norm", s, g - 2))
                    for j in range(HG):
                        if j % 2 == 0:
                            pe.wait_ge(sem["pT_sb"], ph.at("pT_sb", s, 2 * g + j // 2))
                        h = HG * g + j
                        if ph.kind == "latent":
                            mm = pe.matmul(pv_bank[g % 2][:, j * PVW:(j + 1) * PVW], probsT[:, g % 2, j, :],
                                           v_lat[:, s.b, :], start=True, stop=True)
                        else:
                            v, step = (v_self, SELF_D + 1) if ph.kind == "self" else (v_cross, CROSS_D + 1)
                            mm = pe.matmul(pv_bank[g % 2][OVW * j:OVW * (j + 1), 0:T],
                                           v[:, s.b, h * step:h * step + OVW], probsT[:, g % 2, j, :],
                                           start=True, stop=True)
                    mm.then_inc(sem["pv_ps"], 1)

                def PO(s, g, ph=ph):
                    pe.wait_ge(sem["ov_sb"], ph.at("ov_sb", s, g))
                    pe.transpose(pv_bank[g % 2][:, T:2 * T], ov_sb[:, g % 2, :], ident[:, :]).then_inc(sem["po_ps"], 1)

                def oT_step(s, r, ph=ph):
                    chunks = ph.heads * ph.dv // 128
                    if r == 0:
                        pe.wait_ge(sem["o_norm"], ph.at("o_norm", s))
                        if s.plus(-1).there():
                            pe.wait_ge(sem["z_ready"], ph.at("z_ready", s.plus(-1)))
                        if ph.kind == "latent" and not (isinstance(s.n, int) and s.n + 2 >= NB):
                            pe.wait_ge(sem["cT_sb"], ph.at("cT_sb", s.plus(2)))
                    else:
                        pe.wait_ge(sem["oT_sb"], ph.at("oT_sb", s, r - 1))
                    for c in range(4 * r, min(chunks, 4 * r + 4)):
                        mm = pe.transpose(back[:, c % 4 * T:(c % 4 + 1) * T], o_sb[:, s.b, c * 128:(c + 1) * 128],
                                          ident[:, :])
                        if c % 4 == 3 or c == chunks - 1:
                            mm.then_inc(sem["oT_ps"], 1)

                def y_step(s, ph=ph):
                    if ph.kind == "lora":
                        pe.wait_ge(sem["z2T_sb"], ph.at("z2T_sb", s))
                        mm = pe.matmul(back[:, 0:D], z2T[:, s.b, :], w["lora_b2"][:, :], start=True, stop=True)
                    elif ph.kind == "bit":
                        pe.wait_ge(sem["hT_sb"], ph.at("hT_sb", s))
                        if s.plus(-1).there():
                            pe.wait_ge(sem["z_ready"], ph.at("z_ready", s.plus(-1)))
                        for c in range(FC):
                            mm = pe.matmul(back[:, 0:D], hqT[:, s.b, c, :],
                                           w_bit[2][:, c * D:(c + 1) * D], start=(c == 0), stop=(c == FC - 1))
                    else:
                        chunks = ph.heads * ph.dv // 128
                        wo = {"self": w["self_o"], "cross": w[f"cross{ph.layer}_o"], "latent": w_vo}[ph.kind]
                        pe.wait_ge(sem["oT_sb"], ph.at("oT_sb", s))
                        for c in range(chunks):
                            mm = pe.matmul(back[:, 0:D], oT[:, s.b, c, :], wo[:, c, :],
                                           start=(c == 0), stop=(c == chunks - 1))
                    mm.then_inc(sem["y_ps"], 1)

                def ru(s, ph=ph):
                    pe.wait_ge(sem["xT_sb"], ph.at("xT_sb", s))
                    for c in range(DC):
                        mm = pe.matmul(front[:, 0:LA], xT[:, s.b, c, :], w["lora_ru"][:, c, :],
                                       start=(c == 0), stop=(c == DC - 1))
                    mm.then_inc(sem["ru_ps"], 1)

                def zT_step(s, ph=ph):
                    pe.wait_ge(sem["route"], ph.at("route", s))
                    for k in range(2):
                        mm = pe.transpose(front[0:LA, k * T:(k + 1) * T], zcat[:, s.b, k, :], ident[:, :])
                    mm.then_inc(sem["zT_ps"], 1)

                def H(s, q=0, ph=ph):
                    pe.wait_ge(sem["zT_sb"], ph.at("zT_sb", s))
                    if s.plus(-1).there():
                        pe.wait_ge(sem["h1"], ph.at("h1", s.plus(-1), q))
                    for f in range(4):
                        cols = slice((4 * q + f) * 128, (4 * q + f + 1) * 128)
                        for c in range(DC):
                            pe.matmul(bank[q][:, f * T:(f + 1) * T], w["lora_w1"][:, c, cols], xT[:, s.b, c, :],
                                      start=(f == 0 and c == 0), stop=False, skip_group_check=True)
                        mm = pe.matmul(bank[q][:, f * T:(f + 1) * T], w["lora_b1"][:, cols], zT[:, s.b, 0, :],
                                       start=False, stop=True, skip_group_check=True)
                    mm.then_inc(sem["h_ps"], 1)

                def Dl(s, q=0, ph=ph):
                    pe.wait_ge(sem["h0"], ph.at("h0", s, q))
                    for f in range(4):
                        cols = slice((4 * q + f) * 128, (4 * q + f + 1) * 128)
                        mm = pe.matmul(bank[q][:, f * T:(f + 1) * T], w["lora_b1"][:, cols], zT[:, s.b, 1, :],
                                       start=False, stop=True, skip_group_check=True)
                    mm.then_inc(sem["d_ps"], 1)

                def Yk(s, k=0, ph=ph):
                    pe.wait_ge(sem["h1" if k else "h0"], ph.at("h1" if k else "h0", s))
                    if s.plus(-1).there():
                        pe.wait_ge(sem["mix"], ph.at("mix", s.plus(-1)))
                    for f in range(FC):
                        mm = pe.matmul(bank[4 + k][:, 0:D + ER], h_act[s.b][:, k, f, :], w["lora_w2"][:, f, :],
                                       start=(f == 0), stop=(f == FC - 1))
                    mm.then_inc(sem["yk_ps"], 1)

                def z2T_step(s, ph=ph):
                    pe.wait_ge(sem["mix"], ph.at("mix", s))
                    if s.plus(-1).there():
                        pe.wait_ge(sem["z_ready"], ph.at("z_ready", s.plus(-1)))
                    pe.transpose(back[0:LA, 0:T], z2cat[:, s.b, :], ident[:, :]).then_inc(sem["z2T_ps"], 1)

                def xqT_step(s, ph=ph):
                    pe.wait_ge(sem["quant"], ph.at("quant", s))
                    if s.plus(-1).there():
                        pe.wait_ge(sem["xqT_sb"], ph.at("xqT_sb", s.plus(-1)))
                    fb = front[:, :].bitcast(BF16)
                    for c in range(DC):
                        mm = pe.transpose(fb[:, c * T:(c + 1) * T], xq[:, s.b, c * 128:(c + 1) * 128], identb[:, :])
                    mm.then_inc(sem["xqT_ps"], 1)

                def GV(s, ph=ph):
                    pe.wait_ge(sem["xqT_sb"], ph.at("xqT_sb", s))
                    for e in range(2):
                        for q in range(2):
                            if s.plus(-1).there():
                                name = "val" if e else "gpre"
                                pe.wait_ge(sem[name], ph.at(name, s.plus(-1), q))
                            for c in range(DC):
                                mm = pe.matmul(bank[2 * e + q][:, :], xqT[:, s.b, c, :],
                                               w_bit[e][:, c * F + q * 512:c * F + (q + 1) * 512],
                                               start=(c == 0), stop=(c == DC - 1))
                            mm.then_inc(sem["gv_ps"], 1)

                def hT_step(s, ph=ph):
                    pe.wait_ge(sem["hq_ready"], ph.at("hq_ready", s))
                    if s.plus(-1).there():
                        pe.wait_ge(sem["hT_sb"], ph.at("hT_sb", s.plus(-1)))
                    hb = bank[4][:, :].bitcast(BF16)
                    for c in range(FC):
                        mm = pe.transpose(hb[:, c * T:(c + 1) * T], hq[:, s.b, c * 128:(c + 1) * 128], identb[:, :])
                    mm.then_inc(sem["hT_ps"], 1)

                nothing = lambda *a: None
                walk(pe, ph, {
                    "begin": begin, "xT": xT_step, "v": v_step, "qk": qk_step, "qkT": qkT_step, "down": down,
                    "cT": cT, "norm": nothing, "vl": nothing, "Q": Q, "K": K, "S": S, "PT": PT, "PV": PV, "PO": PO, "oT": oT_step, "y": y_step,
                    "ru": ru, "zT": zT_step, "H": H, "H1": lambda s: H(s, 1), "D": Dl, "D1": lambda s: Dl(s, 1),
                    "Y": Yk, "Y1": lambda s: Yk(s, 1), "z2T": z2T_step, "quant": nothing, "xqT": xqT_step,
                    "GV": GV, "act": nothing, "hT": hT_step})

        @block.scalar
        def _(act):
            if len(phases) > 1:
                act.wait_ge(angles, 1)
                nc.scalar.activation(turns[:, :, :, :], ang[:, :, :, :], ACT.Sin).then_inc(table_sin, 1)
            for ph in phases:
                def begin(ph=ph):
                    all_done(act, ph)
                    if ph.kind == "latent":
                        act.wait_ge(weights_in[3], 16 * len(weight_dmas[3]))
                        for b in range(2):
                            act.wait_ge(prep_ps, b + 1)
                            nc.scalar.copy(w_cat[:, 8 * b:8 * b + 8, 0:64],
                                           bank[b][:, :].rearrange("p (h c) -> p h c", h=8)).then_inc(prep_sb, 1)
                        for b in range(4):
                            act.wait_ge(prep_ps, b + 3)
                            nc.scalar.copy(w_vo[:, 2 * b:2 * b + 2, :],
                                           bank[2 + b][:, :].rearrange("p (h c) -> p h c", h=2)).then_inc(prep_sb, 1)

                def xT_step(s, ph=ph):
                    act.wait_ge(sem["xT_ps"], ph.at("xT_ps", s))
                    if s.plus(-2).there():
                        name = {"self": "v_ps", "cross": "qk_ps", "latent": "down_ps", "lora": "h_ps"}[ph.kind]
                        act.wait_ge(sem[name], ph.at(name, s.plus(-2)))
                    place = back if ph.kind == "latent" else front
                    nc.scalar.copy(xT[:, s.b, :, :].rearrange("p c t -> p (c t)"),
                                   place[:, 0:DC * T]).then_inc(sem["xT_sb"], 1)

                def v_step(s, ph=ph):
                    if ph.kind == "cross":
                        act.wait_ge(sem["v_ps"], ph.at("v_ps", s))
                        if s.plus(-2).there():
                            act.wait_ge(sem["pv_ps"], ph.at("pv_ps", s.plus(-2)))
                        else:
                            act.wait_ge(filled, FILLS)
                        v = v_cross[:, s.b, 0:CROSS_H * (CROSS_D + 1)].rearrange("p (h d) -> p h d", h=CROSS_H)
                        nc.scalar.copy(v[:, :, 0:CROSS_D],
                                       front[:, 0:D].rearrange("p (h d) -> p h d", h=CROSS_H)).then_inc(sem["v_sb"], 1)

                def qkT_step(s, ph=ph):
                    act.wait_ge(sem["qkT_ps"], ph.at("qkT_ps", s))
                    if s.plus(-2).there():
                        act.wait_ge(sem["s_ps"], ph.at("s_ps", s.plus(-2)))
                        act.wait_ge(sem["k_diag"], ph.at("k_diag", s.plus(-2)))
                    nc.scalar.copy(qkT[:, s.b, :, :].rearrange("p c t -> p (c t)"),
                                   front[:, :]).then_inc(sem["qkT_sb"], 1)

                def down(s, ph=ph):
                    act.wait_ge(sem["down_ps"], ph.at("down_ps", s))
                    if s.plus(-2).there():
                        act.wait_ge(sem["rms"], ph.at("rms", s.plus(-2)))
                    for k, (a, e) in enumerate(((0, QR), (QR, QR + KVR))):
                        if s.plus(-1).there() or k:
                            act.wait_ge(sem["sumsq"], ph.at("sumsq", s, k - 1))
                        nc.scalar.activation(junk[:, 0:e - a], back[:, a:e], ACT.Square,
                                             accum_out=ssq[:, s.b, k:k + 1]).then_inc(sem["sumsq"], 1)

                def cT(s, ph=ph):
                    act.wait_ge(sem["cT_ps"], ph.at("cT_ps", s))
                    if s.plus(-2).there():
                        act.wait_ge(sem["q_ps"], ph.at("q_ps", s.plus(-2)))
                        act.wait_ge(sem["s_ps"], ph.at("s_ps", s.plus(-2)))
                    nc.scalar.activation(qcT[:, s.b, :], back[:, 0:T], ACT.Copy,
                                         scale=w["lat_qn"][:, 0:1]).then_inc(sem["cT_sb"], 1)
                    nc.scalar.copy(kT[:, s.b, :], back[:, T:2 * T]).then_inc(sem["cT_sb"], 1)

                def Q(s, g, ph=ph):
                    act.wait_ge(sem["q_read"], ph.at("q_read", s, 3 * g + 2))
                    if s.plus(-1).there() or g >= 2:
                        act.wait_ge(sem["qT_ps"], ph.at("qT_ps", s, g - 2))
                    fr = front[:, :].rearrange("p (h c) -> p h c", h=HG)
                    nc.scalar.copy(q_sb[:, g % 2, :, 0:64], fr[:, :, 0:64]).then_inc(sem["q_abs"], 1)

                def K(s, g, ph=ph):
                    act.wait_ge(sem["qT_ps"], ph.at("qT_ps", s, g))
                    if s.plus(-2).there():
                        act.wait_ge(sem["s_ps"], ph.at("s_ps", s.plus(-2), g))
                    nc.scalar.copy(qT[s.b][:, HG * g:HG * (g + 1), :],
                                   front[:, :].rearrange("p (h t) -> p h t", h=HG)).then_inc(sem["qT_sb"], 1)

                def exp(s, g, ph=ph):
                    act.wait_ge(sem["s_sub"], ph.at("s_sub", s, g))
                    if s.plus(-1).there() or g >= 2:
                        act.wait_ge(sem["pT_ps"], ph.at("pT_ps", s, 2 * g - 3))
                    nc.scalar.activation(probs[:, g % 2, :, :], shifted[:, g % 2, :, :], ACT.Exp,
                                         scale=float(ph.scale)).then_inc(sem["p_exp"], 1)

                def S(s, g, exp=exp):
                    if g == 0 and not s.plus(-1).there():
                        exp(s, g)

                def PT(s, g, ph=ph, exp=exp):
                    if s.plus(-1).there() or g >= 2:
                        act.wait_ge(sem["pv_ps"], ph.at("pv_ps", s, g - 2))
                    for j in range(2):
                        act.wait_ge(sem["pT_ps"], ph.at("pT_ps", s, 2 * g + j))
                        nc.scalar.copy(probsT[:, g % 2, 2 * j:2 * j + 2, :].rearrange("p h t -> p (h t)"),
                                       pT_bank[j][:, 0:2 * T]).then_inc(sem["pT_sb"], 1)
                    if g + 1 < ph.groups:
                        exp(s, g + 1)
                    elif not (isinstance(s.n, int) and s.n == NB - 1):
                        exp(s.plus(1), 0)

                def PV(s, g, ph=ph):
                    if ph.kind != "latent":
                        act.wait_ge(sem["pv_ps"], ph.at("pv_ps", s, g))
                        if s.plus(-1).there() or g >= 2:
                            act.wait_ge(sem["po_ps"], ph.at("po_ps", s, g - 2))
                        nc.scalar.copy(ov_sb[:, g % 2, :], pv_bank[g % 2][:, 0:T]).then_inc(sem["ov_sb"], 1)

                def oT_step(s, r, ph=ph):
                    m = min(4, ph.heads * ph.dv // 128 - 4 * r)
                    act.wait_ge(sem["oT_ps"], ph.at("oT_ps", s, r))
                    if s.plus(-2).there():
                        act.wait_ge(sem["y_ps"], ph.at("y_ps", s.plus(-2)))
                    nc.scalar.copy(oT[:, s.b, 4 * r:4 * r + m, :].rearrange("p c t -> p (c t)"),
                                   back[:, 0:m * T]).then_inc(sem["oT_sb"], 1)

                def ru(s, ph=ph):
                    act.wait_ge(sem["route"], ph.at("route", s, 1))
                    nc.scalar.activation(expd[:, s.b, :], logit[:, s.b, :], ACT.Exp, bias=r1[:, s.b, 0:1],
                                         accum_out=r1[:, s.b, 1:2]).then_inc(sem["r_exp"], 1)

                def zT_step(s, ph=ph):
                    act.wait_ge(sem["zT_ps"], ph.at("zT_ps", s))
                    if s.plus(-2).there():
                        act.wait_ge(sem["d_ps"], ph.at("d_ps", s.plus(-2)))
                    nc.scalar.copy(zT[:, s.b, :, :].rearrange("p k t -> p (k t)"),
                                   front[0:LA, 0:2 * T]).then_inc(sem["zT_sb"], 1)

                def hidden(s, k, q, ph=ph):
                    src = "d_ps" if k else "h_ps"
                    act.wait_ge(sem[src], ph.at(src, s, q))
                    if s.plus(-2).there():
                        act.wait_ge(sem["yk_ps"], ph.at("yk_ps", s.plus(-2), k))
                    nc.scalar.activation(h_act[s.b][:, k, 4 * q:4 * q + 4, :].rearrange("p f t -> p (f t)"),
                                         bank[q][:, :], ACT.Gelu_apprx_tanh).then_inc(sem["h1" if k else "h0"], 1)

                def z2T_step(s, ph=ph):
                    act.wait_ge(sem["z2T_ps"], ph.at("z2T_ps", s))
                    if s.plus(-2).there():
                        act.wait_ge(sem["y_ps"], ph.at("y_ps", s.plus(-2)))
                    nc.scalar.copy(z2T[:, s.b, :], back[0:LA, 0:T]).then_inc(sem["z2T_sb"], 1)

                def xqT_step(s, ph=ph):
                    act.wait_ge(sem["xqT_ps"], ph.at("xqT_ps", s))
                    if s.plus(-2).there():
                        act.wait_ge(sem["gv_ps"], ph.at("gv_ps", s.plus(-2)))
                    nc.scalar.copy(xqT[:, s.b, :, :].rearrange("p c t -> p (c t)"),
                                   front[:, :].bitcast(BF16)[:, 0:DC * T]).then_inc(sem["xqT_sb"], 1)

                def act_step(s, ph=ph):
                    for q in range(2):
                        act.wait_ge(sem["gpre"], ph.at("gpre", s, q))
                        if s.plus(-2).there():
                            act.wait_ge(sem["h_ready"], ph.at("h_ready", s.plus(-2)))
                        nc.scalar.activation(g_act[s.b][:, q * 512:(q + 1) * 512], g_pre[s.b][:, q * 512:(q + 1) * 512],
                                             ACT.Silu).then_inc(sem["silu"], 1)
                    act.wait_ge(sem["hquant"], ph.at("hquant", s, 3))
                    nc.scalar.activation(g_pre[s.b][:, :], hid[s.b][:, :], ACT.Copy, bias=ROUND,
                                         scale=q2[:, s.b, 3:4]).then_inc(sem["h_round"], 1)

                def hT_step(s, ph=ph):
                    act.wait_ge(sem["hT_ps"], ph.at("hT_ps", s))
                    if s.plus(-2).there():
                        act.wait_ge(sem["y_ps"], ph.at("y_ps", s.plus(-2)))
                    nc.scalar.copy(hqT[:, s.b, :, :].rearrange("p c t -> p (c t)"),
                                   bank[4][:, :].bitcast(BF16)).then_inc(sem["hT_sb"], 1)

                nothing = lambda *a: None
                walk(act, ph, {
                    "begin": begin, "xT": xT_step, "v": v_step, "qk": nothing, "qkT": qkT_step, "down": down,
                    "cT": cT, "norm": nothing, "vl": nothing, "Q": Q, "K": K, "S": S, "PT": PT, "PV": PV, "PO": nothing, "oT": oT_step, "y": nothing,
                    "ru": ru, "zT": zT_step, "H": lambda s: hidden(s, 0, 0), "H1": lambda s: hidden(s, 0, 1),
                    "D": lambda s: hidden(s, 1, 0), "D1": lambda s: hidden(s, 1, 1),
                    "Y": nothing, "Y1": nothing, "z2T": z2T_step, "quant": nothing, "xqT": xqT_step,
                    "GV": nothing, "act": act_step, "hT": hT_step})

        @block.vector
        def _(dve):
            V = nc.vector
            if len(phases) > 1:
                step = [0]

                def chain(ins):
                    step[0] += 1
                    ins.then_inc(tables, 1)
                    dve.wait_ge(tables, step[0])

                dve.wait_ge(consts_in, 16 * N_CONST)
                p01 = ang[:, 0, :, 0:2]
                t4 = turns[:, 1, :, :].rearrange("p n (a f) -> p n a f", a=2)
                a4 = [ang[:, e, :, :].rearrange("p n (a f) -> p n a f", a=2) for e in range(2)]
                for f in range(2):
                    chain(V.tensor_scalar(t4[:, :, :, f], p01, float(np.float32(10000.0) ** np.float32(-f / 2)),
                                          None, ALU.mult))
                for e in (1, 0):
                    chain(V.tensor_scalar(turns[:, 0], turns[:, 1], float(1 / (2 * np.pi)), 0.25 * e, ALU.mult, ALU.add))
                    chain(V.tensor_scalar(ang[:, e], turns[:, 0], ROUND, None, ALU.add))
                    chain(V.tensor_scalar(turns[:, 0], ang[:, e], ROUND, None, ALU.subtract))
                    chain(V.scalar_tensor_tensor(out=ang[:, e], in0=turns[:, 0], scalar=-TWO_PI[0], in1=turns[:, 1],
                                                 op0=ALU.mult, op1=ALU.add))
                    chain(V.scalar_tensor_tensor(out=ang[:, e], in0=turns[:, 0], scalar=-TWO_PI[1], in1=ang[:, e],
                                                 op0=ALU.mult, op1=ALU.add))
                    chain(V.scalar_tensor_tensor(out=ang[:, e], in0=turns[:, 0], scalar=-TWO_PI[2], in1=ang[:, e],
                                                 op0=ALU.mult, op1=ALU.add))
                    if e:
                        chain(V.tensor_scalar(ang[:, e], ang[:, e], float(np.pi / 2), None, ALU.add))
                V.tensor_scalar(ang[:, :, :, :], ang[:, :, :, :], PI_BELOW, -PI_BELOW, ALU.min,
                                ALU.max).then_inc(angles, 1)
                dve.wait_ge(table_sin, 1)
                V.tensor_copy(cos_x[:, :, :], turns[:, 1]).then_inc(tables, 1)
                V.tensor_copy(sin_x[:, :, 1, :], turns[:, 0]).then_inc(tables, 1)
                V.tensor_scalar(sin_x[:, :, 0, :], turns[:, 0], -1.0, None, ALU.mult).then_inc(tables, 1)
                dve.wait_ge(tables, step[0] + 3)

            for ph in phases:
                def begin(ph=ph):
                    all_done(dve, ph)
                    dve.wait_ge(consts_in, 16 * N_CONST)
                    dve.wait_ge(weights_in[ph.index], 16 * len(weight_dmas[ph.index]))
                    dve.wait_ge(filled, FILLS)
                    if ph.kind == "bit":
                        raws = [w["bit_gate"], w["bit_val"], w["bit_out"]]
                        for i, raw in enumerate(raws):
                            ins = V.tensor_reduce(w_stat[:, i:i + 1], raw[:, :], AX_X, ALU.add,
                                                  apply_absolute_value=True)
                        ins.then_inc(wsum, 1)
                        step = [1]

                        def chain(ins):
                            step[0] += 1
                            ins.then_inc(wsum, 1)
                            dve.wait_ge(wsum, step[0])

                        dve.wait_ge(wsum_ps, 1)
                        chain(V.tensor_scalar(gamma[:, 0], bank[0][:, 0:3], 1.0 / (D * F), 1e-5, ALU.mult, ALU.max))
                        chain(V.reciprocal(gamma[:, 1], gamma[:, 0]))
                        chain(V.tensor_scalar(gamma[:, 2], gamma[:, 0], 1.0 / 127.0, None, ALU.mult))
                        for i, raw in enumerate(raws):
                            chain(V.tensor_scalar(raw[:, :], raw[:, :], gamma[:, 1, i:i + 1], ROUND, ALU.mult, ALU.add))
                            chain(V.tensor_scalar(raw[:, :], raw[:, :], ROUND, 1.0, ALU.subtract, ALU.min))
                            chain(V.tensor_scalar(w_bit[i][:, :], raw[:, :], -1.0, None, ALU.max))
                        assert step[0] == WSUM_STEPS

                def v_step(s, ph=ph):
                    if ph.kind == "self":
                        dve.wait_ge(sem["v_ps"], ph.at("v_ps", s))
                        if s.plus(-2).there():
                            dve.wait_ge(sem["pv_ps"], ph.at("pv_ps", s.plus(-2)))
                        v = v_self[:, s.b, 0:SELF_H * (SELF_D + 1)].rearrange("p (h d) -> p h d", h=SELF_H)
                        V.tensor_tensor(v[:, :, 0:SELF_D], front[:, 0:D].rearrange("p (h d) -> p h d", h=SELF_H),
                                        w["self_bqkv"][:, 2 * D:3 * D].rearrange("p (h d) -> p h d", h=SELF_H),
                                        ALU.add).then_inc(sem["v_sb"], 1)

                def qk_step(s, ph=ph):
                    dve.wait_ge(sem["qk_ps"], ph.at("qk_ps", s))
                    if ph.kind == "self":
                        if s.plus(-2).there():
                            dve.wait_ge(sem["qkT_ps"], ph.at("qkT_ps", s.plus(-2)))
                        V.tensor_tensor(qk[:, s.b, :, :].rearrange("p c d -> p (c d)"), front[:, :],
                                        w["self_bqkv"][:, 0:2 * D], ALU.add).then_inc(sem["qk_sb"], 1)
                        return
                    if s.plus(-2).there():
                        dve.wait_ge(sem["qk_sb"], ph.at("qk_sb", s.plus(-2)))
                    V.tensor_tensor(rot_a[:, s.b, :, :].rearrange("p c (x j) -> p (c x) j", j=4),
                                    front[:, :].rearrange("p (cx j) -> p cx j", j=4),
                                    bc(cos_x[:, bass.ds(s.n, 1), :].rearrange("p a j -> p (a j)"), 1, 128), ALU.mult).then_inc(sem["qk_read"], 1)
                    fr = front[:, :].rearrange("p (c e h j) -> p c e h j", c=4, e=2, h=16)
                    rb = rot_b[:, s.b, :, :].rearrange("p c (e h j) -> p c e h j", e=2, h=16)
                    for e in range(2):
                        sines = sin_x[:, bass.ds(s.n, 1), e, :].rearrange("p a j -> p (a j)")
                        V.tensor_tensor(rb[:, :, e, :, :], fr[:, :, 1 - e, :, :], bc(bc(sines, 1, 16), 1, 4),
                                        ALU.mult).then_inc(sem["qk_read"], 1)

                def down(s, ph=ph):
                    if s.plus(-2).there():
                        dve.wait_ge(sem["cT_ps"], ph.at("cT_ps", s.plus(-2)))
                        dve.wait_ge(sem["c_sb"], ph.at("c_sb", s.plus(-2)))
                    dve.wait_ge(sem["down_ps"], ph.at("down_ps", s))
                    dve.wait_ge(sem["sumsq"], ph.at("sumsq", s))
                    V.tensor_tensor(kr_a[:, s.b, :], back[:, 192:256], lat_cos[:, :], ALU.mult).then_inc(sem["c_read"], 1)
                    V.tensor_tensor(kr_b[:, s.b, 0:32], back[:, 224:256], lat_sin[:, 0:32],
                                    ALU.mult).then_inc(sem["c_read"], 1)
                    V.tensor_tensor(kr_b[:, s.b, 32:64], back[:, 192:224], lat_sin[:, 32:64],
                                    ALU.mult).then_inc(sem["c_read"], 1)

                def norm(s, ph=ph):
                    dve.wait_ge(sem["rms"], ph.at("rms", s))
                    V.scalar_tensor_tensor(out=c_sb[:, s.b, QR:QR + KVR], in0=back[:, QR:QR + KVR],
                                           scalar=rms[:, s.b, 1:2], in1=w["lat_kvn"][:, :], op0=ALU.mult,
                                           op1=ALU.mult).then_inc(sem["c_read"], 1)
                    V.tensor_scalar(c_sb[:, s.b, 0:QR], back[:, 0:QR], rms[:, s.b, 0:1], None,
                                    ALU.mult).then_inc(sem["c_read"], 1)

                def Q(s, g, ph=ph):
                    dve.wait_ge(sem["q_ps"], ph.at("q_ps", s, g))
                    if s.plus(-1).there() or g >= 2:
                        dve.wait_ge(sem["q_sb"], ph.at("q_sb", s, g - 2))
                    fr = front[:, :].rearrange("p (h c) -> p h c", h=HG)
                    V.tensor_tensor(pe_a[:, g % 2, :, :], fr[:, :, 64:128], bc(lat_cos[:, :], 1, HG),
                                    ALU.mult).then_inc(sem["q_read"], 1)
                    V.tensor_tensor(pe_b[:, g % 2, :, 0:32], fr[:, :, 96:128], bc(lat_sin[:, 0:32], 1, HG),
                                    ALU.mult).then_inc(sem["q_read"], 1)
                    V.tensor_tensor(pe_b[:, g % 2, :, 32:64], fr[:, :, 64:96], bc(lat_sin[:, 32:64], 1, HG),
                                    ALU.mult).then_inc(sem["q_read"], 1)

                def S(s, g, ph=ph):
                    dve.wait_ge(sem["s_ps"], ph.at("s_ps", s, g))
                    if s.plus(-1).there() or g >= 2:
                        dve.wait_ge(sem["p_exp"], ph.at("p_exp", s, g - 2))
                    sc = s_bank[g % 2][:, :].rearrange("p (h t) -> p h t", h=HG)
                    V.tensor_reduce(row_max[:, g % 2, :], sc, AX_X, ALU.max).then_inc(sem["row_max"], 1)
                    dve.wait_ge(sem["row_max"], ph.at("row_max", s, g))
                    V.tensor_tensor(shifted[:, g % 2, :, :], sc, bc(row_max[:, g % 2, :], 2, T),
                                    ALU.subtract).then_inc(sem["s_sub"], 1)

                def normalise(s, g, ph=ph):
                    dv = ph.dv
                    source = "pv_ps" if ph.kind == "latent" else "po_ps"
                    dve.wait_ge(sem[source], ph.at(source, s, g))
                    if s.plus(-1).there() or g >= 2:
                        dve.wait_ge(sem["o_norm"], ph.at("o_norm", s, g - 2))
                    if s.plus(-2).there():
                        dve.wait_ge(sem["oT_ps"], ph.at("oT_ps", s.plus(-2)))
                    if ph.kind == "latent":
                        pv = pv_bank[g % 2][:, 0:HG * PVW].rearrange("p (h c) -> p h c", h=HG)
                    else:
                        pv = pv_bank[g % 2][:, T:2 * T].rearrange("p (h c) -> p h c", h=HG)
                    V.reciprocal(rec[:, g % 2, :], pv[:, :, dv]).then_inc(sem["rec"], 1)
                    dve.wait_ge(sem["rec"], ph.at("rec", s, g))
                    V.tensor_tensor(o_sb[:, s.b, HG * g * dv:HG * (g + 1) * dv].rearrange("p (h d) -> p h d", h=HG),
                                    pv[:, :, 0:dv], bc(rec[:, g % 2, :], 2, dv), ALU.mult).then_inc(sem["o_norm"], 1)

                def y_step(s, ph=ph):
                    dve.wait_ge(sem["y_ps"], ph.at("y_ps", s))
                    dve.wait_ge(sem["xb_ready"], ph.at("xb_ready", s))
                    if s.plus(-2).there():
                        dve.wait_ge(sem["xn_ready"], ph.at("xn_ready", s.plus(-2)))
                    if ph.kind == "lora":
                        V.tensor_tensor(z[:, s.b, :], back[:, 0:D], part[:, s.b, 1, :], ALU.add).then_inc(sem["z_ready"], 1)
                    elif ph.kind == "bit":
                        V.scalar_tensor_tensor(out=z[:, s.b, :], in0=back[:, 0:D], scalar=q2[:, s.b, 4:5],
                                               in1=xb[:, s.b, :], op0=ALU.mult, op1=ALU.add).then_inc(sem["z_ready"], 1)
                    else:
                        V.tensor_tensor(z[:, s.b, :], back[:, 0:D], xb[:, s.b, :], ALU.add).then_inc(sem["z_ready"], 1)
                    dve.wait_ge(sem["z_ready"], ph.at("z_ready", s))
                    V.bn_stats(stat6[:, s.b, :], z[:, s.b, :]).then_inc(sem["stats"], 1)
                    dve.wait_ge(sem["stats"], ph.at("stats", s, 0))
                    V.tensor_copy(spare[:, 0:1], stat6[:, s.b, 0:1])
                    V.bn_aggr(mv[:, s.b, :], stat6[:, s.b, :]).then_inc(sem["stats"], 1)

                def ru(s, ph=ph):
                    k = [0]

                    def chain(ins):
                        ins.then_inc(sem["route"], 1)
                        dve.wait_ge(sem["route"], ph.at("route", s, k[0]))
                        k[0] += 1

                    dve.wait_ge(sem["ru_ps"], ph.at("ru_ps", s))
                    if s.plus(-2).there():
                        dve.wait_ge(sem["zT_ps"], ph.at("zT_ps", s.plus(-2)))
                        dve.wait_ge(sem["mix"], ph.at("mix", s.plus(-2)))
                    b = s.b
                    chain(V.tensor_tensor(logit[:, b, :], front[:, ER:ER + E], w["lora_br"][:, :], ALU.add))
                    chain(V.tensor_reduce(r1[:, b, 0:1], logit[:, b, :], AX_X, ALU.max, negate=True))
                    dve.wait_ge(sem["r_exp"], ph.at("r_exp", s))
                    chain(V.reciprocal(r1[:, b, 2:3], r1[:, b, 1:2]))
                    chain(V.tensor_scalar(prob[:, b, :], expd[:, b, :], r1[:, b, 2:3], None, ALU.mult))
                    for c, pr in enumerate((prob, prob2)):
                        chain(V.tensor_reduce(r1[:, b, 3 + 2 * c:4 + 2 * c], pr[:, b, :], AX_X, ALU.max))
                        chain(V.scalar_tensor_tensor(out=key[:, b, c, :], in0=pr[:, b, :], scalar=r1[:, b, 3 + 2 * c:4 + 2 * c],
                                                     in1=descend[:, :], op0=ALU.is_equal, op1=ALU.mult))
                        chain(V.tensor_reduce(r1[:, b, 4 + 2 * c:5 + 2 * c], key[:, b, c, :], AX_X, ALU.max))
                        chain(V.tensor_scalar(onehot[:, b, c, :], key[:, b, c, :], r1[:, b, 4 + 2 * c:5 + 2 * c], 2.0,
                                              ALU.is_equal, ALU.mult))
                        if c == 0:
                            chain(V.scalar_tensor_tensor(out=prob2[:, b, :], in0=onehot[:, b, 0, :], scalar=-2.0,
                                                         in1=prob[:, b, :], op0=ALU.mult, op1=ALU.add))
                        chain(V.tensor_scalar(weighted[:, b, c, :], onehot[:, b, c, :], r1[:, b, 3 + 2 * c:4 + 2 * c],
                                              None, ALU.mult))
                    u1 = front[:, 0:ER].rearrange("p (e r) -> p e r", e=E)
                    chain(V.tensor_tensor(zcat[:, b, 0, 0:ER].rearrange("p (e r) -> p e r", e=E), u1,
                                          bc(onehot[:, b, 0, :], 2, R), ALU.mult))
                    chain(V.tensor_tensor(ztmp[:, b, :].rearrange("p (e r) -> p e r", e=E), u1,
                                          bc(onehot[:, b, 1, :], 2, R), ALU.mult))
                    chain(V.tensor_tensor(zcat[:, b, 1, 0:ER], ztmp[:, b, :], zcat[:, b, 0, 0:ER], ALU.subtract))
                    if s.plus(-2).there():
                        dve.wait_ge(sem["z2T_ps"], ph.at("z2T_ps", s.plus(-2)))
                    chain(V.tensor_tensor(z2cat[:, b, ER:ER + 1], r1[:, b, 3:4], r1[:, b, 5:6], ALU.add))

                def Y1(s, ph=ph):
                    b = s.b
                    dve.wait_ge(sem["yk_ps"], ph.at("yk_ps", s))
                    dve.wait_ge(sem["xb_ready"], ph.at("xb_ready", s))
                    if s.plus(-2).there():
                        dve.wait_ge(sem["z_ready"], ph.at("z_ready", s.plus(-2)))
                    for k in range(2):
                        V.tensor_tensor(u2[:, b, k, :].rearrange("p (e r) -> p e r", e=E),
                                        bank[4 + k][:, D:D + ER].rearrange("p (e r) -> p e r", e=E),
                                        bc(weighted[:, b, k, :], 2, R), ALU.mult).then_inc(sem["mix"], 1)
                    V.scalar_tensor_tensor(out=part[:, b, 0, :], in0=bank[4][:, 0:D], scalar=r1[:, b, 3:4],
                                           in1=xb[:, b, :], op0=ALU.mult, op1=ALU.add).then_inc(sem["mix"], 1)
                    dve.wait_ge(sem["mix"], ph.at("mix", s, 2))
                    V.scalar_tensor_tensor(out=part[:, b, 1, :], in0=bank[5][:, 0:D], scalar=r1[:, b, 5:6],
                                           in1=part[:, b, 0, :], op0=ALU.mult, op1=ALU.add).then_inc(sem["mix"], 1)
                    V.tensor_tensor(z2cat[:, b, 0:ER], u2[:, b, 0, :], u2[:, b, 1, :], ALU.add).then_inc(sem["mix"], 1)

                def scales(s, cols, src, width, sname, gi, ph=ph):
                    b = s.b
                    k = [0]

                    def chain(ins):
                        ins.then_inc(sem[sname], 1)
                        dve.wait_ge(sem[sname], ph.at(sname, s, k[0]))
                        k[0] += 1

                    chain(V.tensor_reduce(cols[:, b, 0:1], src, AX_X, ALU.max, apply_absolute_value=True))
                    chain(V.tensor_scalar(cols[:, b, 1:2], cols[:, b, 0:1], 1e-5, None, ALU.max))
                    chain(V.reciprocal(cols[:, b, 2:3], cols[:, b, 1:2]))
                    chain(V.tensor_scalar(cols[:, b, 3:4], cols[:, b, 2:3], 127.0, None, ALU.mult))
                    for i, g in enumerate(gi):
                        chain(V.tensor_tensor(cols[:, b, 4 + i:5 + i], cols[:, b, 1:2], gamma[:, 2, g:g + 1], ALU.mult))
                    return chain

                def quant(s, ph=ph):
                    dve.wait_ge(x_loaded[s.b], ph.dma("x_loaded", s))
                    if s.plus(-2).there():
                        dve.wait_ge(sem["val"], ph.at("val", s.plus(-2)))
                        dve.wait_ge(sem["xqT_ps"], ph.at("xqT_ps", s.plus(-2)))
                    chain = scales(s, q1, xs[:, s.b, :], D, "quant", (0, 1))
                    chain(V.tensor_scalar(xq_f[:, s.b, :], xs[:, s.b, :], q1[:, s.b, 3:4], ROUND, ALU.mult, ALU.add))
                    chain(V.tensor_scalar(xq[:, s.b, :], xq_f[:, s.b, :], ROUND, 127.0, ALU.subtract, ALU.min))

                def act_step(s, ph=ph):
                    b = s.b
                    for q in range(2):
                        cols = slice(q * 512, (q + 1) * 512)
                        dve.wait_ge(sem["gv_ps"], ph.at("gv_ps", s, q))
                        if s.plus(-2).there():
                            dve.wait_ge(sem["hq_ready"], ph.at("hq_ready", s.plus(-2)))
                        V.scalar_tensor_tensor(out=g_pre[b][:, cols], in0=bank[q][:, :], scalar=q1[:, b, 4:5],
                                               in1=w["bit_bg"][:, cols], op0=ALU.mult, op1=ALU.add).then_inc(sem["gpre"], 1)
                    for q in range(2):
                        cols = slice(q * 512, (q + 1) * 512)
                        dve.wait_ge(sem["gv_ps"], ph.at("gv_ps", s, 2 + q))
                        if s.plus(-2).there():
                            dve.wait_ge(sem["h_ready"], ph.at("h_ready", s.plus(-2)))
                        V.scalar_tensor_tensor(out=val[b][:, cols], in0=bank[2 + q][:, :], scalar=q1[:, b, 5:6],
                                               in1=w["bit_bv"][:, cols], op0=ALU.mult, op1=ALU.add).then_inc(sem["val"], 1)
                    dve.wait_ge(sem["silu"], ph.at("silu", s))
                    dve.wait_ge(sem["val"], ph.at("val", s))
                    if s.plus(-2).there():
                        dve.wait_ge(sem["h_round"], ph.at("h_round", s.plus(-2)))
                        dve.wait_ge(sem["z_ready"], ph.at("z_ready", s.plus(-2)))
                    V.tensor_tensor(hid[b][:, :], g_act[b][:, :], val[b][:, :], ALU.mult).then_inc(sem["h_ready"], 1)
                    dve.wait_ge(sem["h_ready"], ph.at("h_ready", s))
                    scales(s, q2, hid[b][:, :], F, "hquant", (2,))

                nothing = lambda *a: None
                walk(dve, ph, {
                    "begin": begin, "xT": nothing, "v": v_step, "qk": qk_step, "qkT": nothing, "down": down,
                    "norm": norm, "cT": nothing, "vl": nothing, "Q": Q, "K": nothing, "S": S, "PT": nothing,
                    "PV": normalise if ph.kind == "latent" else nothing, "PO": normalise, "oT": nothing, "y": y_step,
                    "ru": ru, "zT": nothing, "H": nothing, "H1": nothing, "D": nothing, "D1": nothing,
                    "Y": nothing, "Y1": Y1, "z2T": nothing, "quant": quant, "xqT": nothing,
                    "GV": nothing, "act": act_step, "hT": nothing})

        @block.gpsimd
        def _(pool):
            P = nc.gpsimd
            P.memset(v_self[:, :, :], 1.0).then_inc(filled, 1)
            P.memset(v_cross[:, :, :], 1.0).then_inc(filled, 1)
            P.memset(v_lat[:, :, :], 1.0).then_inc(filled, 1)
            P.memset(minus_half[:, :], -0.5).then_inc(filled, 1)
            P.memset(ones[:, :], 1.0).then_inc(filled, 1)
            P.memset(ln_eps[:, :], LN_EPS).then_inc(filled, 1)
            P.memset(rms_eps[:, :], RMS_EPS).then_inc(filled, 1)
            P.memset(inv_rank[:, 0:1], 1.0 / QR).then_inc(filled, 1)
            P.memset(inv_rank[:, 1:2], 1.0 / KVR).then_inc(filled, 1)
            P.memset(round_bias[:, :], ROUND).then_inc(filled, 1)
            P.memset(zcat[:, :, :, ER:LA], 0.0).then_inc(filled, 1)
            P.memset(z2cat[:, :, ER:LA], 0.0).then_inc(filled, 1)
            pool.wait_ge(filled, FILLS - 1)
            P.memset(zcat[:, :, 0, ER:ER + 1], 1.0).then_inc(filled, 1)
            pool.wait_ge(filled, FILLS)

            for ph in phases:
                bias = {0: "self_bo", 1: "cross0_bo", 4: "cross1_bo", 5: "bit_bo"}.get(ph.index)

                def begin(ph=ph):
                    all_done(pool, ph)
                    pool.wait_ge(weights_in[ph.index], 16 * len(weight_dmas[ph.index]))
                    pool.wait_ge(consts_in, 16 * N_CONST)
                    pool.wait_ge(filled, FILLS)

                def residual(s, ph=ph, bias=bias):
                    pool.wait_ge(x_loaded[s.b], ph.dma("x_loaded", s))
                    if s.plus(-2).there():
                        name = "mix" if ph.kind == "lora" else "z_ready"
                        pool.wait_ge(sem[name], ph.at(name, s.plus(-2)))
                    if bias:
                        ins = P.tensor_tensor(xb[:, s.b, :], xs[:, s.b, :], w[bias][:, :], ALU.add)
                    else:
                        ins = P.tensor_tensor(xb[:, s.b, :], xs[:, s.b, :], ones[:, 0:1].to_broadcast([T, D]), ALU.mult)
                    ins.then_inc(sem["xb_ready"], 1)

                def qk_step(s, ph=ph):
                    if ph.kind == "cross":
                        pool.wait_ge(sem["qk_read"], ph.at("qk_read", s))
                        if s.plus(-2).there():
                            pool.wait_ge(sem["qkT_ps"], ph.at("qkT_ps", s.plus(-2)))
                        P.tensor_tensor(qk[:, s.b, :, :], rot_a[:, s.b, :, :], rot_b[:, s.b, :, :],
                                        ALU.add).then_inc(sem["qk_sb"], 1)

                def qkT_step(s, ph=ph):
                    mask = self_mask if ph.kind == "self" else cross_mask
                    half = ph.groups // 2
                    for g in range(ph.groups):
                        if g == 0:
                            pool.wait_ge(sem["qkT_sb"], ph.at("qkT_sb", s))
                        if s.plus(-2).there():
                            pool.wait_ge(sem["s_ps"], ph.at("s_ps", s.plus(-2), g))
                        m = (g % half) * HG
                        P.tensor_tensor(kdiag[:, s.b, HG * g:HG * (g + 1), :], bc(qkT[:, s.b, 2 + g // half, :], 1, HG),
                                        bc(mask[:, m:m + HG], 2, T), ALU.mult).then_inc(sem["k_diag"], 1)

                def down(s, ph=ph):
                    pool.wait_ge(sem["sumsq"], ph.at("sumsq", s))
                    if s.plus(-2).there():
                        pool.wait_ge(sem["c_read"], ph.at("c_read", s.plus(-2)))
                    P.tensor_tensor(rms[:, s.b, :], ssq[:, s.b, :], inv_rank[:, :], ALU.mult).then_inc(sem["rms"], 1)
                    pool.wait_ge(sem["rms"], ph.at("rms", s, 0))
                    P.tensor_tensor(rms[:, s.b, :], rms[:, s.b, :], rms_eps[:, :], ALU.add).then_inc(sem["rms"], 1)
                    pool.wait_ge(sem["rms"], ph.at("rms", s, 1))
                    P.tensor_tensor(rms[:, s.b, :], rms[:, s.b, :], minus_half[:, :], ALU.pow).then_inc(sem["rms"], 1)

                def norm(s, ph=ph):
                    pool.wait_ge(sem["c_read"], ph.at("c_read", s, 2))
                    if s.plus(-2).there():
                        pool.wait_ge(sem["cT_ps"], ph.at("cT_ps", s.plus(-2)))
                    P.tensor_tensor(c_sb[:, s.b, QR + KVR:QR + 2 * KVR], kr_a[:, s.b, :], kr_b[:, s.b, :],
                                    ALU.add).then_inc(sem["c_sb"], 1)

                def vl(s, ph=ph):
                    pool.wait_ge(sem["c_read"], ph.at("c_read", s))
                    if s.plus(-2).there():
                        pool.wait_ge(sem["pv_ps"], ph.at("pv_ps", s.plus(-2)))
                    P.tensor_tensor(v_lat[:, s.b, 0:KVR], c_sb[:, s.b, QR:QR + KVR],
                                    ones[:, 0:1].to_broadcast([T, KVR]), ALU.mult).then_inc(sem["c_sb"], 1)

                def Q(s, g, ph=ph):
                    pool.wait_ge(sem["q_read"], ph.at("q_read", s, 3 * g + 2))
                    if s.plus(-1).there() or g >= 2:
                        pool.wait_ge(sem["qT_ps"], ph.at("qT_ps", s, g - 2))
                    P.tensor_tensor(q_sb[:, g % 2, :, 64:128], pe_a[:, g % 2, :, :], pe_b[:, g % 2, :, :],
                                    ALU.add).then_inc(sem["q_sb"], 1)
                    if g == 3:
                        residual(s)

                def y_step(s, ph=ph):
                    b = s.b
                    pool.wait_ge(sem["stats"], ph.at("stats", s))
                    P.tensor_tensor(rs[:, b, 0:1], mv[:, b, 1:2], ln_eps[:, :], ALU.add).then_inc(sem["rstd"], 1)
                    pool.wait_ge(sem["rstd"], ph.at("rstd", s, 0))
                    P.tensor_tensor(rs[:, b, 1:2], rs[:, b, 0:1], minus_half[:, 0:1], ALU.pow).then_inc(sem["rstd"], 1)
                    P.tensor_tensor(zc[:, b, :], z[:, b, :], mv[:, b, 0:1].to_broadcast([T, D]),
                                    ALU.subtract).then_inc(sem["rstd"], 1)
                    pool.wait_ge(sem["rstd"], ph.at("rstd", s))
                    if ph.index or s.plus(-2).there():
                        pool.wait_ge(x_stored[b], ph.dma("x_stored", s.plus(-2)))
                    P.tensor_tensor(xn[:, b, :], zc[:, b, :], rs[:, b, 1:2].to_broadcast([T, D]),
                                    ALU.mult).then_inc(sem["xn_ready"], 1)

                def act_step(s, ph=ph):
                    pool.wait_ge(sem["h_round"], ph.at("h_round", s))
                    if s.plus(-2).there():
                        pool.wait_ge(sem["hT_ps"], ph.at("hT_ps", s.plus(-2)))
                    P.tensor_tensor(hq[:, s.b, :], g_pre[s.b][:, :], round_bias[:, 0:1].to_broadcast([T, F]),
                                    ALU.subtract).then_inc(sem["hq_ready"], 1)

                nothing = lambda *a: None
                walk(pool, ph, {
                    "begin": begin, "xT": residual if ph.kind == "lora" else nothing, "v": residual,
                    "qk": qk_step, "qkT": qkT_step, "down": down, "norm": norm, "cT": nothing, "vl": vl, "Q": Q, "K": nothing, "S": nothing, "PT": nothing, "PV": nothing, "PO": nothing, "oT": nothing,
                    "y": y_step, "ru": nothing, "zT": nothing, "H": nothing, "H1": nothing, "D": nothing,
                    "D1": nothing, "Y": nothing, "Y1": nothing, "z2T": nothing, "quant": nothing,
                    "xqT": nothing, "GV": residual, "act": act_step, "hT": nothing})


WSUM_STEPS = 1 + 3 + 9
PI_BELOW = float(np.nextafter(np.float32(np.pi), np.float32(0)))


def _two_pi_parts():
    parts, rest = [], 2 * np.pi
    for bits in (9, 9):
        e = int(np.floor(np.log2(rest)))
        p = np.floor(rest / 2.0 ** (e - bits + 1)) * 2.0 ** (e - bits + 1)
        parts.append(float(p))
        rest -= p
    return parts + [float(np.float32(rest))]


TWO_PI = _two_pi_parts()

CONSTS = ["ident", "identb", "causal", "self_mask", "cross_mask", "lat_cos", "lat_sin", "descend", "pos"]

WEIGHT_TILES = [
    ("self_qkv", [128, DC, 3 * D], F32), ("self_bqkv", [128, 3 * D], F32),
    ("self_o", [128, DC, D], F32), ("self_bo", [128, D], F32),
    ("cross0_q", [128, DC, D], F32), ("cross0_kv", [128, 2 * D], F32),
    ("cross0_o", [128, DC, D], F32), ("cross0_bo", [128, D], F32),
    ("lora_ru", [128, DC, LA], F32), ("lora_br", [128, E], F32), ("lora_w1", [128, DC, F], F32),
    ("lora_b1", [LA, F], F32), ("lora_w2", [128, FC, D + ER], F32), ("lora_b2", [LA, D], F32),
    ("lat_down", [128, DC, 256], F32), ("lat_qn", [QR, 1], F32), ("lat_kvn", [128, KVR], F32),
    ("cross1_q", [128, DC, D], F32), ("cross1_kv", [128, 2 * D], F32),
    ("cross1_o", [128, DC, D], F32), ("cross1_bo", [128, D], F32),
    ("bit_gate", [128, DC * F], F32), ("bit_val", [128, DC * F], F32), ("bit_out", [128, FC * D], F32),
    ("bit_bg", [128, F], F32), ("bit_bv", [128, F], F32), ("bit_bo", [128, D], F32),
]
BIT_SHARED = ("bit_gate", "bit_val", "bit_out", "bit_bg", "bit_bv")
_PHASE_OF = {"self": 0, "cross0": 1, "lora": 2, "lat": 3, "cross1": 4, "bit": 5}
WEIGHT_PHASE = [(n, _PHASE_OF[n.split("_")[0]]) for n, _, _ in WEIGHT_TILES]



def chunked(a):
    return a.reshape(a.shape[0] // 128, 128, a.shape[1]).transpose(1, 0, 2)


def rows128(v):
    return np.broadcast_to(v[None, :], (128, v.shape[0]))


def cross_columns():
    cols = []
    for c in range(2):
        for e in range(2):
            for h in range(16):
                for j in range(4):
                    cols.append((16 * c + h) * CROSS_D + 2 * j + e)
    return np.array(cols)


def lay_out(i):
    bf = mybir.dt.np(BF16)
    r = {}
    r["x"] = i["x"].transpose(1, 0, 2)
    r["ctxT"] = i["ctx_1024"].transpose(2, 0, 1)
    r["pos"] = i["fside_BxSx2_0"].transpose(1, 0, 2)
    r["ident"] = np.eye(128, dtype=np.float32)
    r["identb"] = np.eye(128, dtype=bf)
    allowed = np.tril(np.ones((T, T), bool))
    r["causal"] = np.broadcast_to(np.where(allowed, 0.0, -1e30).astype(bf)[:, None, :], (T, HG, T))
    rows = np.arange(128)
    r["self_mask"] = (rows[:, None] // SELF_D == np.arange(8)[None, :]).astype(np.float32)
    r["cross_mask"] = ((rows[:, None] % 64) // 4 == np.arange(16)[None, :]).astype(np.float32)
    freq = (1.0 / 10000.0 ** (np.arange(0, KVR, 2, dtype=np.float32) / np.float32(KVR))).astype(np.float32)
    angle = np.outer(np.arange(T, dtype=np.float32), freq).astype(np.float32)
    r["lat_cos"] = np.concatenate([np.cos(angle), np.cos(angle)], 1).astype(np.float32)
    r["lat_sin"] = np.concatenate([-np.sin(angle), np.sin(angle)], 1).astype(np.float32)
    r["descend"] = rows128(np.arange(E, 0, -1).astype(np.float32))
    r["self_qkv"] = chunked(np.concatenate([i["L0_attn_Wq"].T, i["L0_attn_Wk"].T, i["L0_attn_Wv"].T], 1))
    r["self_bqkv"] = rows128(np.concatenate([i["L0_attn_bq"], i["L0_attn_bk"], i["L0_attn_bv"]]))
    r["self_o"] = chunked(i["L0_attn_Wo"].T)
    r["self_bo"] = rows128(i["L0_attn_bo"])
    cols = cross_columns()
    for l in range(2):
        r[f"cross{l}_q"] = chunked(i[f"L{l}_xattn_Wq"][:, cols])
        kv = i[f"L{l}_xattn_Wkv"]
        r[f"cross{l}_kv"] = np.concatenate([kv[:, :D][:, cols], kv[:, D:]], 1)
        r[f"cross{l}_o"] = chunked(i[f"L{l}_xattn_Wout"])
        r[f"cross{l}_bo"] = rows128(i[f"L{l}_xattn_bout"])
    ru = np.zeros((D, LA), np.float32)
    ru[:, :ER] = i["L0_ffn_A1"].reshape(ER, D).T
    ru[:, ER:ER + E] = i["L0_ffn_W_r"].T
    r["lora_ru"] = chunked(ru)
    r["lora_br"] = rows128(i["L0_ffn_b_r"])
    r["lora_w1"] = chunked(i["L0_ffn_W1"].T)
    b1 = np.zeros((LA, F), np.float32)
    b1[:ER] = i["L0_ffn_B1"].transpose(0, 2, 1).reshape(ER, F)
    b1[ER] = i["L0_ffn_b1"]
    r["lora_b1"] = b1
    r["lora_w2"] = chunked(np.concatenate([i["L0_ffn_W2"].T, i["L0_ffn_A2"].reshape(ER, F).T], 1))
    b2 = np.zeros((LA, D), np.float32)
    b2[:ER] = i["L0_ffn_B2"].transpose(0, 2, 1).reshape(ER, D)
    b2[ER] = i["L0_ffn_b2"]
    r["lora_b2"] = b2
    halves = np.concatenate([np.arange(0, KVR, 2), np.arange(1, KVR, 2)])
    r["lat_down"] = chunked(np.concatenate([i["L1_attn_wq_down"].T, i["L1_attn_wkv_down"].T,
                                            i["L1_attn_wk_rope"].T[:, halves]], 1))
    r["lat_qn"] = i["L1_attn_q_norm_w"][:, None]
    r["lat_kvn"] = rows128(i["L1_attn_kv_norm_w"])
    r["lat_rope"] = i["L1_attn_wq_rope"].reshape(LAT_H, KVR, QR)[:, halves, :].transpose(2, 0, 1)
    r["lat_q"] = i["L1_attn_wq_up"].reshape(LAT_H, NOPE, QR).transpose(1, 0, 2)
    r["lat_kv"] = i["L1_attn_wkv_up"].reshape(LAT_H, 2, NOPE, KVR).transpose(2, 0, 1, 3)
    r["lat_o"] = i["L1_attn_wo"].T.reshape(LAT_H, VD, D).transpose(1, 0, 2)
    for name in ("gate", "val"):
        r[f"bit_{name}"] = chunked(i[f"L1_ffn_{name}_w"].T).reshape(128, DC * F)
    r["bit_out"] = chunked(i["L1_ffn_out_w"].T).reshape(128, FC * D)
    r["bit_bg"] = rows128(i["L1_ffn_gate_b"])
    r["bit_bv"] = rows128(i["L1_ffn_val_b"])
    r["bit_bo"] = rows128(i["L1_ffn_out_b"])
    return {k: np.ascontiguousarray(v) for k, v in r.items()}


def kernel(**inputs):
    import concourse.bacc as bacc
    from concourse.bass_utils import run_bass_kernel_spmd

    laid = lay_out({k: np.asarray(v) for k, v in inputs.items()})
    nc = bacc.Bacc("TRN2", target_bir_lowering=False, num_devices=1)
    ins, arrays = {}, {}
    for name, a in laid.items():
        arrays["in_" + name] = a
        ins[name] = nc.dram_tensor("in_" + name, a.shape, mybir.dt.from_np(a.dtype), kind="ExternalInput").ap()
    out = nc.dram_tensor("out_x", (T, NB, D), F32, kind="ExternalOutput").ap()
    build_decoder(nc, ins, out, SUBLAYERS)
    result = run_bass_kernel_spmd(nc, [arrays], core_ids=[0])
    return np.ascontiguousarray(result.results[0]["out_x"].transpose(1, 0, 2))


SUBLAYERS = 6
```

```python
from contextlib import ExitStack

import numpy as np

import concourse.bass as bass
from concourse import mybir

F32 = mybir.dt.float32
BF16 = mybir.dt.bfloat16
ALU = mybir.AluOpType
ACT = mybir.ActivationFunctionType
AX_X = mybir.AxisListType.X

NB = 16
T = 128
D = 256
DC = D // 128
CTX = 128
F = 1024
FC = F // 128
E = 8
R = 8
ER = E * R
LA = 96
HG = 4
GW = HG * T
PVW = 96
OVW = 32
SELF_H, SELF_D = 16, 16
CROSS_H, CROSS_D = 32, 8
LAT_H, KVR = 16, 64
QR = 128
NOPE = 128
VD = 128
LN_EPS = 1e-5
RMS_EPS = 1e-6
ROUND = 1.5 * 2.0 ** 23


class Seq:

    def __init__(self, pair, b):
        self.pair, self.b = pair, b
        self.n = pair * 2 + b

    def plus(self, k):
        return Seq(self.pair + (self.b + k) // 2, (self.b + k) % 2)

    def there(self):
        return not isinstance(self.n, int) or self.n >= 0


class Phase:

    def __init__(self, kind, index, totals, heads=0, dv=0, scale=1.0, causal=False):
        self.kind, self.index, self.heads, self.dv = kind, index, heads, dv
        self.scale, self.causal = scale, causal
        self.groups = heads // HG
        self.layer = index // 3
        self.base, self.per, self.totals = {}, {}, totals

    def signals(self, **per_sequence):
        for name, per in per_sequence.items():
            self.per[name] = per
            self.base[name] = self.totals.get(name, 0)
            self.totals[name] = self.base[name] + NB * per

    def at(self, name, s, k=None):
        per = self.per[name]
        k = per if k is None else k + 1
        return s.pair * (2 * per) + (self.base[name] + per * s.b + k)

    def dma(self, name, s):
        return s.pair * 16 + (self.base[name] // 2 * 16 + 16)


def finish(previous, part):
    if previous:
        ph, steps = previous
        s = Seq(NB // 2 - 1, 1)
        if ph.kind == "lora":
            if part == 0:
                steps["A"](s)
                steps["Y"](s)
        elif part == 0:
            if ph.kind != "latent":
                steps["PO"](s, ph.groups - 1)
        elif part == 1:
            for r in range(ph.per["oT_ps"]):
                steps["oT"](s, r)
        if part == 2:
            steps["y"](s)


def start(ph, steps, previous, names):
    steps["begin"]()
    for k in range(max(3, len(names))):
        if k < 3:
            finish(previous, k)
        if k < len(names):
            steps[names[k]](Seq(0, 0))


def walk_attention(eng, ph, steps, previous):
    G = ph.groups
    between = {
        "self": {(0, 0): ["qkT+1"], (0, 1): ["oT0-1"], (1, 0): ["y-1"], (1, 1): ["v+1"], (2, 1): ["xT+2"],
                 (3, 0): ["qk+2"]},
        "cross": {(0, 0): ["xT+1"], (0, 2): ["oT0-1"], (1, 1): ["y-1"], (1, 2): ["qk+1"], (3, 2): ["qkT+1"],
                  (4, 2): ["v+1"]},
        "latent": {(0, 0): ["Q0+1", "oT0-1"], (0, 2): ["K0+1", "oT1-1"], (1, 0): ["Q1+1"], (1, 1): ["y-1"],
                   (1, 2): ["K1+1", "xT+2"], (2, 0): ["Q2+1"], (2, 1): ["down+2"], (2, 2): ["norm+2", "K2+1"],
                   (3, 0): ["Q3+1"], (3, 2): ["K3+1", "cT+2", "vl+2"]},
    }[ph.kind]

    def extra(s, place, back, ahead):
        for what in between.get(place, []):
            name, shift = what[:-2], int(what[-2:])
            if shift < 0 and not back or shift > ahead:
                continue
            if name[-1].isdigit():
                steps[name[:-1]](s.plus(shift), int(name[-1]))
            else:
                steps[name](s.plus(shift))

    def body(s, back=True, ahead=2):
        for g in range(G):
            steps["PT"](s, g)
            extra(s, (g, 0), back, ahead)
            if ph.kind != "latent" and (g or back):
                steps["PO"](s if g else s.plus(-1), (g - 1) % G)
            if g + 2 < G:
                steps["S"](s, g + 2)
            elif ahead:
                steps["S"](s.plus(1), g + 2 - G)
            extra(s, (g, 1), back, ahead)
            if g == 0 and not back and ph.kind != "latent":
                steps["ready"]()
            steps["PV"](s, g)
            extra(s, (g, 2), back, ahead)

    first = Seq(0, 0)
    second = first.plus(1)
    if ph.kind == "latent":
        for part in range(3):
            finish(previous, part)
        steps["begin"]()
        steps["ready"]()
        for name in ("xT", "down", "norm", "cT", "vl"):
            steps[name](first)
        steps["Q"](first, 0)
        steps["xT"](second)
        steps["K"](first, 0)
        steps["Q"](first, 1)
        steps["down"](second)
        steps["S"](first, 0)
        steps["K"](first, 1)
        steps["norm"](second)
        steps["S"](first, 1)
        steps["Q"](first, 2)
        steps["cT"](second)
        steps["vl"](second)
        steps["K"](first, 2)
        steps["Q"](first, 3)
        steps["K"](first, 3)
    else:
        start(ph, steps, previous, ("xT", "qk", "qkT", "v"))
        steps["S"](first, 0)
        steps["S"](first, 1)
        if ph.kind == "self":
            steps["xT"](second)
            steps["qk"](second)
    body(first, back=False)
    body(first.plus(1))
    with eng.Fori(1, NB // 2 - 1) as pair:
        body(Seq(pair, 0))
        body(Seq(pair, 1))
    body(first.plus(NB - 2), ahead=1)
    body(first.plus(NB - 1), ahead=0)


def walk_ffn(eng, ph, steps, previous, names, order, turn, end):
    def body(s):
        for name, shift in order:
            t = s.plus(shift)
            if isinstance(t.n, int) and not 0 <= t.n < NB:
                continue
            steps[name](t)

    start(ph, steps, previous, names)
    steps["pool_ready"]()
    for n in range(turn, 2):
        body(Seq(0, 0).plus(n))
        if n == turn:
            steps["ready"]()
    with eng.Fori(1, NB // 2 - 1) as pair:
        body(Seq(pair, 0))
        body(Seq(pair, 1))
    for n in range(NB - 2, end):
        body(Seq(0, 0).plus(n))


LORA_ORDER = [("A", -1), ("xT", 1), ("H", 0), ("ru", 1), ("H1", 0), ("D", 0), ("D1", 0), ("Y", -1), ("y", -1),
              ("zT", 1)]
BIT_ORDER = [("quant", 2), ("y", -1), ("residual", 1), ("xqT", 2), ("act", 1), ("GV", 2), ("hT", 0), ("round", 1)]


def walk(eng, ph, steps, previous):
    if ph.kind == "lora":
        walk_ffn(eng, ph, steps, previous, ("xT", "ru", "zT"), LORA_ORDER, 0, NB)
    elif ph.kind == "bit":
        walk_ffn(eng, ph, steps, previous, ("quant", "xqT", "GV"), BIT_ORDER, -1, NB + 1)
    else:
        walk_attention(eng, ph, steps, previous)


def bc(ap, axis, n):
    a = ap.unsqueeze(axis)
    shape = list(a.shape)
    shape[axis] = n
    return a.to_broadcast(shape)


def build_decoder(nc, ins, out, sublayers=6):
    totals = {}
    phases = [
        Phase("self", 0, totals, SELF_H, SELF_D, 1.0 / np.sqrt(SELF_D), True),
        Phase("cross", 1, totals, CROSS_H, CROSS_D, 1.0 / np.sqrt(CROSS_D)),
        Phase("lora", 2, totals),
        Phase("latent", 3, totals, LAT_H, KVR, 1.0 / np.sqrt(NOPE + KVR), True),
        Phase("cross", 4, totals, CROSS_H, CROSS_D, 1.0 / np.sqrt(CROSS_D)),
        Phase("bit", 5, totals),
    ][:sublayers]
    for ph in phases:
        G = ph.groups
        ph.signals(x_loaded=1, x_stored=1, xb_ready=1, y_ps=1, z_ready=1, stats=2, rstd=3, xn_ready=1)
        if ph.kind in ("self", "cross", "latent"):
            ph.signals(xT_ps=1, xT_sb=1, s_ps=G, row_max=G, s_sub=G, p_exp=G, pT_ps=2 * G, pT_sb=2 * G, pv_ps=G,
                       rec=G, o_norm=G, oT_ps=ph.heads * ph.dv // 512 or 1,
                       oT_sb=ph.heads * ph.dv // 512 or 1)
        if ph.kind in ("self", "cross"):
            ph.signals(v_ps=1, v_sb=1, ov_sb=G, po_ps=G, qk_ps=1, qk_sb=1, qkT_ps=1, qkT_sb=1, k_diag=G)
        if ph.kind == "cross":
            ph.signals(ctx_loaded=1, qk_read=3)
        if ph.kind == "latent":
            ph.signals(down_ps=1, sumsq=2, rms=3, c_read=5, c_sb=2, cT_ps=1, cT_sb=2, q_ps=G,
                       q_abs=G, q_read=3 * G, q_sb=G, qT_ps=G, qT_sb=G)
        if ph.kind == "lora":
            ph.signals(xT_ps=1, xT_sb=1, ru_ps=1, route=23, r_exp=1, zT_ps=2, zT_sb=2, h_ps=2, h0=2, d_ps=2,
                       h1=2, h_weighted=2, h_mixed=1, a_ps=1, a_weighted=1, z2T_sb=1, part_ready=1)
        if ph.kind == "bit":
            ph.signals(quant=8, xqT_ps=1, xqT_sb=1, gv_ps=4, gpre=2, silu=2, val=2, h_ready=1, hquant=5,
                       h_round=1, hq_ready=1, hT_ps=1, hT_sb=1)

    with ExitStack() as ctx:
        def sb(name, shape, dt=F32):
            return ctx.enter_context(nc.sbuf_tensor(name, shape, dt))

        bank = [ctx.enter_context(nc.psum_tensor(f"bank{i}", [128, 512], F32)) for i in range(8)]
        s_bank, pT_bank, pv_bank = bank[0:2], bank[2:4], bank[4:6]
        front, back = bank[6], bank[7]
        w_sums = pv_bank[0][:, HG * PVW:HG * PVW + 3]

        ident = sb("ident", [128, 128])
        identb = sb("identb", [128, 128], BF16)
        causal = sb("causal", [128, HG, T], BF16)
        self_mask = sb("self_mask", [128, 8])
        cross_mask = sb("cross_mask", [128, 16])
        lat_cos = sb("lat_cos", [T, 2 * 32])
        lat_sin = sb("lat_sin", [T, 2 * 32])
        minus_half = sb("minus_half", [128, 2])
        ln_eps = sb("ln_eps", [128, 1])
        rms_eps = sb("rms_eps", [128, 2])
        inv_rank = sb("inv_rank", [128, 2])
        round_bias = sb("round_bias", [128, 1])

        x_all = sb("x_all", [T, NB, D])
        xs = sb("xs", [T, 2, D])
        xb = sb("xb", [T, 2, D])
        xT = sb("xT", [128, 2, DC, T])
        z = sb("z", [T, 2, D])
        stat6 = sb("stat6", [T, 2, 6])
        mv = sb("mv", [T, 2, 2])
        rs = sb("rs", [T, 2, 2])
        zc = sb("zc", [T, 2, D])
        xn = sb("xn", [T, 2, D])
        spare = sb("spare", [T, 1])

        ctxT = sb("ctxT", [CTX, 2, T])
        qk = sb("qk", [T, 2, 4, 128])
        rot_a = sb("rot_a", [T, 2, 4, 128])
        rot_b = sb("rot_b", [T, 2, 4, 128])
        qkT = sb("qkT", [128, 2, 4, T])
        kdiag = sb("kdiag", [128, 2, CROSS_H, T])
        row_max = sb("row_max", [T, 2, HG])
        shifted = sb("shifted", [T, 2, HG, T])
        probs = sb("probs", [T, 2, HG, T])
        probsT = sb("probsT", [T, 2, HG, T])
        rec = sb("rec", [T, 2, HG])
        o_sb = sb("o_sb", [T, 2, LAT_H * KVR])
        oT = sb("oT", [128, 2, 8, T])
        v_self = sb("v_self", [T, 2, SELF_H * (SELF_D + 1) + OVW])
        v_cross = sb("v_cross", [T, 2, CROSS_H * (CROSS_D + 1) + OVW])
        ov_sb = sb("ov_sb", [128, 2, T])
        v_lat = sb("v_lat", [T, 2, PVW])
        cos_x = sb("cos_x", [T, NB, 4])
        sin_x = sb("sin_x", [T, NB, 2, 4])
        ang = sb("ang", [T, 2, NB, 4])
        turns = sb("turns", [T, 2, NB, 4])

        ssq = sb("ssq", [T, 2, 2])
        rms = sb("rms", [T, 2, 2])
        junk = sb("junk", [T, QR])
        c_sb = sb("c_sb", [T, 2, 256])
        kr_a = sb("kr_a", [T, 2, 64])
        kr_b = sb("kr_b", [T, 2, 64])
        qcT = sb("qcT", [QR, 2, T])
        kT = sb("kT", [128, 2, T])
        q_sb = rot_a
        pe_a = rot_b[:, :, 0:2, :].rearrange("p b c (a d) -> p b (c a) d", a=2)
        pe_b = rot_b[:, :, 2:4, :].rearrange("p b c (a d) -> p b (c a) d", a=2)

        logit = sb("logit", [T, 2, E])
        r1 = sb("r1", [T, 2, 8])
        expd = sb("expd", [T, 2, E])
        prob = sb("prob", [T, 2, E])
        key = sb("key", [T, 2, 2, E])
        prob2 = sb("prob2", [T, 2, E])
        onehot = sb("onehot", [T, 2, 2, E])
        weighted = sb("weighted", [T, 2, 2, E])
        descend = sb("descend", [T, E])
        zcat = sb("zcat", [T, 2, 2, LA])
        ztmp = sb("ztmp", [T, 2, ER])
        zT = sb("zT", [LA, 2, 2, T])
        z2T = sb("z2T", [128, 2, T])
        z2w = sb("z2w", [128, 2, T])
        spread = probsT
        spreadT = probs
        h_mix = [t[:].rearrange("p b c t -> p (b c t)").rearrange("p (f t) -> p f t", f=FC) for t in (qk, qkT)]
        h_tmp = [t[:].rearrange("p b c t -> p (b c t)").rearrange("p (f t) -> p f t", f=FC) for t in (rot_a, rot_b)]
        part = shifted[:].rearrange("p b (k c) t -> p b k (c t)", k=2)

        q1 = sb("q1", [T, 2, 8])
        q2 = sb("q2", [T, 2, 8])
        xq_f = sb("xq_f", [T, 2, D])
        xq = sb("xq", [T, 2, D], BF16)
        xqT = sb("xqT", [128, 2, DC, T], BF16)
        hq = o_sb[:, 0, :].bitcast(BF16).rearrange("p (b f) -> p b f", b=2)
        hqT = oT[:, 0, :, :].rearrange("p c t -> p (c t)").bitcast(BF16).rearrange(
            "p (b c t) -> p b c t", b=2, c=FC)
        w_stat = sb("w_stat", [128, 3])
        ones = sb("ones", [128, 128])
        gamma = sb("gamma", [128, 4, 3])

        w = {}
        for name, shape, dt in WEIGHT_TILES:
            if name not in BIT_SHARED:
                whole = sb("w_" + name, [128] + shape[1:], dt)
                w[name] = whole[0:shape[0]]
                if name == "lora_b1":
                    whole_b1 = whole
        w_cat = sb("w_cat", [QR, LAT_H, 128])
        w_vo = sb("w_vo", [128, LAT_H // 2, D])
        bit_gate_bf16 = whole_b1[:, :].bitcast(BF16)
        w["bit_gate"] = w["lora_w1"].rearrange("p c f -> p (c f)")
        w["bit_val"] = w["lora_w2"].rearrange("p c f -> p (c f)")[:, 0:DC * F]
        w["bit_bg"] = w_vo[:, 0:4, :].rearrange("p h c -> p (h c)")
        w["bit_bv"] = w_vo[:, 4:8, :].rearrange("p h c -> p (h c)")
        w1_bf16 = w["bit_gate"].bitcast(BF16)
        w_bit = [bit_gate_bf16[:, :], w1_bf16[:, 0:DC * F], w1_bf16[:, DC * F:2 * DC * F]]

        kd = [kdiag[:, b].rearrange("p h t -> p (h t)") for b in range(2)]
        w["bit_out"] = kd[0][:, 2048:4096]
        qT = [kd[b][:, 0:LAT_H * T].rearrange("p (h t) -> p h t", h=LAT_H) for b in range(2)]
        h_act = [kd[b][:, 0:2 * F].rearrange("p (k f t) -> p k f t", k=2, f=FC) for b in range(2)]
        g_pre = [kd[b][:, 0:F] for b in range(2)]
        g_act = [kd[b][:, F:2 * F] for b in range(2)]
        val = [kd[b][:, 2 * F:3 * F] for b in range(2)]
        hid = [kd[b][:, 3 * F:4 * F] for b in range(2)]
        lat_q_raw = o_sb[:].rearrange("p b c -> p (b c)").rearrange("p (h r) -> p h r", h=LAT_H)
        lat_kv_raw = kd[0][:, 2048:4096].rearrange("p (h e c) -> p h e c", h=LAT_H, e=2)
        lat_o_raw = [kd[1][:, 2048:4096].rearrange("p (h o) -> p h o", h=LAT_H // 2),
                     oT[:].rearrange("p b c t -> p (b c t)").rearrange("p (h o) -> p h o", h=LAT_H // 2)]

        sem = {}
        for name in list(totals):
            if name not in ("x_loaded", "x_stored", "ctx_loaded"):
                sem[name] = ctx.enter_context(nc.semaphore(name))
        x_loaded = [ctx.enter_context(nc.semaphore(f"x_loaded{b}")) for b in range(2)]
        x_stored = [ctx.enter_context(nc.semaphore(f"x_stored{b}")) for b in range(2)]
        ctx_loaded = [ctx.enter_context(nc.semaphore(f"ctx_loaded{b}")) for b in range(2)]
        consts_in = ctx.enter_context(nc.semaphore("consts_in"))
        weights_in = [ctx.enter_context(nc.semaphore(f"weights_in{i}")) for i in range(6)]
        raw_in = ctx.enter_context(nc.semaphore("raw_in"))
        bit_raw_in = ctx.enter_context(nc.semaphore("bit_raw_in"))
        ident_in = ctx.enter_context(nc.semaphore("ident_in"))
        pos_in = ctx.enter_context(nc.semaphore("pos_in"))
        filled = ctx.enter_context(nc.semaphore("filled"))
        tables = ctx.enter_context(nc.semaphore("tables"))
        angles = ctx.enter_context(nc.semaphore("angles"))
        table_sin = ctx.enter_context(nc.semaphore("table_sin"))
        prep_ps = ctx.enter_context(nc.semaphore("prep_ps"))
        prep_sb = ctx.enter_context(nc.semaphore("prep_sb"))
        wsum = ctx.enter_context(nc.semaphore("wsum"))

        weight_dmas = [[n for n, i in WEIGHT_PHASE if i == p] for p in range(6)]
        N_CONST = len(CONSTS) - 2

        def weight_count(p):
            return 16 * len([n for n in weight_dmas[p] if n not in BIT_RAW])

        FILLS = 12
        last = phases[-1]

        def heads_done(eng, ph):
            if ph.index:
                q = phases[ph.index - 1]
                name = "z_ready" if q.kind == "lora" else "pv_ps"
                eng.wait_ge(sem[name], q.at(name, Seq(NB // 2 - 1, 1)))

        def all_done(eng, ph):
            if ph.index:
                eng.wait_ge(sem["xn_ready"], ph.base["xn_ready"])

        block = ctx.enter_context(nc.Block())

        @block.sync
        def _(sp):
            const_tiles = {"identb": identb, "causal": causal, "self_mask": self_mask,
                           "cross_mask": cross_mask, "lat_cos": lat_cos, "lat_sin": lat_sin,
                           "descend": descend}

            def load_weights(p):
                for name in weight_dmas[p]:
                    if name in BIT_RAW:
                        continue
                    sp.dma_start(w[name][:], ins[name]).then_inc(weights_in[p], 16)

            for ph in phases:
                def load(s, ph=ph):
                    old, q = (s.plus(-2), ph) if s.plus(-2).there() else (Seq(NB // 2 - 1, s.b), phases[ph.index - 1])
                    if ph.index or s.plus(-2).there():
                        sp.wait_ge(sem["xb_ready"], q.at("xb_ready", old))
                        if q.kind == "bit":
                            sp.wait_ge(sem["quant"], q.at("quant", old))
                        else:
                            sp.wait_ge(sem["xT_ps"], q.at("xT_ps", old))
                    if ph.index and not s.plus(-2).there():
                        sp.wait_ge(x_stored[s.b], q.dma("x_stored", s))
                    src = ins["x"][:, s.n, :] if ph.index == 0 else x_all[:, s.n, :]
                    sp.dma_start(xs[:, s.b, :], src).then_inc(x_loaded[s.b], 16)
                    if ph.kind == "cross":
                        if s.plus(-2).there():
                            sp.wait_ge(sem["qk_ps"], ph.at("qk_ps", s.plus(-2)))
                            sp.wait_ge(sem["v_ps"], ph.at("v_ps", s.plus(-2)))
                        sp.dma_start(ctxT[:, s.b, :], ins["ctxT"][:, s.n, :]).then_inc(ctx_loaded[s.b], 16)

                def store(s, ph=ph):
                    sp.wait_ge(sem["xn_ready"], ph.at("xn_ready", s))
                    dst = out[:, s.n, :] if ph is last else x_all[:, s.n, :]
                    sp.dma_start(dst, xn[:, s.b, :]).then_inc(x_stored[s.b], 16)

                first = Seq(0, 0)
                if ph.index == 0:
                    sp.dma_start(ang[:, 0, :, 0:2], ins["pos"]).then_inc(pos_in, 16)
                    load(first)
                    sp.dma_start(ident[:], ins["ident"]).then_inc(ident_in, 16)
                    load_weights(0)
                    for name in const_tiles:
                        sp.dma_start(const_tiles[name][:], ins[name]).then_inc(consts_in, 16)
                    load(first.plus(1))
                else:
                    load(first)
                    load(first.plus(1))
                    last_stores()
                    for b in range(2):
                        sp.wait_ge(x_stored[b], ph.index * (NB // 2) * 16)
                if ph.index == 0:
                    for p in range(1, min(5, len(phases))):
                        load_weights(p)
                if ph.index == 4 and len(phases) > 5:
                    load_weights(5)
                load(first.plus(2))
                for n in range(2):
                    load(first.plus(n + 3))
                    if ph.index == 2 and len(phases) > 3:
                        if n == 0:
                            sp.dma_start(lat_q_raw, ins["lat_q"]).then_inc(raw_in, 16)
                            sp.dma_start(lat_kv_raw, ins["lat_kv"]).then_inc(raw_in, 16)
                            sp.dma_start(w_cat[:, :, 64:128], ins["lat_rope"]).then_inc(raw_in, 16)
                        else:
                            for i in range(2):
                                sp.dma_start(lat_o_raw[i], ins["lat_o"][:, 8 * i:8 * i + 8, :]).then_inc(raw_in, 16)
                    if ph.kind == "latent" and len(phases) > 5 and n == 0:
                        for name in BIT_RAW:
                            if name == "bit_out":
                                sp.wait_ge(prep_sb, 6)
                            sp.dma_start(w[name], ins[name]).then_inc(bit_raw_in, 16)
                    store(first.plus(n))
                with sp.Fori(1, NB // 2 - 2) as pair:
                    for b in range(2):
                        load(Seq(pair, b).plus(3))
                        store(Seq(pair, b))
                load(first.plus(NB - 1))
                for n in range(NB - 4, NB - 2):
                    store(first.plus(n))

                def last_stores(store=store):
                    for n in range(NB - 2, NB):
                        store(Seq(0, 0).plus(n))

            last_stores()
            for b in range(2):
                sp.wait_ge(x_stored[b], len(phases) * (NB // 2) * 16)

        @block.tensor
        def _(pe):
            pe.wait_ge(ident_in, 16)
            previous = None
            for ph in phases:
                def begin(ph=ph):
                    heads_done(pe, ph)
                    pe.wait_ge(weights_in[ph.index], weight_count(ph.index))
                    pe.wait_ge(filled, FILLS)
                    if ph.kind == "latent":
                        pe.wait_ge(raw_in, 80)
                        for h in range(LAT_H):
                            mm = pe.matmul(bank[h // 8][:, (h % 8) * 64:(h % 8) * 64 + 64],
                                           lat_q_raw[:, h, :], lat_kv_raw[:, h, 0, :], start=True, stop=True)
                            if h % 8 == 7:
                                mm.then_inc(prep_ps, 1)
                        for h in range(LAT_H):
                            p0 = 64 * (h % 2)
                            mm = pe.matmul(bank[2 + h // 4][p0:p0 + 64, (h // 2 % 2) * D:(h // 2 % 2) * D + D],
                                           lat_kv_raw[:, h, 1, :], lat_o_raw[h // 8][:, h % 8, :], start=True, stop=True)
                            if h % 4 == 3:
                                mm.then_inc(prep_ps, 1)
                        pe.wait_ge(prep_sb, 6)
                    if ph.kind == "bit":
                        pe.wait_ge(wsum, WSUM_STEPS)

                def xT_step(s, ph=ph):
                    pe.wait_ge(x_loaded[s.b], ph.dma("x_loaded", s))
                    if s.plus(-1).there():
                        if ph.kind in ("self", "cross"):
                            pe.wait_ge(sem["v_sb"], ph.at("v_sb", s.plus(-1)))
                        elif ph.kind == "lora":
                            pe.wait_ge(sem["zT_sb"], ph.at("zT_sb", s.plus(-1)))
                        elif s.plus(-3).there():
                            pe.wait_ge(sem["z_ready"], ph.at("z_ready", s.plus(-3)))
                        else:
                            pe.wait_ge(sem["cT_sb"], ph.at("cT_sb", s.plus(-1)))
                    place = back if ph.kind == "latent" else front
                    for c in range(DC):
                        mm = pe.transpose(place[:, c * T:(c + 1) * T], xs[:, s.b, c * 128:(c + 1) * 128], ident[:, :])
                    mm.then_inc(sem["xT_ps"], 1)

                def v_step(s, ph=ph):
                    pe.wait_ge(sem["qkT_sb"], ph.at("qkT_sb", s))
                    if ph.kind == "self":
                        for c in range(DC):
                            mm = pe.matmul(front[:, 0:D], xT[:, s.b, c, :], w["self_qkv"][:, c, 2 * D:3 * D],
                                           start=(c == 0), stop=(c == DC - 1))
                    else:
                        mm = pe.matmul(front[:, 0:D], ctxT[:, s.b, :], w[f"cross{ph.layer}_kv"][:, D:2 * D],
                                       start=True, stop=True)
                    mm.then_inc(sem["v_ps"], 1)

                def qk_step(s, ph=ph):
                    pe.wait_ge(sem["xT_sb"], ph.at("xT_sb", s))
                    if ph.kind == "self":
                        for c in range(DC):
                            mm = pe.matmul(front[:, :], xT[:, s.b, c, :], w["self_qkv"][:, c, 0:2 * D],
                                           start=(c == 0), stop=(c == DC - 1))
                    else:
                        pe.wait_ge(ctx_loaded[s.b], ph.dma("ctx_loaded", s))
                        for c in range(DC):
                            pe.matmul(front[:, 0:D], xT[:, s.b, c, :], w[f"cross{ph.layer}_q"][:, c, :],
                                      start=(c == 0), stop=(c == DC - 1))
                        mm = pe.matmul(front[:, D:2 * D], ctxT[:, s.b, :], w[f"cross{ph.layer}_kv"][:, 0:D],
                                       start=True, stop=True)
                    mm.then_inc(sem["qk_ps"], 1)

                def qkT_step(s, ph=ph):
                    pe.wait_ge(sem["qk_sb"], ph.at("qk_sb", s))
                    for c in range(4):
                        mm = pe.transpose(front[:, c * T:(c + 1) * T], qk[:, s.b, c, :], ident[:, :])
                    mm.then_inc(sem["qkT_ps"], 1)

                def down(s, ph=ph):
                    pe.wait_ge(sem["xT_sb"], ph.at("xT_sb", s))
                    for c in range(DC):
                        mm = pe.matmul(back[:, 0:256], xT[:, s.b, c, :], w["lat_down"][:, c, :],
                                       start=(c == 0), stop=(c == DC - 1))
                    mm.then_inc(sem["down_ps"], 1)

                def cT(s, ph=ph):
                    pe.wait_ge(sem["c_sb"], ph.at("c_sb", s, 0))
                    pe.wait_ge(sem["c_read"], ph.at("c_read", s))
                    for c in range(2):
                        mm = pe.transpose(back[:, c * T:(c + 1) * T], c_sb[:, s.b, c * 128:(c + 1) * 128], ident[:, :])
                    mm.then_inc(sem["cT_ps"], 1)

                def Q(s, g, ph=ph):
                    if g == 0:
                        pe.wait_ge(sem["cT_sb"], ph.at("cT_sb", s))
                        if s.plus(-1).there():
                            pe.wait_ge(sem["qT_sb"], ph.at("qT_sb", s.plus(-1)))
                    else:
                        pe.wait_ge(sem["qT_sb"], ph.at("qT_sb", s, g - 1))
                    pe.matmul(front[:, :], qcT[:, s.b, :],
                              w_cat[:, HG * g:HG * (g + 1), :].rearrange("p h c -> p (h c)"),
                              start=True, stop=True).then_inc(sem["q_ps"], 1)

                def K(s, g, ph=ph):
                    pe.wait_ge(sem["q_sb"], ph.at("q_sb", s, g))
                    pe.wait_ge(sem["q_abs"], ph.at("q_abs", s, g))
                    for j in range(HG):
                        mm = pe.transpose(front[:, j * T:(j + 1) * T], q_sb[:, g % 2, j, :], ident[:, :])
                    mm.then_inc(sem["qT_ps"], 1)

                def S(s, g, ph=ph):
                    if s.plus(-1).there() or g >= 2:
                        pe.wait_ge(sem["s_sub"], ph.at("s_sub", s, g - 2))
                    if ph.kind == "latent":
                        pe.wait_ge(sem["qT_sb"], ph.at("qT_sb", s, g))
                    else:
                        pe.wait_ge(sem["qkT_sb"], ph.at("qkT_sb", s))
                        pe.wait_ge(sem["k_diag"], ph.at("k_diag", s, g))
                    if ph.index == 0 and g == 0 and not s.plus(-1).there():
                        pe.wait_ge(consts_in, 16 * N_CONST)
                    sbank = s_bank[g % 2]
                    if ph.causal:
                        pe.matmul(sbank[:, :], identb[:, :], causal[:, :, :].rearrange("p h t -> p (h t)"),
                                  start=True, stop=False)
                    if ph.kind == "latent":
                        for j in range(HG):
                            mm = pe.matmul(sbank[:, j * T:(j + 1) * T], qT[s.b][:, HG * g + j, :], kT[:, s.b, :],
                                           start=False, stop=(j == HG - 1))
                    else:
                        chunk = g // (ph.groups // 2)
                        mm = pe.matmul(sbank[:, :], qkT[:, s.b, chunk, :],
                                       kdiag[:, s.b, HG * g:HG * (g + 1), :].rearrange("p h t -> p (h t)"),
                                       start=not ph.causal, stop=True)
                    mm.then_inc(sem["s_ps"], 1)

                def PT(s, g, ph=ph):
                    pe.wait_ge(sem["p_exp"], ph.at("p_exp", s, g))
                    for j in range(HG):
                        if j % 2 == 0 and (s.plus(-1).there() or g):
                            pe.wait_ge(sem["pT_sb"], ph.at("pT_sb", s, 2 * g - 2 + j // 2))
                        mm = pe.transpose(pT_bank[j // 2][:, j % 2 * T:(j % 2 + 1) * T], probs[:, g % 2, j, :],
                                          ident[:, :])
                        if j % 2:
                            mm.then_inc(sem["pT_ps"], 1)

                def PV(s, g, ph=ph):
                    if g == 0:
                        name = "c_sb" if ph.kind == "latent" else "v_sb"
                        pe.wait_ge(sem[name], ph.at(name, s))
                    if s.plus(-1).there() or g >= 2:
                        pe.wait_ge(sem["o_norm"], ph.at("o_norm", s, g - 2))
                    if ph.kind == "latent" and len(phases) > 5 and g == 0 and isinstance(s.n, int) and s.n == NB - 2:
                        pe.wait_ge(wsum, 1)
                        pe.matmul(w_sums, ones[:, :], w_stat[:, :], start=True, stop=True)
                    for j in range(HG):
                        if j % 2 == 0:
                            pe.wait_ge(sem["pT_sb"], ph.at("pT_sb", s, 2 * g + j // 2))
                        h = HG * g + j
                        if ph.kind == "latent":
                            mm = pe.matmul(pv_bank[g % 2][:, j * PVW:(j + 1) * PVW], probsT[:, g % 2, j, :],
                                           v_lat[:, s.b, :], start=True, stop=True)
                        else:
                            v, step = (v_self, SELF_D + 1) if ph.kind == "self" else (v_cross, CROSS_D + 1)
                            mm = pe.matmul(pv_bank[g % 2][OVW * j:OVW * (j + 1), 0:T],
                                           v[:, s.b, h * step:h * step + OVW], probsT[:, g % 2, j, :],
                                           start=True, stop=True)
                    mm.then_inc(sem["pv_ps"], 1)

                def PO(s, g, ph=ph):
                    pe.wait_ge(sem["ov_sb"], ph.at("ov_sb", s, g))
                    pe.transpose(pv_bank[g % 2][:, T:2 * T], ov_sb[:, g % 2, :], ident[:, :]).then_inc(sem["po_ps"], 1)

                def oT_step(s, r, ph=ph):
                    chunks = ph.heads * ph.dv // 128
                    if r == 0:
                        pe.wait_ge(sem["o_norm"], ph.at("o_norm", s))
                        if s.plus(-1).there():
                            pe.wait_ge(sem["z_ready"], ph.at("z_ready", s.plus(-1)))
                        if ph.kind == "latent" and not (isinstance(s.n, int) and s.n + 2 >= NB):
                            pe.wait_ge(sem["cT_sb"], ph.at("cT_sb", s.plus(2)))
                    else:
                        pe.wait_ge(sem["oT_sb"], ph.at("oT_sb", s, r - 1))
                    for c in range(4 * r, min(chunks, 4 * r + 4)):
                        mm = pe.transpose(back[:, c % 4 * T:(c % 4 + 1) * T], o_sb[:, s.b, c * 128:(c + 1) * 128],
                                          ident[:, :])
                        if c % 4 == 3 or c == chunks - 1:
                            mm.then_inc(sem["oT_ps"], 1)

                def y_step(s, ph=ph):
                    if ph.kind == "lora":
                        pe.wait_ge(sem["z2T_sb"], ph.at("z2T_sb", s))
                        mm = pe.matmul(bank[4][:, 0:D], z2T[:, s.b, :], w["lora_b2"][:, :], start=False, stop=True)
                    elif ph.kind == "bit":
                        pe.wait_ge(sem["hT_sb"], ph.at("hT_sb", s))
                        if s.plus(-1).there():
                            pe.wait_ge(sem["z_ready"], ph.at("z_ready", s.plus(-1)))
                        for c in range(FC):
                            mm = pe.matmul(back[:, 0:D], hqT[:, s.b, c, :],
                                           w_bit[2][:, c * D:(c + 1) * D], start=(c == 0), stop=(c == FC - 1))
                    else:
                        chunks = ph.heads * ph.dv // 128
                        wo = {"self": w["self_o"], "cross": w[f"cross{ph.layer}_o"], "latent": w_vo}[ph.kind]
                        pe.wait_ge(sem["oT_sb"], ph.at("oT_sb", s))
                        for c in range(chunks):
                            mm = pe.matmul(back[:, 0:D], oT[:, s.b, c, :], wo[:, c, :],
                                           start=(c == 0), stop=(c == chunks - 1))
                    mm.then_inc(sem["y_ps"], 1)

                def ru(s, ph=ph):
                    pe.wait_ge(sem["xT_sb"], ph.at("xT_sb", s))
                    for c in range(DC):
                        mm = pe.matmul(front[:, 0:LA], xT[:, s.b, c, :], w["lora_ru"][:, c, :],
                                       start=(c == 0), stop=(c == DC - 1))
                    mm.then_inc(sem["ru_ps"], 1)

                def zT_step(s, ph=ph):
                    pe.wait_ge(sem["route"], ph.at("route", s))
                    for k in range(2):
                        mm = pe.transpose(front[0:LA, k * T:(k + 1) * T], zcat[:, s.b, k, :], ident[:, :])
                    mm.then_inc(sem["zT_ps"], 1)
                    for k in range(4):
                        mm = pe.transpose(bank[2][:, k * T:(k + 1) * T], spread[:, s.b, k, :], ident[:, :])
                    mm.then_inc(sem["zT_ps"], 1)

                def H(s, q=0, ph=ph):
                    pe.wait_ge(sem["zT_sb"], ph.at("zT_sb", s, 0))
                    if s.plus(-1).there():
                        pe.wait_ge(sem["h1"], ph.at("h1", s.plus(-1), q))
                    for f in range(4):
                        cols = slice((4 * q + f) * 128, (4 * q + f + 1) * 128)
                        for c in range(DC):
                            pe.matmul(bank[q][:, f * T:(f + 1) * T], w["lora_w1"][:, c, cols], xT[:, s.b, c, :],
                                      start=(f == 0 and c == 0), stop=False, skip_group_check=True)
                        mm = pe.matmul(bank[q][:, f * T:(f + 1) * T], w["lora_b1"][:, cols], zT[:, s.b, 0, :],
                                       start=False, stop=True, skip_group_check=True)
                    mm.then_inc(sem["h_ps"], 1)

                def Dl(s, q=0, ph=ph):
                    pe.wait_ge(sem["h0"], ph.at("h0", s, q))
                    for f in range(4):
                        cols = slice((4 * q + f) * 128, (4 * q + f + 1) * 128)
                        mm = pe.matmul(bank[q][:, f * T:(f + 1) * T], w["lora_b1"][:, cols], zT[:, s.b, 1, :],
                                       start=False, stop=True, skip_group_check=True)
                    mm.then_inc(sem["d_ps"], 1)

                def A_step(s, ph=ph):
                    pe.wait_ge(sem["h1"], ph.at("h1", s))
                    if s.plus(-1).there():
                        pe.wait_ge(sem["a_weighted"], ph.at("a_weighted", s.plus(-1)))
                    for f in range(FC):
                        p0 = f % 2 * ER
                        mm = pe.matmul(bank[5][p0:p0 + ER, 0:2 * T], w["lora_w2"][:, f, D:D + ER],
                                       h_act[s.b][:, :, f, :], start=(f < 2), stop=(f >= FC - 2),
                                       skip_group_check=True)
                    mm.then_inc(sem["a_ps"], 1)

                def Y(s, ph=ph):
                    pe.wait_ge(sem["h_mixed"], ph.at("h_mixed", s))
                    if s.plus(-1).there():
                        pe.wait_ge(sem["z_ready"], ph.at("z_ready", s.plus(-1)))
                    for f in range(FC):
                        pe.matmul(bank[4][:, 0:D], h_mix[s.b][:, f, :], w["lora_w2"][:, f, 0:D],
                                  start=(f == 0), stop=False)

                def xqT_step(s, ph=ph):
                    pe.wait_ge(sem["quant"], ph.at("quant", s))
                    if s.plus(-1).there():
                        pe.wait_ge(sem["xqT_sb"], ph.at("xqT_sb", s.plus(-1)))
                    fb = front[:, :].bitcast(BF16)
                    for c in range(DC):
                        mm = pe.transpose(fb[:, c * T:(c + 1) * T], xq[:, s.b, c * 128:(c + 1) * 128], identb[:, :])
                    mm.then_inc(sem["xqT_ps"], 1)

                def GV(s, ph=ph):
                    pe.wait_ge(sem["xqT_sb"], ph.at("xqT_sb", s))
                    for e in range(2):
                        for q in range(2):
                            if s.plus(-1).there():
                                name = "val" if e else "gpre"
                                pe.wait_ge(sem[name], ph.at(name, s.plus(-1), q))
                            for c in range(DC):
                                mm = pe.matmul(bank[2 * e + q][:, :], xqT[:, s.b, c, :],
                                               w_bit[e][:, c * F + q * 512:c * F + (q + 1) * 512],
                                               start=(c == 0), stop=(c == DC - 1))
                            mm.then_inc(sem["gv_ps"], 1)

                def hT_step(s, ph=ph):
                    pe.wait_ge(sem["hq_ready"], ph.at("hq_ready", s))
                    if s.plus(-1).there():
                        pe.wait_ge(sem["hT_sb"], ph.at("hT_sb", s.plus(-1)))
                    hb = bank[4][:, :].bitcast(BF16)
                    for c in range(FC):
                        mm = pe.transpose(hb[:, c * T:(c + 1) * T], hq[:, s.b, c * 128:(c + 1) * 128], identb[:, :])
                    mm.then_inc(sem["hT_ps"], 1)

                nothing = lambda *a: None
                steps = {
                    "begin": begin, "ready": lambda ph=ph: all_done(pe, ph), "pool_ready": nothing,
                    "xT": xT_step, "v": v_step, "qk": qk_step, "qkT": qkT_step, "down": down,
                    "cT": cT, "norm": nothing, "vl": nothing, "Q": Q, "K": K, "S": S, "PT": PT, "PV": PV,
                    "PO": PO, "oT": oT_step, "y": y_step,
                    "ru": ru, "zT": zT_step, "H": H, "H1": lambda s: H(s, 1), "D": Dl, "D1": lambda s: Dl(s, 1),
                    "Y": Y, "A": A_step, "round": nothing, "quant": nothing, "residual": nothing,
                    "xqT": xqT_step,
                    "GV": GV, "act": nothing, "hT": hT_step}
                walk(pe, ph, steps, previous)
                previous = (ph, steps)
            if previous[0].kind != "bit":
                for end in range(3):
                    finish(previous, end)

        @block.scalar
        def _(act):
            if len(phases) > 1:
                act.wait_ge(angles, 1)
                nc.scalar.activation(turns[:, :, :, :], ang[:, :, :, :], ACT.Sin).then_inc(table_sin, 1)
            previous = None
            for ph in phases:
                def begin(ph=ph):
                    heads_done(act, ph)
                    if ph.kind == "latent":
                        act.wait_ge(weights_in[3], weight_count(3))
                        for b in range(2):
                            act.wait_ge(prep_ps, b + 1)
                            nc.scalar.copy(w_cat[:, 8 * b:8 * b + 8, 0:64],
                                           bank[b][:, :].rearrange("p (h c) -> p h c", h=8)).then_inc(prep_sb, 1)
                        for b in range(4):
                            act.wait_ge(prep_ps, b + 3)
                            nc.scalar.copy(w_vo[:, 2 * b:2 * b + 2, :],
                                           bank[2 + b][:, :].rearrange("p (h c) -> p h c", h=2)).then_inc(prep_sb, 1)

                def xT_step(s, ph=ph):
                    act.wait_ge(sem["xT_ps"], ph.at("xT_ps", s))
                    if s.plus(-2).there():
                        name = {"self": "v_ps", "cross": "qk_ps", "latent": "down_ps", "lora": "h_ps"}[ph.kind]
                        act.wait_ge(sem[name], ph.at(name, s.plus(-2)))
                    place = back if ph.kind == "latent" else front
                    nc.scalar.copy(xT[:, s.b, :, :].rearrange("p c t -> p (c t)"),
                                   place[:, 0:DC * T]).then_inc(sem["xT_sb"], 1)

                def v_step(s, ph=ph):
                    if ph.kind == "cross":
                        act.wait_ge(sem["v_ps"], ph.at("v_ps", s))
                        if s.plus(-2).there():
                            act.wait_ge(sem["pv_ps"], ph.at("pv_ps", s.plus(-2)))
                        else:
                            act.wait_ge(filled, FILLS)
                        v = v_cross[:, s.b, 0:CROSS_H * (CROSS_D + 1)].rearrange("p (h d) -> p h d", h=CROSS_H)
                        nc.scalar.copy(v[:, :, 0:CROSS_D],
                                       front[:, 0:D].rearrange("p (h d) -> p h d", h=CROSS_H)).then_inc(sem["v_sb"], 1)

                def qkT_step(s, ph=ph):
                    act.wait_ge(sem["qkT_ps"], ph.at("qkT_ps", s))
                    if s.plus(-2).there():
                        act.wait_ge(sem["s_ps"], ph.at("s_ps", s.plus(-2)))
                        act.wait_ge(sem["k_diag"], ph.at("k_diag", s.plus(-2)))
                    nc.scalar.copy(qkT[:, s.b, :, :].rearrange("p c t -> p (c t)"),
                                   front[:, :]).then_inc(sem["qkT_sb"], 1)

                def down(s, ph=ph):
                    act.wait_ge(sem["down_ps"], ph.at("down_ps", s))
                    if s.plus(-2).there():
                        act.wait_ge(sem["rms"], ph.at("rms", s.plus(-2)))
                    for k, (a, e) in enumerate(((0, QR), (QR, QR + KVR))):
                        if s.plus(-1).there() or k:
                            act.wait_ge(sem["sumsq"], ph.at("sumsq", s, k - 1))
                        nc.scalar.activation(junk[:, 0:e - a], back[:, a:e], ACT.Square,
                                             accum_out=ssq[:, s.b, k:k + 1]).then_inc(sem["sumsq"], 1)

                def cT(s, ph=ph):
                    act.wait_ge(sem["cT_ps"], ph.at("cT_ps", s))
                    if s.plus(-2).there():
                        act.wait_ge(sem["q_ps"], ph.at("q_ps", s.plus(-2)))
                        act.wait_ge(sem["s_ps"], ph.at("s_ps", s.plus(-2)))
                    nc.scalar.activation(qcT[:, s.b, :], back[:, 0:T], ACT.Copy,
                                         scale=w["lat_qn"][:, 0:1]).then_inc(sem["cT_sb"], 1)
                    nc.scalar.copy(kT[:, s.b, :], back[:, T:2 * T]).then_inc(sem["cT_sb"], 1)

                def Q(s, g, ph=ph):
                    act.wait_ge(sem["q_read"], ph.at("q_read", s, 3 * g + 2))
                    if s.plus(-1).there() or g >= 2:
                        act.wait_ge(sem["qT_ps"], ph.at("qT_ps", s, g - 2))
                    fr = front[:, :].rearrange("p (h c) -> p h c", h=HG)
                    nc.scalar.copy(q_sb[:, g % 2, :, 0:64], fr[:, :, 0:64]).then_inc(sem["q_abs"], 1)

                def K(s, g, ph=ph):
                    act.wait_ge(sem["qT_ps"], ph.at("qT_ps", s, g))
                    if s.plus(-2).there():
                        act.wait_ge(sem["s_ps"], ph.at("s_ps", s.plus(-2), g))
                    nc.scalar.copy(qT[s.b][:, HG * g:HG * (g + 1), :],
                                   front[:, :].rearrange("p (h t) -> p h t", h=HG)).then_inc(sem["qT_sb"], 1)

                def exp(s, g, ph=ph):
                    act.wait_ge(sem["s_sub"], ph.at("s_sub", s, g))
                    if s.plus(-1).there() or g >= 2:
                        act.wait_ge(sem["pT_ps"], ph.at("pT_ps", s, 2 * g - 3))
                    nc.scalar.activation(probs[:, g % 2, :, :], shifted[:, g % 2, :, :], ACT.Exp,
                                         scale=float(ph.scale)).then_inc(sem["p_exp"], 1)

                def S(s, g, exp=exp):
                    if g == 0 and not s.plus(-1).there():
                        exp(s, g)

                def PT(s, g, ph=ph, exp=exp):
                    if s.plus(-1).there() or g >= 2:
                        act.wait_ge(sem["pv_ps"], ph.at("pv_ps", s, g - 2))
                    for j in range(2):
                        act.wait_ge(sem["pT_ps"], ph.at("pT_ps", s, 2 * g + j))
                        nc.scalar.copy(probsT[:, g % 2, 2 * j:2 * j + 2, :].rearrange("p h t -> p (h t)"),
                                       pT_bank[j][:, 0:2 * T]).then_inc(sem["pT_sb"], 1)
                    if g + 1 < ph.groups:
                        exp(s, g + 1)
                    elif not (isinstance(s.n, int) and s.n == NB - 1):
                        exp(s.plus(1), 0)

                def PV(s, g, ph=ph):
                    if ph.kind != "latent":
                        act.wait_ge(sem["pv_ps"], ph.at("pv_ps", s, g))
                        if s.plus(-1).there() or g >= 2:
                            act.wait_ge(sem["po_ps"], ph.at("po_ps", s, g - 2))
                        nc.scalar.copy(ov_sb[:, g % 2, :], pv_bank[g % 2][:, 0:T]).then_inc(sem["ov_sb"], 1)

                def oT_step(s, r, ph=ph):
                    m = min(4, ph.heads * ph.dv // 128 - 4 * r)
                    act.wait_ge(sem["oT_ps"], ph.at("oT_ps", s, r))
                    if s.plus(-2).there():
                        act.wait_ge(sem["y_ps"], ph.at("y_ps", s.plus(-2)))
                    nc.scalar.copy(oT[:, s.b, 4 * r:4 * r + m, :].rearrange("p c t -> p (c t)"),
                                   back[:, 0:m * T]).then_inc(sem["oT_sb"], 1)

                def ru(s, ph=ph):
                    act.wait_ge(sem["route"], ph.at("route", s, 1))
                    nc.scalar.activation(expd[:, s.b, :], logit[:, s.b, :], ACT.Exp, bias=r1[:, s.b, 0:1],
                                         accum_out=r1[:, s.b, 1:2]).then_inc(sem["r_exp"], 1)

                def zT_step(s, ph=ph):
                    act.wait_ge(sem["zT_ps"], ph.at("zT_ps", s, 0))
                    if s.plus(-2).there():
                        act.wait_ge(sem["d_ps"], ph.at("d_ps", s.plus(-2)))
                    nc.scalar.copy(zT[:, s.b, :, :].rearrange("p k t -> p (k t)"),
                                   front[0:LA, 0:2 * T]).then_inc(sem["zT_sb"], 1)
                    act.wait_ge(sem["zT_ps"], ph.at("zT_ps", s))
                    if s.plus(-2).there():
                        act.wait_ge(sem["a_weighted"], ph.at("a_weighted", s.plus(-2)))
                        act.wait_ge(sem["h_weighted"], ph.at("h_weighted", s.plus(-2)))
                    nc.scalar.copy(spreadT[:, s.b, :, :].rearrange("p k t -> p (k t)"),
                                   bank[2][:, :]).then_inc(sem["zT_sb"], 1)

                def hidden(s, k, q, ph=ph):
                    src = "d_ps" if k else "h_ps"
                    act.wait_ge(sem[src], ph.at(src, s, q))
                    if s.plus(-2).there():
                        act.wait_ge(sem["a_ps"], ph.at("a_ps", s.plus(-2)))
                        act.wait_ge(sem["h_weighted"], ph.at("h_weighted", s.plus(-2), k))
                    nc.scalar.activation(h_act[s.b][:, k, 4 * q:4 * q + 4, :].rearrange("p f t -> p (f t)"),
                                         bank[q][:, :], ACT.Gelu_apprx_tanh).then_inc(sem["h1" if k else "h0"], 1)

                def xqT_step(s, ph=ph):
                    act.wait_ge(sem["xqT_ps"], ph.at("xqT_ps", s))
                    if s.plus(-2).there():
                        act.wait_ge(sem["gv_ps"], ph.at("gv_ps", s.plus(-2)))
                    nc.scalar.copy(xqT[:, s.b, :, :].rearrange("p c t -> p (c t)"),
                                   front[:, :].bitcast(BF16)[:, 0:DC * T]).then_inc(sem["xqT_sb"], 1)

                def act_step(s, ph=ph):
                    for q in range(2):
                        act.wait_ge(sem["gpre"], ph.at("gpre", s, q))
                        if s.plus(-2).there():
                            act.wait_ge(sem["h_ready"], ph.at("h_ready", s.plus(-2)))
                        nc.scalar.activation(g_act[s.b][:, q * 512:(q + 1) * 512], g_pre[s.b][:, q * 512:(q + 1) * 512],
                                             ACT.Silu).then_inc(sem["silu"], 1)

                def round_step(s, ph=ph):
                    act.wait_ge(sem["hquant"], ph.at("hquant", s, 3))
                    nc.scalar.activation(g_pre[s.b][:, :], hid[s.b][:, :], ACT.Copy, bias=ROUND,
                                         scale=q2[:, s.b, 3:4]).then_inc(sem["h_round"], 1)

                def hT_step(s, ph=ph):
                    act.wait_ge(sem["hT_ps"], ph.at("hT_ps", s))
                    if s.plus(-2).there():
                        act.wait_ge(sem["y_ps"], ph.at("y_ps", s.plus(-2)))
                    nc.scalar.copy(hqT[:, s.b, :, :].rearrange("p c t -> p (c t)"),
                                   bank[4][:, :].bitcast(BF16)).then_inc(sem["hT_sb"], 1)

                nothing = lambda *a: None
                steps = {
                    "begin": begin, "ready": lambda ph=ph: all_done(act, ph), "pool_ready": nothing,
                    "xT": xT_step, "v": v_step, "qk": nothing, "qkT": qkT_step, "down": down,
                    "cT": cT, "norm": nothing, "vl": nothing, "Q": Q, "K": K, "S": S, "PT": PT, "PV": PV,
                    "PO": nothing, "oT": oT_step, "y": nothing,
                    "ru": ru, "zT": zT_step, "H": lambda s: hidden(s, 0, 0), "H1": lambda s: hidden(s, 0, 1),
                    "D": lambda s: hidden(s, 1, 0), "D1": lambda s: hidden(s, 1, 1),
                    "Y": nothing, "A": nothing, "round": round_step, "quant": nothing, "residual": nothing,
                    "xqT": xqT_step,
                    "GV": nothing, "act": act_step, "hT": hT_step}
                walk(act, ph, steps, previous)
                previous = (ph, steps)
            if previous[0].kind != "bit":
                for end in range(3):
                    finish(previous, end)

        @block.vector
        def _(dve):
            V = nc.vector
            if len(phases) > 1:
                step = [0]

                def chain(ins):
                    step[0] += 1
                    ins.then_inc(tables, 1)
                    dve.wait_ge(tables, step[0])

                dve.wait_ge(pos_in, 16)
                p01 = ang[:, 0, :, 0:2]
                t4 = turns[:, 1, :, :].rearrange("p n (a f) -> p n a f", a=2)
                for f in range(2):
                    chain(V.tensor_scalar(t4[:, :, :, f], p01, float(np.float32(10000.0) ** np.float32(-f / 2)),
                                          None, ALU.mult))
                for e in (1, 0):
                    chain(V.tensor_scalar(turns[:, 0], turns[:, 1], float(1 / (2 * np.pi)), 0.25 * e, ALU.mult, ALU.add))
                    chain(V.tensor_scalar(ang[:, e], turns[:, 0], ROUND, None, ALU.add))
                    chain(V.tensor_scalar(turns[:, 0], ang[:, e], ROUND, None, ALU.subtract))
                    chain(V.scalar_tensor_tensor(out=ang[:, e], in0=turns[:, 0], scalar=-TWO_PI[0], in1=turns[:, 1],
                                                 op0=ALU.mult, op1=ALU.add))
                    chain(V.scalar_tensor_tensor(out=ang[:, e], in0=turns[:, 0], scalar=-TWO_PI[1], in1=ang[:, e],
                                                 op0=ALU.mult, op1=ALU.add))
                    chain(V.scalar_tensor_tensor(out=ang[:, e], in0=turns[:, 0], scalar=-TWO_PI[2], in1=ang[:, e],
                                                 op0=ALU.mult, op1=ALU.add))
                    if e:
                        chain(V.tensor_scalar(ang[:, e], ang[:, e], float(np.pi / 2), None, ALU.add))
                V.tensor_scalar(ang[:, :, :, :], ang[:, :, :, :], PI_BELOW, -PI_BELOW, ALU.min,
                                ALU.max).then_inc(angles, 1)
                dve.wait_ge(table_sin, 1)
                V.tensor_copy(cos_x[:, :, :], turns[:, 1]).then_inc(tables, 1)
                V.tensor_copy(sin_x[:, :, 1, :], turns[:, 0]).then_inc(tables, 1)
                V.tensor_scalar(sin_x[:, :, 0, :], turns[:, 0], -1.0, None, ALU.mult).then_inc(tables, 1)
                dve.wait_ge(tables, step[0] + 3)

            previous = None
            for ph in phases:
                def begin(ph=ph):
                    heads_done(dve, ph)
                    dve.wait_ge(consts_in, 16 * N_CONST)
                    dve.wait_ge(weights_in[ph.index], weight_count(ph.index))
                    dve.wait_ge(filled, FILLS)

                def v_step(s, ph=ph):
                    if ph.kind == "self":
                        dve.wait_ge(sem["v_ps"], ph.at("v_ps", s))
                        if s.plus(-2).there():
                            dve.wait_ge(sem["pv_ps"], ph.at("pv_ps", s.plus(-2)))
                        v = v_self[:, s.b, 0:SELF_H * (SELF_D + 1)].rearrange("p (h d) -> p h d", h=SELF_H)
                        V.tensor_tensor(v[:, :, 0:SELF_D], front[:, 0:D].rearrange("p (h d) -> p h d", h=SELF_H),
                                        w["self_bqkv"][:, 2 * D:3 * D].rearrange("p (h d) -> p h d", h=SELF_H),
                                        ALU.add).then_inc(sem["v_sb"], 1)

                def qk_step(s, ph=ph):
                    dve.wait_ge(sem["qk_ps"], ph.at("qk_ps", s))
                    if ph.kind == "self":
                        if s.plus(-2).there():
                            dve.wait_ge(sem["qkT_ps"], ph.at("qkT_ps", s.plus(-2)))
                        V.tensor_tensor(qk[:, s.b, :, :].rearrange("p c d -> p (c d)"), front[:, :],
                                        w["self_bqkv"][:, 0:2 * D], ALU.add).then_inc(sem["qk_sb"], 1)
                        return
                    if s.plus(-2).there():
                        dve.wait_ge(sem["qk_sb"], ph.at("qk_sb", s.plus(-2)))
                    V.tensor_tensor(rot_a[:, s.b, :, :].rearrange("p c (x j) -> p (c x) j", j=4),
                                    front[:, :].rearrange("p (cx j) -> p cx j", j=4),
                                    bc(cos_x[:, bass.ds(s.n, 1), :].rearrange("p a j -> p (a j)"), 1, 128),
                                    ALU.mult).then_inc(sem["qk_read"], 1)
                    fr = front[:, :].rearrange("p (c e h j) -> p c e h j", c=4, e=2, h=16)
                    rb = rot_b[:, s.b, :, :].rearrange("p c (e h j) -> p c e h j", e=2, h=16)
                    for e in range(2):
                        sines = sin_x[:, bass.ds(s.n, 1), e, :].rearrange("p a j -> p (a j)")
                        V.tensor_tensor(rb[:, :, e, :, :], fr[:, :, 1 - e, :, :], bc(bc(sines, 1, 16), 1, 4),
                                        ALU.mult).then_inc(sem["qk_read"], 1)

                def down(s, ph=ph):
                    if s.plus(-2).there():
                        dve.wait_ge(sem["cT_ps"], ph.at("cT_ps", s.plus(-2)))
                        dve.wait_ge(sem["c_sb"], ph.at("c_sb", s.plus(-2)))
                    dve.wait_ge(sem["down_ps"], ph.at("down_ps", s))
                    dve.wait_ge(sem["sumsq"], ph.at("sumsq", s))
                    V.tensor_tensor(kr_a[:, s.b, :], back[:, 192:256], lat_cos[:, :], ALU.mult).then_inc(sem["c_read"], 1)
                    V.tensor_tensor(kr_b[:, s.b, 0:32], back[:, 224:256], lat_sin[:, 0:32],
                                    ALU.mult).then_inc(sem["c_read"], 1)
                    V.tensor_tensor(kr_b[:, s.b, 32:64], back[:, 192:224], lat_sin[:, 32:64],
                                    ALU.mult).then_inc(sem["c_read"], 1)

                def norm(s, ph=ph):
                    dve.wait_ge(sem["rms"], ph.at("rms", s))
                    V.scalar_tensor_tensor(out=c_sb[:, s.b, QR:QR + KVR], in0=back[:, QR:QR + KVR],
                                           scalar=rms[:, s.b, 1:2], in1=w["lat_kvn"][:, :], op0=ALU.mult,
                                           op1=ALU.mult).then_inc(sem["c_read"], 1)
                    V.tensor_scalar(c_sb[:, s.b, 0:QR], back[:, 0:QR], rms[:, s.b, 0:1], None,
                                    ALU.mult).then_inc(sem["c_read"], 1)

                def Q(s, g, ph=ph):
                    dve.wait_ge(sem["q_ps"], ph.at("q_ps", s, g))
                    if s.plus(-1).there() or g >= 2:
                        dve.wait_ge(sem["q_sb"], ph.at("q_sb", s, g - 2))
                    fr = front[:, :].rearrange("p (h c) -> p h c", h=HG)
                    V.tensor_tensor(pe_a[:, g % 2, :, :], fr[:, :, 64:128], bc(lat_cos[:, :], 1, HG),
                                    ALU.mult).then_inc(sem["q_read"], 1)
                    V.tensor_tensor(pe_b[:, g % 2, :, 0:32], fr[:, :, 96:128], bc(lat_sin[:, 0:32], 1, HG),
                                    ALU.mult).then_inc(sem["q_read"], 1)
                    V.tensor_tensor(pe_b[:, g % 2, :, 32:64], fr[:, :, 64:96], bc(lat_sin[:, 32:64], 1, HG),
                                    ALU.mult).then_inc(sem["q_read"], 1)

                def S(s, g, ph=ph):
                    dve.wait_ge(sem["s_ps"], ph.at("s_ps", s, g))
                    if s.plus(-1).there() or g >= 2:
                        dve.wait_ge(sem["p_exp"], ph.at("p_exp", s, g - 2))
                    sc = s_bank[g % 2][:, :].rearrange("p (h t) -> p h t", h=HG)
                    V.tensor_reduce(row_max[:, g % 2, :], sc, AX_X, ALU.max).then_inc(sem["row_max"], 1)
                    dve.wait_ge(sem["row_max"], ph.at("row_max", s, g))
                    V.tensor_tensor(shifted[:, g % 2, :, :], sc, bc(row_max[:, g % 2, :], 2, T),
                                    ALU.subtract).then_inc(sem["s_sub"], 1)

                def ternary(n, g):
                    raws = [w[name] for name in BIT_RAW]
                    if n == 1 and g < 3:
                        if g == 0:
                            dve.wait_ge(bit_raw_in, 16 * len(BIT_RAW))
                        ins = V.tensor_reduce(w_stat[:, g:g + 1], raws[g], AX_X, ALU.add, apply_absolute_value=True)
                        if g == 2:
                            ins.then_inc(wsum, 1)

                    def chain(step, ins):
                        ins.then_inc(wsum, 1)
                        dve.wait_ge(wsum, step)

                    if (n, g) == (NB - 2, 0):
                        chain(2, V.tensor_scalar(gamma[:, 0], w_sums, 1.0 / (D * F), 1e-5, ALU.mult, ALU.max))
                        chain(3, V.reciprocal(gamma[:, 1], gamma[:, 0]))
                        chain(4, V.tensor_scalar(gamma[:, 2], gamma[:, 0], 1.0 / 127.0, None, ALU.mult))
                    for k in {(NB - 2, 0): [0], (NB - 2, 1): [1, 2], (NB - 2, 2): [3], (NB - 2, 3): [4, 5],
                              (NB - 1, 0): [6], (NB - 1, 1): [7], (NB - 1, 2): [8]}.get((n, g), []):
                        i, raw = k // 3, raws[k // 3]
                        if k % 3 == 0:
                            ins = V.tensor_scalar(raw, raw, gamma[:, 1, i:i + 1], ROUND, ALU.mult, ALU.add)
                        elif k % 3 == 1:
                            ins = V.tensor_scalar(raw, raw, ROUND, 1.0, ALU.subtract, ALU.min)
                        else:
                            ins = V.tensor_scalar(w_bit[i], raw, -1.0, None, ALU.max)
                        chain(5 + k, ins)

                def normalise(s, g, ph=ph):
                    dv = ph.dv
                    source = "pv_ps" if ph.kind == "latent" else "po_ps"
                    dve.wait_ge(sem[source], ph.at(source, s, g))
                    if s.plus(-1).there() or g >= 2:
                        dve.wait_ge(sem["o_norm"], ph.at("o_norm", s, g - 2))
                    if s.plus(-2).there():
                        dve.wait_ge(sem["oT_ps"], ph.at("oT_ps", s.plus(-2)))
                    if ph.kind == "latent":
                        pv = pv_bank[g % 2][:, 0:HG * PVW].rearrange("p (h c) -> p h c", h=HG)
                    else:
                        pv = pv_bank[g % 2][:, T:2 * T].rearrange("p (h c) -> p h c", h=HG)
                    V.reciprocal(rec[:, g % 2, :], pv[:, :, dv]).then_inc(sem["rec"], 1)
                    dve.wait_ge(sem["rec"], ph.at("rec", s, g))
                    V.tensor_tensor(o_sb[:, s.b, HG * g * dv:HG * (g + 1) * dv].rearrange("p (h d) -> p h d", h=HG),
                                    pv[:, :, 0:dv], bc(rec[:, g % 2, :], 2, dv), ALU.mult).then_inc(sem["o_norm"], 1)
                    if ph.kind == "latent" and len(phases) > 5 and isinstance(s.n, int):
                        ternary(s.n, g)

                def y_step(s, ph=ph):
                    dve.wait_ge(sem["y_ps"], ph.at("y_ps", s))
                    dve.wait_ge(sem["xb_ready"], ph.at("xb_ready", s))
                    if s.plus(-2).there():
                        dve.wait_ge(sem["xn_ready"], ph.at("xn_ready", s.plus(-2)))
                    if ph.kind == "lora":
                        V.tensor_tensor(z[:, s.b, :], bank[4][:, 0:D], part[:, s.b, 0, :],
                                        ALU.add).then_inc(sem["z_ready"], 1)
                    elif ph.kind == "bit":
                        V.scalar_tensor_tensor(out=z[:, s.b, :], in0=back[:, 0:D], scalar=q2[:, s.b, 4:5],
                                               in1=xb[:, s.b, :], op0=ALU.mult, op1=ALU.add).then_inc(sem["z_ready"], 1)
                    else:
                        V.tensor_tensor(z[:, s.b, :], back[:, 0:D], xb[:, s.b, :], ALU.add).then_inc(sem["z_ready"], 1)
                    dve.wait_ge(sem["z_ready"], ph.at("z_ready", s))
                    V.bn_stats(stat6[:, s.b, :], z[:, s.b, :]).then_inc(sem["stats"], 1)
                    dve.wait_ge(sem["stats"], ph.at("stats", s, 0))
                    V.tensor_copy(spare[:, 0:1], stat6[:, s.b, 0:1])
                    V.bn_aggr(mv[:, s.b, :], stat6[:, s.b, :]).then_inc(sem["stats"], 1)

                def ru(s, ph=ph):
                    k = [0]

                    def chain(ins):
                        ins.then_inc(sem["route"], 1)
                        dve.wait_ge(sem["route"], ph.at("route", s, k[0]))
                        k[0] += 1

                    dve.wait_ge(sem["ru_ps"], ph.at("ru_ps", s))
                    if s.plus(-2).there():
                        dve.wait_ge(sem["zT_ps"], ph.at("zT_ps", s.plus(-2)))
                        dve.wait_ge(sem["part_ready"], ph.at("part_ready", s.plus(-2)))
                    b = s.b
                    chain(V.tensor_tensor(logit[:, b, :], front[:, ER:ER + E], w["lora_br"][:, :], ALU.add))
                    chain(V.tensor_reduce(r1[:, b, 0:1], logit[:, b, :], AX_X, ALU.max, negate=True))
                    dve.wait_ge(sem["r_exp"], ph.at("r_exp", s))
                    chain(V.reciprocal(r1[:, b, 2:3], r1[:, b, 1:2]))
                    chain(V.tensor_scalar(prob[:, b, :], expd[:, b, :], r1[:, b, 2:3], None, ALU.mult))
                    for c, pr in enumerate((prob, prob2)):
                        chain(V.tensor_reduce(r1[:, b, 3 + 2 * c:4 + 2 * c], pr[:, b, :], AX_X, ALU.max))
                        chain(V.scalar_tensor_tensor(out=key[:, b, c, :], in0=pr[:, b, :], scalar=r1[:, b, 3 + 2 * c:4 + 2 * c],
                                                     in1=descend[:, :], op0=ALU.is_equal, op1=ALU.mult))
                        chain(V.tensor_reduce(r1[:, b, 4 + 2 * c:5 + 2 * c], key[:, b, c, :], AX_X, ALU.max))
                        chain(V.tensor_scalar(onehot[:, b, c, :], key[:, b, c, :], r1[:, b, 4 + 2 * c:5 + 2 * c], 2.0,
                                              ALU.is_equal, ALU.mult))
                        if c == 0:
                            chain(V.scalar_tensor_tensor(out=prob2[:, b, :], in0=onehot[:, b, 0, :], scalar=-2.0,
                                                         in1=prob[:, b, :], op0=ALU.mult, op1=ALU.add))
                        chain(V.tensor_scalar(weighted[:, b, c, :], onehot[:, b, c, :], r1[:, b, 3 + 2 * c:4 + 2 * c],
                                              None, ALU.mult))
                    u1 = front[:, 0:ER].rearrange("p (e r) -> p e r", e=E)
                    chain(V.tensor_tensor(zcat[:, b, 0, 0:ER].rearrange("p (e r) -> p e r", e=E), u1,
                                          bc(onehot[:, b, 0, :], 2, R), ALU.mult))
                    chain(V.tensor_tensor(ztmp[:, b, :].rearrange("p (e r) -> p e r", e=E), u1,
                                          bc(onehot[:, b, 1, :], 2, R), ALU.mult))
                    chain(V.tensor_tensor(zcat[:, b, 1, 0:ER], ztmp[:, b, :], zcat[:, b, 0, 0:ER], ALU.subtract))
                    chain(V.tensor_tensor(r1[:, b, 7:8], r1[:, b, 3:4], r1[:, b, 5:6], ALU.add))
                    for c in range(2):
                        chain(V.tensor_copy(spread[:, b, c, :].rearrange("p (d e r) -> p d e r", d=2, e=E),
                                            bc(bc(weighted[:, b, c, :], 2, R), 1, 2)))
                        chain(V.tensor_copy(spread[:, b, 2 + c, :], r1[:, b, 3 + 2 * c:4 + 2 * c].to_broadcast([T, 128])))

                def zT_step(s, ph=ph):
                    dve.wait_ge(sem["xb_ready"], ph.at("xb_ready", s))
                    if s.plus(-2).there():
                        dve.wait_ge(sem["z_ready"], ph.at("z_ready", s.plus(-2)))
                    V.scalar_tensor_tensor(out=part[:, s.b, 0, :], in0=w["lora_b2row"][:, :], scalar=r1[:, s.b, 7:8],
                                           in1=xb[:, s.b, :], op0=ALU.mult, op1=ALU.add).then_inc(sem["part_ready"], 1)

                def weigh_hidden(s, k, ph=ph):
                    dve.wait_ge(sem["h1" if k else "h0"], ph.at("h1" if k else "h0", s))
                    dve.wait_ge(sem["zT_sb"], ph.at("zT_sb", s))
                    if s.plus(-2).there():
                        dve.wait_ge(sem["y_ps"], ph.at("y_ps", s.plus(-2)))
                    V.tensor_tensor((h_tmp if k else h_mix)[s.b], h_act[s.b][:, k, :, :],
                                    bc(spreadT[:, s.b, 2 + k, :], 1, FC), ALU.mult).then_inc(sem["h_weighted"], 1)

                def A_step(s, ph=ph):
                    dve.wait_ge(sem["a_ps"], ph.at("a_ps", s))
                    if s.plus(-1).there():
                        dve.wait_ge(sem["z2T_sb"], ph.at("z2T_sb", s.plus(-1)))
                    V.tensor_tensor(z2w[:, :, :], bank[5][:, 0:2 * T].rearrange("p (k t) -> p k t", k=2),
                                    spreadT[:, s.b, 0:2, :], ALU.mult).then_inc(sem["a_weighted"], 1)
                    dve.wait_ge(sem["a_weighted"], ph.at("a_weighted", s))
                    if s.plus(-2).there():
                        dve.wait_ge(sem["y_ps"], ph.at("y_ps", s.plus(-2)))
                    V.tensor_tensor(z2T[:, s.b, :], z2w[:, 0, :], z2w[:, 1, :], ALU.add).then_inc(sem["z2T_sb"], 1)

                def scales(s, cols, src, width, sname, gi, ph=ph):
                    b = s.b
                    k = [0]

                    def chain(ins):
                        ins.then_inc(sem[sname], 1)
                        dve.wait_ge(sem[sname], ph.at(sname, s, k[0]))
                        k[0] += 1

                    chain(V.tensor_reduce(cols[:, b, 0:1], src, AX_X, ALU.max, apply_absolute_value=True))
                    chain(V.tensor_scalar(cols[:, b, 1:2], cols[:, b, 0:1], 1e-5, None, ALU.max))
                    chain(V.reciprocal(cols[:, b, 2:3], cols[:, b, 1:2]))
                    chain(V.tensor_scalar(cols[:, b, 3:4], cols[:, b, 2:3], 127.0, None, ALU.mult))
                    for i, g in enumerate(gi):
                        chain(V.tensor_tensor(cols[:, b, 4 + i:5 + i], cols[:, b, 1:2], gamma[:, 2, g:g + 1], ALU.mult))
                    return chain

                def quant(s, ph=ph):
                    dve.wait_ge(x_loaded[s.b], ph.dma("x_loaded", s))
                    if s.plus(-2).there():
                        dve.wait_ge(sem["val"], ph.at("val", s.plus(-2)))
                        dve.wait_ge(sem["xqT_ps"], ph.at("xqT_ps", s.plus(-2)))
                    chain = scales(s, q1, xs[:, s.b, :], D, "quant", (0, 1))
                    chain(V.tensor_scalar(xq_f[:, s.b, :], xs[:, s.b, :], q1[:, s.b, 3:4], ROUND, ALU.mult, ALU.add))
                    chain(V.tensor_scalar(xq[:, s.b, :], xq_f[:, s.b, :], ROUND, 127.0, ALU.subtract, ALU.min))

                def act_step(s, ph=ph):
                    b = s.b
                    for q in range(2):
                        cols = slice(q * 512, (q + 1) * 512)
                        dve.wait_ge(sem["gv_ps"], ph.at("gv_ps", s, q))
                        if s.plus(-2).there():
                            dve.wait_ge(sem["hq_ready"], ph.at("hq_ready", s.plus(-2)))
                        V.scalar_tensor_tensor(out=g_pre[b][:, cols], in0=bank[q][:, :], scalar=q1[:, b, 4:5],
                                               in1=w["bit_bg"][:, cols], op0=ALU.mult, op1=ALU.add).then_inc(sem["gpre"], 1)
                    for q in range(2):
                        cols = slice(q * 512, (q + 1) * 512)
                        dve.wait_ge(sem["gv_ps"], ph.at("gv_ps", s, 2 + q))
                        if s.plus(-2).there():
                            dve.wait_ge(sem["h_ready"], ph.at("h_ready", s.plus(-2)))
                        V.scalar_tensor_tensor(out=val[b][:, cols], in0=bank[2 + q][:, :], scalar=q1[:, b, 5:6],
                                               in1=w["bit_bv"][:, cols], op0=ALU.mult, op1=ALU.add).then_inc(sem["val"], 1)
                    dve.wait_ge(sem["silu"], ph.at("silu", s))
                    dve.wait_ge(sem["val"], ph.at("val", s))
                    if s.plus(-2).there():
                        dve.wait_ge(sem["h_round"], ph.at("h_round", s.plus(-2)))
                        dve.wait_ge(sem["z_ready"], ph.at("z_ready", s.plus(-2)))
                    V.tensor_tensor(hid[b][:, :], g_act[b][:, :], val[b][:, :], ALU.mult).then_inc(sem["h_ready"], 1)
                    dve.wait_ge(sem["h_ready"], ph.at("h_ready", s))
                    scales(s, q2, hid[b][:, :], F, "hquant", (2,))

                nothing = lambda *a: None
                steps = {
                    "begin": begin, "ready": lambda ph=ph: all_done(dve, ph), "pool_ready": nothing,
                    "xT": nothing, "v": v_step, "qk": qk_step, "qkT": nothing, "down": down,
                    "norm": norm, "cT": nothing, "vl": nothing, "Q": Q, "K": nothing, "S": S, "PT": nothing,
                    "PV": normalise if ph.kind == "latent" else nothing, "PO": normalise, "oT": nothing,
                    "y": y_step,
                    "ru": ru, "zT": zT_step, "H": nothing, "H1": nothing, "D": lambda s: weigh_hidden(s, 0),
                    "D1": lambda s: weigh_hidden(s, 1),
                    "Y": nothing, "A": A_step, "round": nothing, "quant": quant, "residual": nothing,
                    "xqT": nothing,
                    "GV": nothing, "act": act_step, "hT": nothing}
                walk(dve, ph, steps, previous)
                previous = (ph, steps)
            if previous[0].kind != "bit":
                for end in range(3):
                    finish(previous, end)

        @block.gpsimd
        def _(pool):
            P = nc.gpsimd
            P.memset(v_self[:, :, :], 1.0).then_inc(filled, 1)
            P.memset(v_cross[:, :, :], 1.0).then_inc(filled, 1)
            P.memset(v_lat[:, :, :], 1.0).then_inc(filled, 1)
            P.memset(minus_half[:, :], -0.5).then_inc(filled, 1)
            P.memset(ones[:, :], 1.0).then_inc(filled, 1)
            P.memset(ln_eps[:, :], LN_EPS).then_inc(filled, 1)
            P.memset(rms_eps[:, :], RMS_EPS).then_inc(filled, 1)
            P.memset(inv_rank[:, 0:1], 1.0 / QR).then_inc(filled, 1)
            P.memset(inv_rank[:, 1:2], 1.0 / KVR).then_inc(filled, 1)
            P.memset(round_bias[:, :], ROUND).then_inc(filled, 1)
            P.memset(zcat[:, :, :, ER:LA], 0.0).then_inc(filled, 1)
            pool.wait_ge(filled, FILLS - 1)
            P.memset(zcat[:, :, 0, ER:ER + 1], 1.0).then_inc(filled, 1)
            pool.wait_ge(filled, FILLS)

            previous = None
            for ph in phases:
                bias = {0: "self_bo", 1: "cross0_bo", 4: "cross1_bo", 5: "bit_bo"}.get(ph.index)

                def begin(ph=ph):
                    heads_done(pool, ph)
                    pool.wait_ge(weights_in[ph.index], weight_count(ph.index))
                    pool.wait_ge(consts_in, 16 * N_CONST)
                    pool.wait_ge(filled, FILLS)

                def residual(s, ph=ph, bias=bias):
                    pool.wait_ge(x_loaded[s.b], ph.dma("x_loaded", s))
                    if s.plus(-2).there():
                        name = "part_ready" if ph.kind == "lora" else "z_ready"
                        pool.wait_ge(sem[name], ph.at(name, s.plus(-2)))
                    if bias:
                        ins = P.tensor_tensor(xb[:, s.b, :], xs[:, s.b, :], w[bias][:, :], ALU.add)
                    else:
                        ins = P.tensor_tensor(xb[:, s.b, :], xs[:, s.b, :], ones[:, 0:1].to_broadcast([T, D]), ALU.mult)
                    ins.then_inc(sem["xb_ready"], 1)

                def qk_step(s, ph=ph):
                    if ph.kind == "cross":
                        pool.wait_ge(sem["qk_read"], ph.at("qk_read", s))
                        if s.plus(-2).there():
                            pool.wait_ge(sem["qkT_ps"], ph.at("qkT_ps", s.plus(-2)))
                        P.tensor_tensor(qk[:, s.b, :, :], rot_a[:, s.b, :, :], rot_b[:, s.b, :, :],
                                        ALU.add).then_inc(sem["qk_sb"], 1)

                def qkT_step(s, ph=ph):
                    mask = self_mask if ph.kind == "self" else cross_mask
                    half = ph.groups // 2
                    for g in range(ph.groups):
                        if g == 0:
                            pool.wait_ge(sem["qkT_sb"], ph.at("qkT_sb", s))
                        if s.plus(-2).there():
                            pool.wait_ge(sem["s_ps"], ph.at("s_ps", s.plus(-2), g))
                        m = (g % half) * HG
                        P.tensor_tensor(kdiag[:, s.b, HG * g:HG * (g + 1), :], bc(qkT[:, s.b, 2 + g // half, :], 1, HG),
                                        bc(mask[:, m:m + HG], 2, T), ALU.mult).then_inc(sem["k_diag"], 1)

                def down(s, ph=ph):
                    pool.wait_ge(sem["sumsq"], ph.at("sumsq", s))
                    if s.plus(-2).there():
                        pool.wait_ge(sem["c_read"], ph.at("c_read", s.plus(-2)))
                    P.tensor_tensor(rms[:, s.b, :], ssq[:, s.b, :], inv_rank[:, :], ALU.mult).then_inc(sem["rms"], 1)
                    pool.wait_ge(sem["rms"], ph.at("rms", s, 0))
                    P.tensor_tensor(rms[:, s.b, :], rms[:, s.b, :], rms_eps[:, :], ALU.add).then_inc(sem["rms"], 1)
                    pool.wait_ge(sem["rms"], ph.at("rms", s, 1))
                    P.tensor_tensor(rms[:, s.b, :], rms[:, s.b, :], minus_half[:, :], ALU.pow).then_inc(sem["rms"], 1)

                def norm(s, ph=ph):
                    pool.wait_ge(sem["c_read"], ph.at("c_read", s, 2))
                    if s.plus(-2).there():
                        pool.wait_ge(sem["cT_ps"], ph.at("cT_ps", s.plus(-2)))
                    P.tensor_tensor(c_sb[:, s.b, QR + KVR:QR + 2 * KVR], kr_a[:, s.b, :], kr_b[:, s.b, :],
                                    ALU.add).then_inc(sem["c_sb"], 1)

                def vl(s, ph=ph):
                    pool.wait_ge(sem["c_read"], ph.at("c_read", s))
                    if s.plus(-2).there():
                        pool.wait_ge(sem["pv_ps"], ph.at("pv_ps", s.plus(-2)))
                    P.tensor_tensor(v_lat[:, s.b, 0:KVR], c_sb[:, s.b, QR:QR + KVR],
                                    ones[:, 0:1].to_broadcast([T, KVR]), ALU.mult).then_inc(sem["c_sb"], 1)

                def Q(s, g, ph=ph):
                    pool.wait_ge(sem["q_read"], ph.at("q_read", s, 3 * g + 2))
                    if s.plus(-1).there() or g >= 2:
                        pool.wait_ge(sem["qT_ps"], ph.at("qT_ps", s, g - 2))
                    P.tensor_tensor(q_sb[:, g % 2, :, 64:128], pe_a[:, g % 2, :, :], pe_b[:, g % 2, :, :],
                                    ALU.add).then_inc(sem["q_sb"], 1)
                    if g == 3:
                        residual(s)

                def y_step(s, ph=ph):
                    b = s.b
                    pool.wait_ge(sem["stats"], ph.at("stats", s))
                    P.tensor_tensor(rs[:, b, 0:1], mv[:, b, 1:2], ln_eps[:, :], ALU.add).then_inc(sem["rstd"], 1)
                    pool.wait_ge(sem["rstd"], ph.at("rstd", s, 0))
                    P.tensor_tensor(rs[:, b, 1:2], rs[:, b, 0:1], minus_half[:, 0:1], ALU.pow).then_inc(sem["rstd"], 1)
                    P.tensor_tensor(zc[:, b, :], z[:, b, :], mv[:, b, 0:1].to_broadcast([T, D]),
                                    ALU.subtract).then_inc(sem["rstd"], 1)
                    pool.wait_ge(sem["rstd"], ph.at("rstd", s))
                    if ph.index or s.plus(-2).there():
                        pool.wait_ge(x_stored[b], ph.dma("x_stored", s.plus(-2)))
                    P.tensor_tensor(xn[:, b, :], zc[:, b, :], rs[:, b, 1:2].to_broadcast([T, D]),
                                    ALU.mult).then_inc(sem["xn_ready"], 1)

                def mix_hidden(s, ph=ph):
                    pool.wait_ge(sem["h_weighted"], ph.at("h_weighted", s))
                    P.tensor_tensor(h_mix[s.b], h_mix[s.b], h_tmp[s.b], ALU.add).then_inc(sem["h_mixed"], 1)

                def act_step(s, ph=ph):
                    pool.wait_ge(sem["h_round"], ph.at("h_round", s))
                    if s.plus(-2).there():
                        pool.wait_ge(sem["hT_ps"], ph.at("hT_ps", s.plus(-2)))
                    P.tensor_tensor(hq[:, s.b, :], g_pre[s.b][:, :], round_bias[:, 0:1].to_broadcast([T, F]),
                                    ALU.subtract).then_inc(sem["hq_ready"], 1)

                nothing = lambda *a: None
                steps = {
                    "begin": begin, "ready": lambda ph=ph: all_done(pool, ph),
                    "pool_ready": lambda ph=ph: all_done(pool, ph),
                    "xT": residual if ph.kind == "lora" else nothing, "v": residual,
                    "qk": qk_step, "qkT": qkT_step, "down": down, "norm": norm, "cT": nothing, "vl": vl,
                    "Q": Q, "K": nothing, "S": nothing, "PT": nothing, "PV": nothing, "PO": nothing,
                    "oT": nothing,
                    "y": y_step, "ru": nothing, "zT": nothing, "H": nothing, "H1": nothing, "D": nothing,
                    "D1": mix_hidden, "Y": nothing, "A": nothing, "round": nothing, "quant": nothing,
                    "xqT": nothing, "GV": nothing, "residual": residual, "act": act_step, "hT": nothing}
                walk(pool, ph, steps, previous)
                previous = (ph, steps)
            if previous[0].kind != "bit":
                for end in range(3):
                    finish(previous, end)


WSUM_STEPS = 1 + 3 + 9
PI_BELOW = float(np.nextafter(np.float32(np.pi), np.float32(0)))


def _two_pi_parts():
    parts, rest = [], 2 * np.pi
    for bits in (9, 9):
        e = int(np.floor(np.log2(rest)))
        p = np.floor(rest / 2.0 ** (e - bits + 1)) * 2.0 ** (e - bits + 1)
        parts.append(float(p))
        rest -= p
    return parts + [float(np.float32(rest))]


TWO_PI = _two_pi_parts()

CONSTS = ["ident", "identb", "causal", "self_mask", "cross_mask", "lat_cos", "lat_sin", "descend", "pos"]

WEIGHT_TILES = [
    ("self_qkv", [128, DC, 3 * D], F32), ("self_bqkv", [128, 3 * D], F32),
    ("self_o", [128, DC, D], F32), ("self_bo", [128, D], F32),
    ("cross0_q", [128, DC, D], F32), ("cross0_kv", [128, 2 * D], F32),
    ("cross0_o", [128, DC, D], F32), ("cross0_bo", [128, D], F32),
    ("lora_ru", [128, DC, LA], F32), ("lora_br", [128, E], F32), ("lora_w1", [128, DC, F], F32),
    ("lora_b1", [LA, F], F32), ("lora_w2", [128, FC, D + ER], F32), ("lora_b2", [128, D], F32),
    ("lora_b2row", [128, D], F32),
    ("lat_down", [128, DC, 256], F32), ("lat_qn", [QR, 1], F32), ("lat_kvn", [128, KVR], F32),
    ("cross1_q", [128, DC, D], F32), ("cross1_kv", [128, 2 * D], F32),
    ("cross1_o", [128, DC, D], F32), ("cross1_bo", [128, D], F32),
    ("bit_gate", [128, DC * F], F32), ("bit_val", [128, DC * F], F32), ("bit_out", [128, FC * D], F32),
    ("bit_bg", [128, F], F32), ("bit_bv", [128, F], F32), ("bit_bo", [128, D], F32),
]
BIT_RAW = ("bit_gate", "bit_val", "bit_out")
BIT_SHARED = ("bit_gate", "bit_val", "bit_out", "bit_bg", "bit_bv")
_PHASE_OF = {"self": 0, "cross0": 1, "lora": 2, "lat": 3, "cross1": 4, "bit": 5}
WEIGHT_PHASE = [(n, _PHASE_OF[n.split("_")[0]]) for n, _, _ in WEIGHT_TILES]



def chunked(a):
    return a.reshape(a.shape[0] // 128, 128, a.shape[1]).transpose(1, 0, 2)


def rows128(v):
    return np.broadcast_to(v[None, :], (128, v.shape[0]))


def cross_columns():
    cols = []
    for c in range(2):
        for e in range(2):
            for h in range(16):
                for j in range(4):
                    cols.append((16 * c + h) * CROSS_D + 2 * j + e)
    return np.array(cols)


def lay_out(i):
    bf = mybir.dt.np(BF16)
    r = {}
    r["x"] = i["x"].transpose(1, 0, 2)
    r["ctxT"] = i["ctx_1024"].transpose(2, 0, 1)
    r["pos"] = i["fside_BxSx2_0"].transpose(1, 0, 2)
    r["ident"] = np.eye(128, dtype=np.float32)
    r["identb"] = np.eye(128, dtype=bf)
    allowed = np.tril(np.ones((T, T), bool))
    r["causal"] = np.broadcast_to(np.where(allowed, 0.0, -1e30).astype(bf)[:, None, :], (T, HG, T))
    rows = np.arange(128)
    r["self_mask"] = (rows[:, None] // SELF_D == np.arange(8)[None, :]).astype(np.float32)
    r["cross_mask"] = ((rows[:, None] % 64) // 4 == np.arange(16)[None, :]).astype(np.float32)
    freq = (1.0 / 10000.0 ** (np.arange(0, KVR, 2, dtype=np.float32) / np.float32(KVR))).astype(np.float32)
    angle = np.outer(np.arange(T, dtype=np.float32), freq).astype(np.float32)
    r["lat_cos"] = np.concatenate([np.cos(angle), np.cos(angle)], 1).astype(np.float32)
    r["lat_sin"] = np.concatenate([-np.sin(angle), np.sin(angle)], 1).astype(np.float32)
    r["descend"] = rows128(np.arange(E, 0, -1).astype(np.float32))
    r["self_qkv"] = chunked(np.concatenate([i["L0_attn_Wq"].T, i["L0_attn_Wk"].T, i["L0_attn_Wv"].T], 1))
    r["self_bqkv"] = rows128(np.concatenate([i["L0_attn_bq"], i["L0_attn_bk"], i["L0_attn_bv"]]))
    r["self_o"] = chunked(i["L0_attn_Wo"].T)
    r["self_bo"] = rows128(i["L0_attn_bo"])
    cols = cross_columns()
    for l in range(2):
        r[f"cross{l}_q"] = chunked(i[f"L{l}_xattn_Wq"][:, cols])
        kv = i[f"L{l}_xattn_Wkv"]
        r[f"cross{l}_kv"] = np.concatenate([kv[:, :D][:, cols], kv[:, D:]], 1)
        r[f"cross{l}_o"] = chunked(i[f"L{l}_xattn_Wout"])
        r[f"cross{l}_bo"] = rows128(i[f"L{l}_xattn_bout"])
    ru = np.zeros((D, LA), np.float32)
    ru[:, :ER] = i["L0_ffn_A1"].reshape(ER, D).T
    ru[:, ER:ER + E] = i["L0_ffn_W_r"].T
    r["lora_ru"] = chunked(ru)
    r["lora_br"] = rows128(i["L0_ffn_b_r"])
    r["lora_w1"] = chunked(i["L0_ffn_W1"].T)
    b1 = np.zeros((LA, F), np.float32)
    b1[:ER] = i["L0_ffn_B1"].transpose(0, 2, 1).reshape(ER, F)
    b1[ER] = i["L0_ffn_b1"]
    r["lora_b1"] = b1
    r["lora_w2"] = chunked(np.concatenate([i["L0_ffn_W2"].T, i["L0_ffn_A2"].reshape(ER, F).T], 1))
    b2 = i["L0_ffn_B2"].transpose(0, 2, 1).reshape(ER, D)
    r["lora_b2"] = np.concatenate([b2, b2], 0)
    r["lora_b2row"] = rows128(i["L0_ffn_b2"])
    halves = np.concatenate([np.arange(0, KVR, 2), np.arange(1, KVR, 2)])
    r["lat_down"] = chunked(np.concatenate([i["L1_attn_wq_down"].T, i["L1_attn_wkv_down"].T,
                                            i["L1_attn_wk_rope"].T[:, halves]], 1))
    r["lat_qn"] = i["L1_attn_q_norm_w"][:, None]
    r["lat_kvn"] = rows128(i["L1_attn_kv_norm_w"])
    r["lat_rope"] = i["L1_attn_wq_rope"].reshape(LAT_H, KVR, QR)[:, halves, :].transpose(2, 0, 1)
    r["lat_q"] = i["L1_attn_wq_up"].reshape(LAT_H, NOPE, QR).transpose(1, 0, 2)
    r["lat_kv"] = i["L1_attn_wkv_up"].reshape(LAT_H, 2, NOPE, KVR).transpose(2, 0, 1, 3)
    r["lat_o"] = i["L1_attn_wo"].T.reshape(LAT_H, VD, D).transpose(1, 0, 2)
    for name in ("gate", "val"):
        r[f"bit_{name}"] = chunked(i[f"L1_ffn_{name}_w"].T).reshape(128, DC * F)
    r["bit_out"] = chunked(i["L1_ffn_out_w"].T).reshape(128, FC * D)
    r["bit_bg"] = rows128(i["L1_ffn_gate_b"])
    r["bit_bv"] = rows128(i["L1_ffn_val_b"])
    r["bit_bo"] = rows128(i["L1_ffn_out_b"])
    return {k: np.ascontiguousarray(v) for k, v in r.items()}


def kernel(**inputs):
    import concourse.bacc as bacc
    from concourse.bass_utils import run_bass_kernel_spmd

    laid = lay_out({k: np.asarray(v) for k, v in inputs.items()})
    nc = bacc.Bacc("TRN2", target_bir_lowering=False, num_devices=1)
    ins, arrays = {}, {}
    for name, a in laid.items():
        arrays["in_" + name] = a
        ins[name] = nc.dram_tensor("in_" + name, a.shape, mybir.dt.from_np(a.dtype), kind="ExternalInput").ap()
    out = nc.dram_tensor("out_x", (T, NB, D), F32, kind="ExternalOutput").ap()
    build_decoder(nc, ins, out)
    result = run_bass_kernel_spmd(nc, [arrays], core_ids=[0])
    return np.ascontiguousarray(result.results[0]["out_x"].transpose(1, 0, 2))
```
